# Optimizing a Trainium2 kernel written in Bass

```python
import numpy as np
import jax
import jax.numpy as jnp

def _softmax(x, axis=-1):
    return jax.nn.softmax(x, axis=axis)

def _gelu(x):
    return jax.nn.gelu(x, approximate=True)

def _silu(x):
    return jax.nn.silu(x)

def _sigmoid(x):
    return jax.nn.sigmoid(x)

def _layernorm(x, axis=-1, eps=1e-05):
    m = jnp.mean(x, axis=axis, keepdims=True)
    v = jnp.var(x, axis=axis, keepdims=True)
    return (x - m) / jnp.sqrt(v + eps)

def _scatter_add(tgt, idx, src, axis=0):
    return tgt.at[idx].add(src)

def _segment_sum(src, seg, n):
    return jax.ops.segment_sum(src, seg, n)
kernel_name = 'mk_gnn_preln_d4_gnn_r64_656788'

def setup_inputs(seed: int=0):
    np.random.seed(seed)
    _w = jnp.asarray

    def _rec_inputs():
        import jax
        import jax.numpy as jnp
        _gk = jax.random.key(seed)
        x = -0.000202 + 1 * jax.random.normal(jax.random.fold_in(_gk, 1), (50000, 128), jnp.float32)
        src = jax.random.randint(jax.random.fold_in(_gk, 2), (25000,), 0, 50000, jnp.int32)
        dst = jnp.minimum((50000 * jax.random.uniform(jax.random.fold_in(_gk, 3), (25000,)) ** 2.0).astype(jnp.int32), 49999)
        _o = jnp.argsort(dst, stable=True)
        src = src[_o]
        dst = dst[_o]
        edge_type_9 = jax.random.randint(jax.random.fold_in(_gk, 13), (25000,), 0, 9, jnp.int32)
        edge_weight1 = 0.000614103 + 0.999867 * jax.random.normal(jax.random.fold_in(_gk, 14), (25000, 1), jnp.float32)
        return (x, src, dst, edge_type_9, edge_weight1)
    x, src, dst, edge_type_9, edge_weight1 = _rec_inputs()

    def _L0_gnn_setup():
        import jax, jax.numpy as jnp
        import numpy as np
        key = jax.random.key(seed)
        k1, k2, k3, k4 = jax.random.split(key, 4)
        N, E, F_IN, F_OUT = (50000, 12500, 128, 128)
        x = jax.random.normal(k1, (N, F_IN), dtype=jnp.float32)
        src = jax.random.randint(k2, (E,), 0, N, dtype=jnp.int32)
        dst = jax.random.randint(k3, (E,), 0, N, dtype=jnp.int32)
        W = jax.random.normal(k4, (F_OUT, 2 * F_IN), dtype=jnp.float32) * (1.0 / np.sqrt(2 * F_IN))
        return {'x': x, 'src': src, 'dst': dst, 'num_nodes': N, 'W': W}
    _L0_gnn_all = _L0_gnn_setup()
    _L0_gnn_in = {k: v for k, v in _L0_gnn_all.items() if k in ('W',)}
    del _L0_gnn_all

    def _L1_gnn_setup():
        import jax, jax.numpy as jnp
        import numpy as np
        N_NODES = 100000
        EPS = 1e-05

        def batch_norm(x, gamma, beta):
            mu = jnp.mean(x, axis=0)
            var = jnp.mean(jnp.square(x - mu), axis=0)
            return gamma * (x - mu) * jax.lax.rsqrt(var + EPS) + beta

        def gcn_conv(x, W, b, src, dst, n):
            h = x @ W
            ones = jnp.ones(src.shape[0], dtype=x.dtype)
            deg = jax.ops.segment_sum(ones, dst, num_segments=n) + 1.0
            dinv = jax.lax.rsqrt(deg)
            norm = dinv[src] * dinv[dst]
            agg = jax.ops.segment_sum(h[src] * norm[:, None], dst, num_segments=n)
            agg = agg + h * jnp.square(dinv)[:, None]
            return agg + b
        key = jax.random.key(seed)
        ks = jax.random.split(key, 8)
        c_in, hidden = (128, 128)
        n, e = (N_NODES, 9375)
        x = jax.random.normal(ks[0], (n, c_in), dtype=jnp.float32)
        edge_index = jax.random.randint(ks[1], (2, e), 0, n, dtype=jnp.int64)
        s = 1.0 / np.sqrt(c_in)
        return {'x': x, 'edge_index': edge_index, 'bn0_gamma': jnp.ones((c_in,), jnp.float32), 'bn0_beta': jnp.zeros((c_in,), jnp.float32), 'W1': jax.random.uniform(ks[2], (c_in, hidden), jnp.float32, -s, s), 'b1': jnp.zeros((hidden,), jnp.float32), 'bn1_gamma': jnp.ones((hidden,), jnp.float32), 'bn1_beta': jnp.zeros((hidden,), jnp.float32), 'W2': jax.random.uniform(ks[3], (hidden, hidden), jnp.float32, -s, s), 'b2': jnp.zeros((hidden,), jnp.float32), 'bn2_gamma': jnp.ones((hidden,), jnp.float32), 'bn2_beta': jnp.zeros((hidden,), jnp.float32)}
    _L1_gnn_all = _L1_gnn_setup()
    _L1_gnn_in = {k: v for k, v in _L1_gnn_all.items() if k in ('bn0_gamma', 'bn0_beta', 'W1', 'b1', 'bn1_gamma', 'bn1_beta', 'W2', 'b2', 'bn2_gamma', 'bn2_beta')}
    del _L1_gnn_all

    def _L2_gnn_setup():
        import jax, jax.numpy as jnp
        import numpy as np
        N_NODES = 50000
        N_EDGES = 12500
        HIDDEN = 128
        key = jax.random.key(seed)
        k1, k2, k3, k4, k5 = jax.random.split(key, 5)
        x_hidden = jax.random.normal(k1, (N_NODES, HIDDEN), dtype=jnp.float32)
        edge_index = jax.random.randint(k2, (2, N_EDGES), 0, N_NODES, dtype=jnp.int64)
        edge_attr = jax.random.normal(k3, (N_EDGES, 1), dtype=jnp.float32)
        lim = 1.0 / np.sqrt(HIDDEN)
        W = jax.random.uniform(k4, (HIDDEN, HIDDEN), minval=-lim, maxval=lim, dtype=jnp.float32)
        b = jax.random.uniform(k5, (HIDDEN,), minval=-lim, maxval=lim, dtype=jnp.float32)
        return {'x_hidden': x_hidden, 'edge_index': edge_index, 'edge_attr': edge_attr, 'W': W, 'b': b}
    _L2_gnn_all = _L2_gnn_setup()
    _L2_gnn_in = {k: v for k, v in _L2_gnn_all.items() if k in ('W', 'b')}
    del _L2_gnn_all

    def _L3_gnn_setup():
        import jax, jax.numpy as jnp
        import numpy as np
        NUM_EDGE_TYPES = 8
        HIDDEN = 128
        N_NODES = 50000
        N_EDGES = 9375

        def _gru_cell(x, h, W_ih, W_hh, b_ih, b_hh):
            H = h.shape[-1]
            gi = x @ W_ih.T + b_ih
            gh = h @ W_hh.T + b_hh
            i_r, i_z, i_n = (gi[:, :H], gi[:, H:2 * H], gi[:, 2 * H:])
            h_r, h_z, h_n = (gh[:, :H], gh[:, H:2 * H], gh[:, 2 * H:])
            r = jax.nn.sigmoid(i_r + h_r)
            z = jax.nn.sigmoid(i_z + h_z)
            n = jnp.tanh(i_n + r * h_n)
            return (1.0 - z) * n + z * h
        key = jax.random.key(seed)
        ks = jax.random.split(key, 10)
        H = HIDDEN
        h = jax.random.normal(ks[0], (N_NODES, H), dtype=jnp.float32)
        edge_index = jax.random.randint(ks[1], (2, N_EDGES), 0, N_NODES, dtype=jnp.int32)
        edge_type = jax.random.randint(ks[2], (N_EDGES,), 0, NUM_EDGE_TYPES + 1, dtype=jnp.int32)
        s = 1.0 / np.sqrt(H)
        W_msg = jax.random.uniform(ks[3], (H, H), jnp.float32, -s, s)
        b_msg = jax.random.uniform(ks[4], (H,), jnp.float32, -s, s)
        edge_embed = jax.random.normal(ks[5], (NUM_EDGE_TYPES + 1, H), dtype=jnp.float32)
        W_ih = jax.random.uniform(ks[6], (3 * H, H), jnp.float32, -s, s)
        W_hh = jax.random.uniform(ks[7], (3 * H, H), jnp.float32, -s, s)
        b_ih = jax.random.uniform(ks[8], (3 * H,), jnp.float32, -s, s)
        b_hh = jax.random.uniform(ks[9], (3 * H,), jnp.float32, -s, s)
        return {'h': h, 'edge_index': edge_index, 'edge_type': edge_type, 'num_nodes': N_NODES, 'W_msg': W_msg, 'b_msg': b_msg, 'edge_embed': edge_embed, 'W_ih': W_ih, 'W_hh': W_hh, 'b_ih': b_ih, 'b_hh': b_hh}
    _L3_gnn_all = _L3_gnn_setup()
    _L3_gnn_in = {k: v for k, v in _L3_gnn_all.items() if k in ('W_msg', 'b_msg', 'edge_embed', 'W_ih', 'W_hh', 'b_ih', 'b_hh')}
    del _L3_gnn_all
    return {'x': x, 'src': src, 'dst': dst, 'edge_type_9': edge_type_9, 'edge_weight1': edge_weight1, 'L0_gnn_W': _L0_gnn_in['W'], 'L1_gnn_bn0_gamma': _L1_gnn_in['bn0_gamma'], 'L1_gnn_bn0_beta': _L1_gnn_in['bn0_beta'], 'L1_gnn_W1': _L1_gnn_in['W1'], 'L1_gnn_b1': _L1_gnn_in['b1'], 'L1_gnn_bn1_gamma': _L1_gnn_in['bn1_gamma'], 'L1_gnn_bn1_beta': _L1_gnn_in['bn1_beta'], 'L1_gnn_W2': _L1_gnn_in['W2'], 'L1_gnn_b2': _L1_gnn_in['b2'], 'L1_gnn_bn2_gamma': _L1_gnn_in['bn2_gamma'], 'L1_gnn_bn2_beta': _L1_gnn_in['bn2_beta'], 'L2_gnn_W': _L2_gnn_in['W'], 'L2_gnn_b': _L2_gnn_in['b'], 'L3_gnn_W_msg': _L3_gnn_in['W_msg'], 'L3_gnn_b_msg': _L3_gnn_in['b_msg'], 'L3_gnn_edge_embed': _L3_gnn_in['edge_embed'], 'L3_gnn_W_ih': _L3_gnn_in['W_ih'], 'L3_gnn_W_hh': _L3_gnn_in['W_hh'], 'L3_gnn_b_ih': _L3_gnn_in['b_ih'], 'L3_gnn_b_hh': _L3_gnn_in['b_hh']}

def reference(x, src, dst, edge_type_9, edge_weight1, L0_gnn_W, L1_gnn_bn0_gamma, L1_gnn_bn0_beta, L1_gnn_W1, L1_gnn_b1, L1_gnn_bn1_gamma, L1_gnn_bn1_beta, L1_gnn_W2, L1_gnn_b2, L1_gnn_bn2_gamma, L1_gnn_bn2_beta, L2_gnn_W, L2_gnn_b, L3_gnn_W_msg, L3_gnn_b_msg, L3_gnn_edge_embed, L3_gnn_W_ih, L3_gnn_W_hh, L3_gnn_b_ih, L3_gnn_b_hh):
    import jax
    import jax.numpy as jnp

    def _L0_gnn_ref(x, src, dst, num_nodes, W):
        import jax, jax.numpy as jnp
        import numpy as np
        msgs = x[src]
        summed = jax.ops.segment_sum(msgs, dst, num_segments=num_nodes)
        deg = jax.ops.segment_sum(jnp.ones_like(dst, dtype=x.dtype), dst, num_segments=num_nodes)
        agg = summed / jnp.maximum(deg, 1.0)[:, None]
        h = jnp.concatenate([x, agg], axis=1)
        out = h @ W.T
        return jax.nn.relu(out)

    def _L1_gnn_ref(x, edge_index, bn0_gamma, bn0_beta, W1, b1, bn1_gamma, bn1_beta, W2, b2, bn2_gamma, bn2_beta):
        import jax, jax.numpy as jnp
        import numpy as np
        N_NODES = 100000
        EPS = 1e-05

        def batch_norm(x, gamma, beta):
            mu = jnp.mean(x, axis=0)
            var = jnp.mean(jnp.square(x - mu), axis=0)
            return gamma * (x - mu) * jax.lax.rsqrt(var + EPS) + beta

        def gcn_conv(x, W, b, src, dst, n):
            h = x @ W
            ones = jnp.ones(src.shape[0], dtype=x.dtype)
            deg = jax.ops.segment_sum(ones, dst, num_segments=n) + 1.0
            dinv = jax.lax.rsqrt(deg)
            norm = dinv[src] * dinv[dst]
            agg = jax.ops.segment_sum(h[src] * norm[:, None], dst, num_segments=n)
            agg = agg + h * jnp.square(dinv)[:, None]
            return agg + b
        n = x.shape[0]
        src, dst = (edge_index[0], edge_index[1])
        x_norm = batch_norm(x, bn0_gamma, bn0_beta)
        h = batch_norm(jax.nn.relu(gcn_conv(x_norm, W1, b1, src, dst, n)), bn1_gamma, bn1_beta)
        h = batch_norm(jax.nn.relu(gcn_conv(h, W2, b2, src, dst, n)), bn2_gamma, bn2_beta)
        return x_norm + h

    def _L2_gnn_ref(x_hidden, edge_index, edge_attr, W, b):
        import jax, jax.numpy as jnp
        import numpy as np
        N_NODES = 50000
        N_EDGES = 12500
        HIDDEN = 128
        src, dst = (edge_index[0], edge_index[1])
        msg = x_hidden[src] * edge_attr[:, 0:1]
        agg = jax.ops.segment_sum(msg, dst, num_segments=x_hidden.shape[0])
        h = jax.nn.gelu(agg)
        return jax.nn.gelu(h @ W.T + b)

    def _L3_gnn_ref(h, edge_index, edge_type, num_nodes, W_msg, b_msg, edge_embed, W_ih, W_hh, b_ih, b_hh):
        import jax, jax.numpy as jnp
        import numpy as np
        NUM_EDGE_TYPES = 8
        HIDDEN = 128
        N_NODES = 50000
        N_EDGES = 9375

        def _gru_cell(x, h, W_ih, W_hh, b_ih, b_hh):
            H = h.shape[-1]
            gi = x @ W_ih.T + b_ih
            gh = h @ W_hh.T + b_hh
            i_r, i_z, i_n = (gi[:, :H], gi[:, H:2 * H], gi[:, 2 * H:])
            h_r, h_z, h_n = (gh[:, :H], gh[:, H:2 * H], gh[:, 2 * H:])
            r = jax.nn.sigmoid(i_r + h_r)
            z = jax.nn.sigmoid(i_z + h_z)
            n = jnp.tanh(i_n + r * h_n)
            return (1.0 - z) * n + z * h
        src = edge_index[0]
        dst = edge_index[1]
        src_h = h[src] @ W_msg.T + b_msg
        emb = edge_embed[jnp.clip(edge_type, 0, NUM_EDGE_TYPES)]
        msg = src_h + emb
        messages = jax.ops.segment_sum(msg, dst, num_segments=num_nodes)
        h_new = _gru_cell(messages, h[:num_nodes], W_ih, W_hh, b_ih, b_hh)
        result = jnp.zeros_like(h).at[:num_nodes].set(h_new)
        return result
    edge_index = jnp.stack([src, dst])
    h = jnp.maximum(_layernorm(x, axis=-1), 0.0)
    x = x + _L0_gnn_ref(h, src, dst, 50000, L0_gnn_W)
    h = jnp.maximum(_layernorm(x, axis=-1), 0.0)
    x = x + _L1_gnn_ref(h, edge_index, L1_gnn_bn0_gamma, L1_gnn_bn0_beta, L1_gnn_W1, L1_gnn_b1, L1_gnn_bn1_gamma, L1_gnn_bn1_beta, L1_gnn_W2, L1_gnn_b2, L1_gnn_bn2_gamma, L1_gnn_bn2_beta)
    h = jnp.maximum(_layernorm(x, axis=-1), 0.0)
    x = x + _L2_gnn_ref(h, edge_index, edge_weight1, L2_gnn_W, L2_gnn_b)
    h = jnp.maximum(_layernorm(x, axis=-1), 0.0)
    x = x + _L3_gnn_ref(h, edge_index, edge_type_9, 50000, L3_gnn_W_msg, L3_gnn_b_msg, L3_gnn_edge_embed, L3_gnn_W_ih, L3_gnn_W_hh, L3_gnn_b_ih, L3_gnn_b_hh)
    return x

_drawn_inputs = setup_inputs


def setup_inputs(seed=0):
    import zlib

    import numpy as np

    out = dict(_drawn_inputs(seed))
    spreads = {'L1_gnn_bn0_gamma': (1.0, 0.2),
     'L1_gnn_bn0_beta': (0.0, 0.1),
     'L1_gnn_b1': (0.0, 0.1),
     'L1_gnn_bn1_gamma': (1.0, 0.2),
     'L1_gnn_bn1_beta': (0.0, 0.283),
     'L1_gnn_b2': (0.0, 0.1),
     'L1_gnn_bn2_gamma': (1.0, 0.2),
     'L1_gnn_bn2_beta': (0.0, 0.1)}
    factors = {'L2_gnn_b': 4.983, 'L3_gnn_b_msg': 8.0, 'L3_gnn_b_ih': 5.464, 'L3_gnn_b_hh': 8.0}
    for name, (base, spread) in spreads.items():
        noise = np.random.default_rng([zlib.crc32(name.encode()), seed]).standard_normal(out[name].shape)
        drawn = base * np.exp(spread * noise) if base else spread * noise
        out[name] = jnp.asarray(drawn.astype(out[name].dtype))
    for name, factor in factors.items():
        out[name] = (out[name] * factor).astype(out[name].dtype)
    return out
```

```python
import numpy as np
import concourse.bass as bass
from concourse import mybir

N_NODES, N_EDGES, F = 50000, 25000, 128
P = 128
STEPS = 49
NT = 8
ET = 4
NODE_TILES, EDGE_TILES = STEPS * NT, STEPS * ET
NPAD, EPAD = NODE_TILES * P, EDGE_TILES * P
W1C = F + 4
NTYPES = 9
EPS = 1e-5
DST_NONE = 60000
LAST_ROWS = N_NODES - (NODE_TILES - 2) * P

PHASES = ["E0", "A1", "E1", "A3", "E2", "A5", "A6", "E3", "A7", "E4", "A8"]
EDGE = ["E0", "E1", "E2", "E3", "E4"]
LN_EDGE = ["E0", "E1", "E3", "E4"]
DENSE = ["A1", "A3", "A5", "A6", "A7", "A8"]


class Stage:

    def __init__(self, nc, name, per):
        self.sem = nc.alloc_semaphore(name)
        self.per = per

    def before(self, phase):
        return sum(STEPS * self.per.get(p, 0) for p in PHASES[:PHASES.index(phase)])

    def at(self, phase, step, k=None):
        per = self.per[phase]
        return step * per + (self.before(phase) + (per if k is None else k))

    def end(self, phase):
        return self.before(phase) + STEPS * self.per.get(phase, 0)


class Slots:

    def __init__(self, nc, name, per):
        self.sems = [nc.alloc_semaphore(f"{name}{s}") for s in range(2)]
        self.per = per

    def uses(self, phase, s):
        return self.per.get(phase, 0) * (STEPS + 1 - s) // 2

    def before(self, phase, s):
        return 16 * sum(self.per.get(p, 0) * ((STEPS + 1 - s) // 2) for p in PHASES[:PHASES.index(phase)])

    def at(self, phase, half, s):
        per = 16 * self.per[phase]
        return half * per + (self.before(phase, s) + per)

    def end(self, phase, s):
        return self.before(phase, s) + 16 * self.per.get(phase, 0) * ((STEPS + 1 - s) // 2)


def steps(eng, body):
    body(0, 0, 0)
    body(1, 0, 1)
    with eng.Fori(1, STEPS // 2) as half:
        body(half * 2, half, 0)
        body(half * 2 + 1, half, 1)
    body(STEPS - 1, STEPS // 2, 0)


def build(nc, x, gidx_d, dst_d, nxt_d, typ_d, wgt_d, dstrow_d, WaT, WbT, W1, W2, WL2T, WmT, WihT, WhhT,
          emb, vecs, rows, b3, out):
    f32, u32, i32 = mybir.dt.float32, mybir.dt.uint32, mybir.dt.int32
    bf16, u16 = mybir.dt.bfloat16, mybir.dt.uint16
    ALU, ACT, AX = mybir.AluOpType, mybir.ActivationFunctionType, mybir.AxisListType
    add, sub, mul, mx, eq = ALU.add, ALU.subtract, ALU.mult, ALU.max, ALU.is_equal

    def sb(name, shape, dt=f32):
        return nc.alloc_sbuf_tensor(name, shape, dt)

    def sem(name):
        return nc.alloc_semaphore(name)

    x1_d = nc.dram_tensor("x1_rows", [NPAD, W1C], f32).ap()
    t1_d = nc.dram_tensor("t1_rows", [NPAD, F], f32).ap()
    t2_d = nc.dram_tensor("t2_rows", [NPAD, F], f32).ap()
    x2_d = nc.dram_tensor("x2_rows", [NPAD, F], f32).ap()
    x3_d = nc.dram_tensor("x3_rows", [NPAD, F], f32).ap()
    agg_d = nc.dram_tensor("agg_rows", [NPAD, F], f32).ap()
    gates_d = nc.dram_tensor("gate_rows", [NPAD, 3 * F], f32).ap()

    def node_view(ap):
        return ap.rearrange("(c k p) f -> c p k f", k=NT, p=P)

    ident, ones = sb("ident", [P, P]), sb("ones", [P, P])
    iota_lo, iota_hi = sb("iota_lo", [P, P]), sb("iota_hi", [P, NODE_TILES])
    wa, wb = sb("wa", [P, F]), sb("wb", [P, F])
    w1, w2, wl2, wm = sb("w1", [P, F]), sb("w2", [P, F]), sb("wl2", [P, F]), sb("wm", [P, F])
    wih, whh = sb("wih", [P, 3 * F]), sb("whh", [P, 3 * F])
    emb_sb, bmsg_sb = sb("emb_sb", [NTYPES, F]), sb("bmsg_sb", [NTYPES, F])
    vec = sb("vec", [P, 6])
    row = sb("row", [P, 3, F])
    brow = sb("brow", [P, 7 * F])
    bgate = sb("bgate", [P, 4, 3 * F])
    zeros = sb("zeros", [P, NT * F])
    zero_col, eps_col = sb("zero_col", [P, 1]), sb("eps_col", [P, 1])
    gidx, scat = sb("gidx", [P, EDGE_TILES], u32), sb("scat", [P, EDGE_TILES], u32)
    dst_i, nxt_i = sb("dst_i", [P, EDGE_TILES], i32), sb("nxt_i", [P, EDGE_TILES], i32)
    dst_f, nxt_f = sb("dst_f", [P, EDGE_TILES]), sb("nxt_f", [P, EDGE_TILES])
    hi_f, lo_f = sb("hi_f", [P, EDGE_TILES]), sb("lo_f", [P, EDGE_TILES])
    typ_i, typ_f = sb("typ_i", [P, EDGE_TILES], i32), sb("typ_f", [P, EDGE_TILES])
    wgt = sb("wgt", [P, EDGE_TILES])
    dinv_src = sb("dinv_src", [P, EDGE_TILES])
    dst_row = sb("dst_row", [P, 1 + EPAD], u16)
    dst_row_i = sb("dst_row_i", [P, 2, EPAD // 64], i32)
    deg, rdeg = sb("deg", [P, NODE_TILES]), sb("rdeg", [P, NODE_TILES])
    sqd, dinv, dinv2 = sb("sqd", [P, NODE_TILES]), sb("dinv", [P, NODE_TILES]), sb("dinv2", [P, NODE_TILES])
    mean, rstd = sb("mean", [P, NODE_TILES]), sb("rstd", [P, NODE_TILES])
    valid = sb("valid", [P, 1])
    bn_col = sb("bn_col", [P, 8])
    bn_tmp = sb("bn_tmp", [P, P])
    diag_a, diag_c = sb("diag_a", [P, P]), sb("diag_c", [P, P])
    a_col, c_col = [sb(f"a_col{i}", [P, 1]) for i in range(3)], [sb(f"c_col{i}", [P, 1]) for i in range(3)]
    a_row, c_row = [sb(f"a_row{i}", [P, F]) for i in range(3)], [sb(f"c_row{i}", [P, F]) for i in range(3)]

    eidx = sb("eidx", [P, 2, 2 * ET], u32)
    msg = [sb(f"msg{s}", [P, ET, F]) for s in range(2)]
    msgw = [sb(f"msgw{s}", [P, ET, W1C]) for s in range(2)]
    ecol = [sb(f"ecol{s}", [P, 4, ET]) for s in range(2)]
    est, emv = sb("est", [P, ET, 6]), sb("emv", [P, ET, 2])
    estd, ers, eww = sb("estd", [P, ET]), sb("ers", [P, ET]), sb("eww", [P, ET])
    sel = [sb(f"sel{s}", [P, ET, P]) for s in range(2)]
    onehot = [sb(f"onehot{s}", [P, ET, NTYPES]) for s in range(2)]
    cmask = sb("cmask", [P, P])
    segT = [sb(f"segT{s}", [P, ET * P]) for s in range(2)]
    act_in = sb("act_in", [P, ET * P])
    cnt = sb("cnt", [NTYPES, ET * P])
    res = [sb(f"res{s}", [P, ET, F]) for s in range(2)]
    oh_lo, oh_hi = sb("oh_lo", [P, ET, P], bf16), sb("oh_hi", [P, ET, NODE_TILES], bf16)

    xin = [sb(f"xin{s}", [P, NT, F]) for s in range(2)]
    din = [sb(f"din{s}", [P, NT, F]) for s in range(2)]
    din3 = [sb(f"din3{s}", [P, NT, 3 * F]) for s in range(2)]
    res3 = [din3[s][:, 0:ET, :] for s in range(2)]
    ncol = [sb(f"ncol{s}", [P, 4, NT]) for s in range(2)]
    nst, nmv = sb("nst", [P, NT, 6]), sb("nmv", [P, NT, 2])
    nstd, nrs, nbias = sb("nstd", [P, NT]), sb("nrs", [P, NT]), sb("nbias", [P, NT])
    z = sb("z", [P, NT, F])
    zT = sb("zT", [P, NT * F])
    yout = [sb(f"yout{s}", [P, NT, W1C]) for s in range(2)]
    hbuf = sb("hbuf", [P, NT, F + 1])
    rz = sb("rz", [P, 4, 2 * F])

    bank = [nc.alloc_psum_tensor(f"bank{i}", [P, 512], f32) for i in range(8)]
    seg_ps, out_ps = bank[0:2], bank[2:4]
    cnt_ps, msg_ps = bank[4], bank[5]
    tp_ps, y_ps, gram_ps = bank[0:2], bank[2:4], bank[7]
    deg_ps = bank[6]

    D = DENSE
    loaded = Slots(nc, "loaded", {p: 1 for p in ["E0"] + D})
    agg_in = Slots(nc, "agg_in", {p: 1 for p in D})
    stored = Slots(nc, "stored", {p: 1 for p in D})
    gathered = Slots(nc, "gathered", {p: ET for p in EDGE})
    scattered = Slots(nc, "scattered", {p: ET for p in EDGE})
    idx_ok = Stage(nc, "idx_ok", {p: 1 for p in EDGE})
    cols_ok = Stage(nc, "cols_ok", {p: 3 for p in EDGE})
    estats = Stage(nc, "estats", {p: ET for p in LN_EDGE})
    emoments = Stage(nc, "emoments", {p: ET for p in LN_EDGE})
    ers_ok = Stage(nc, "ers_ok", {p: 1 for p in LN_EDGE})
    eww_ok = Stage(nc, "eww_ok", {p: 1 for p in EDGE})
    centred = Stage(nc, "centred", {p: ET for p in LN_EDGE})
    scaled = Stage(nc, "scaled", {"E1": ET, "E2": 1, "E4": ET})
    msg_ok = Stage(nc, "msg_ok", {"E1": 1, "E2": 1})
    sel_ok = Stage(nc, "sel_ok", {p: ET for p in EDGE})
    onehot_ok = Stage(nc, "onehot_ok", {"E4": ET})
    mask_ok = Stage(nc, "mask_ok", {p: ET for p in EDGE})
    seg_ok = Stage(nc, "seg_ok", {p: ET for p in EDGE})
    res_ok = Stage(nc, "res_ok", {p: ET if p == "E4" else 1 for p in EDGE})
    oh_ok = Stage(nc, "oh_ok", {"E0": 2 * ET})
    estd_ok = Stage(nc, "estd_ok", {p: 1 for p in LN_EDGE})
    act_ok = Stage(nc, "act_ok", {"E3": 1, "E4": 2})
    seg_done = Stage(nc, "seg_done", {p: 1 for p in EDGE})
    msg_done = Stage(nc, "msg_done", {"E4": 1})
    out_done = Stage(nc, "out_done", {p: ET if p == "E4" else 1 for p in EDGE})
    deg_done = Stage(nc, "deg_done", {"E0": 1})
    ST = ["E0", "A1", "A6", "A7"]
    ncols_ok = Stage(nc, "ncols_ok", {p: 4 for p in D})
    z_ok = Stage(nc, "z_ok", {"A1": NT, "A3": NT, "A6": NT, "A8": NT})
    agg_ok = Stage(nc, "agg_ok", {"A1": NT, "A3": NT, "A5": NT, "A6": 1, "A7": 1})
    tp_done = Stage(nc, "tp_done", {"A1": 2, "A3": 2, "A5": 2, "A8": 2})
    zT_raw = Stage(nc, "zT_raw", {"A3": 2})
    zT_ok = Stage(nc, "zT_ok", {"A1": 2, "A3": 2, "A5": 2, "A8": 2})
    y_done = Stage(nc, "y_done", {"A1": 2, "A3": 2, "A5": 2, "A8": NT})
    y_raw = Stage(nc, "y_raw", {"A3": NT, "A5": NT, "A6": 4})
    y_sum = Stage(nc, "y_sum", {"A6": 1})
    y_ok = Stage(nc, "y_ok", {"A1": 2, "A3": 1, "A5": 1, "A6": 1, "A7": 1, "A8": 2})
    gelu_ok = Stage(nc, "gelu_ok", {"A7": 1})
    nstats = Stage(nc, "nstats", {p: NT for p in ST})
    nmoments = Stage(nc, "nmoments", {p: NT for p in ST})
    nstd_ok = Stage(nc, "nstd_ok", {p: 1 for p in ST})
    nrs_ok = Stage(nc, "nrs_ok", {p: 1 for p in ST})
    kept = Stage(nc, "kept", {p: 2 for p in ST})
    nbias_ok = Stage(nc, "nbias_ok", {"A1": 1})
    h_ok = Stage(nc, "h_ok", {"A1": NT})
    gram_done = Stage(nc, "gram_done", {"A1": 1, "A3": 1, "A5": 1})
    gate_ok = Stage(nc, "gate_ok", {"A8": NT})
    hn_ok = Stage(nc, "hn_ok", {"A8": NT})
    rhn_ok = Stage(nc, "rhn_ok", {"A8": 2})
    nin_ok = Stage(nc, "nin_ok", {"A8": 2})
    tanh_ok = Stage(nc, "tanh_ok", {"A8": 2})
    hmn_ok = Stage(nc, "hmn_ok", {"A8": 2})
    zhn_ok = Stage(nc, "zhn_ok", {"A8": 2})
    nzh_ok = Stage(nc, "nzh_ok", {"A8": 2})
    consts, weights_in, edges_in, row_in = sem("consts"), sem("weights_in"), sem("edges_in"), [sem("row_in0"), sem("row_in1")]
    filled, gates_filled, prep = sem("filled"), sem("gates_filled"), sem("prep")
    rowcast, bgate_ok, ready, degs = sem("rowcast"), sem("bgate_ok"), sem("ready"), sem("degs")
    last_ok = Stage(nc, "last_ok", {p: 1 for p in EDGE})
    lastcol = [sb(f"lastcol{s}", [P, ET]) for s in range(2)]
    coef_end, ones_ok = sem("coef_end"), sem("ones_ok")
    coef, coef_std, coef_rows, coef_ready, passed = (sem("coef"), sem("coef_std"), sem("coef_rows"),
                                                     sem("coef_ready"), sem("passed"))
    READY = 1
    W_DMAS, E_DMAS = 8 + 2 + 1 + 3 + 2, 6
    ROWC = EPAD // 64
    COEF_OF = {"A1": 0, "A3": 1, "A5": 2}
    SRC = {"E0": x, "E1": x1_d, "E2": t1_d, "E3": x2_d, "E4": x3_d}
    XIN = {"A1": x, "A3": x1_d, "A5": t1_d, "A6": x1_d, "A7": x2_d, "A8": x3_d}
    DIN = {"A1": agg_d, "A3": agg_d, "A5": agg_d, "A6": t2_d, "A7": agg_d, "A8": gates_d}
    OUT = {"A1": x1_d, "A3": t1_d, "A5": t2_d, "A6": x2_d, "A7": x3_d, "A8": out}
    EW = {"E0": wb, "E1": w1, "E2": w2, "E3": wl2}
    NW = {"A1": wa, "A3": w1, "A5": w2}

    def held(eng, semaphore, value):
        eng.wait_ge(semaphore, value)
        eng.sem_inc(passed, 1)

    def gate(eng, phase):
        if phase == "E0":
            return
        last = PHASES[PHASES.index(phase) - 1]
        landed = scattered if last in EDGE else stored
        for s in range(2):
            held(eng, landed.sems[s], landed.end(last, s))
        if last in COEF_OF:
            held(eng, coef_ready, COEF_OF[last] + 1)

    with nc.Block() as block:

        @block.sync
        def _(sp):
            for a, b in ((gidx, gidx_d), (dst_i, dst_d), (nxt_i, nxt_d), (typ_i, typ_d), (wgt, wgt_d)):
                sp.dma_start(a[:], b).then_inc(edges_in, 16)
            sp.dma_start(vec[:], vecs).then_inc(edges_in, 16)
            for i in range(64):
                if i >= 2:
                    sp.wait_ge(rowcast, i - 1)
                sp.dma_start(dst_row_i[:, i % 2, :],
                             dstrow_d[0:1, i * ROWC:(i + 1) * ROWC].to_broadcast([P, ROWC])).then_inc(row_in[i % 2], 16)
            for a, b in ((wa, WaT), (wb, WbT), (w1, W1), (w2, W2), (wl2, WL2T), (wm, WmT), (wih, WihT), (whh, WhhT)):
                sp.dma_start(a[:], b).then_inc(weights_in, 16)
            sp.dma_start(emb_sb[:], emb).then_inc(weights_in, 16)
            sp.dma_start(bmsg_sb[:], rows[3:4, :].to_broadcast([NTYPES, F])).then_inc(weights_in, 16)
            sp.dma_start(brow[:, 0:6 * F], b3.to_broadcast([P, 6 * F])).then_inc(weights_in, 16)
            for i in range(3):
                sp.dma_start(row[:, i, :], rows[i:i + 1, :].to_broadcast([P, F])).then_inc(weights_in, 16)

            def dense_in(ph):
                src = node_view(XIN[ph])[:, :, :, 0:F] if ph != "E0" else node_view(x)
                if ph != "E0":
                    other = node_view(DIN[ph])

                def body(c, half, s):
                    if not (isinstance(c, int) and c < 2):
                        if ph == "E0":
                            held(sp, nstats.sem, nstats.at(ph, c - 2))
                        else:
                            held(sp, y_ok.sem, y_ok.at(ph, c - 2))
                    sp.dma_start(xin[s][:], src[c]).then_inc(loaded.sems[s], 16)
                    if ph != "E0":
                        target = din3[s] if ph == "A8" else din[s]
                        sp.dma_start(target[:], other[c]).then_inc(agg_in.sems[s], 16)
                    if ph == "E0":
                        gv = gates_d.rearrange("(c k p) f -> c p k f", k=4, p=P)
                        if isinstance(c, int) and c == 0:
                            held(sp, bgate_ok, 2)
                        sp.dma_start(gv[c * 2], bgate[:]).then_inc(gates_filled, 16)
                        sp.dma_start(gv[c * 2 + 1], bgate[:]).then_inc(gates_filled, 16)
                steps(sp, body)

            for ph in PHASES:
                gate(sp, ph)
                if ph == "E0" or ph in DENSE:
                    dense_in(ph)
            sp.wait_ge(gates_filled, 16 * 2 * STEPS)
            for s in range(2):
                sp.wait_ge(stored.sems[s], stored.end("A8", s))

        @block.gpsimd
        def _(pool):
            nc.gpsimd.memset(ident[:], 0.0).then_inc(consts, 1)
            nc.gpsimd.memset(ones[:], 1.0).then_inc(consts, 1)
            nc.gpsimd.iota(iota_lo[:], [[1, P]], base=0, channel_multiplier=0,
                           allow_small_or_imprecise_dtypes=True).then_inc(consts, 1)
            nc.gpsimd.iota(iota_hi[:], [[1, NODE_TILES]], base=0, channel_multiplier=0,
                           allow_small_or_imprecise_dtypes=True).then_inc(consts, 1)
            nc.gpsimd.memset(valid[:], 1.0).then_inc(consts, 1)
            pool.wait_ge(consts, 5)
            nc.gpsimd.affine_select(out=ident[:], in_=ident[:], compare_op=ALU.not_equal, fill=1.0, base=0,
                                    pattern=[[-1, P]], channel_multiplier=1).then_inc(consts, 1)
            nc.gpsimd.affine_select(out=valid[:], in_=valid[:], compare_op=ALU.is_gt, fill=0.0, base=LAST_ROWS,
                                    pattern=[[0, 1]], channel_multiplier=-1).then_inc(consts, 1)

            def edge(ph):
                table = SRC[ph]
                dest = gates_d if ph == "E4" else agg_d

                def scatter(c, half, s):
                    held(pool, res_ok.sem, res_ok.at(ph, c))
                    for k in range(ET):
                        src = (res3 if ph == "E4" else res)[s][:, k, :]
                        pool.indirect_dma_start(
                            out=dest, out_offset=bass.IndirectOffsetOnAxis(ap=eidx[:, s, ET + k:ET + k + 1], axis=0),
                            in_=src, in_offset=None, bounds_check=NPAD - 1, oob_is_err=False,
                        ).then_inc(scattered.sems[s], 16)

                def body(c, half, s):
                    first = isinstance(c, int) and c < 2
                    if not first:
                        held(pool, scattered.sems[s], scattered.at(ph, half - 1, s))
                        held(pool, seg_done.sem, seg_done.at(ph, c - 2))
                    nc.gpsimd.tensor_copy(eidx[:, s, 0:ET], gidx[:, bass.ds(c * ET, ET)])
                    nc.gpsimd.tensor_copy(eidx[:, s, ET:2 * ET], scat[:, bass.ds(c * ET, ET)]).then_inc(idx_ok.sem, 1)
                    held(pool, idx_ok.sem, idx_ok.at(ph, c))
                    for k in range(ET):
                        to = msgw[s][:, k, :] if ph == "E1" else msg[s][:, k, :]
                        pool.indirect_dma_start(
                            out=to, out_offset=None, in_=table,
                            in_offset=bass.IndirectOffsetOnAxis(ap=eidx[:, s, k:k + 1], axis=0),
                        ).then_inc(gathered.sems[s], 16)
                    if not (isinstance(c, int) and c == 0):
                        scatter(c - 1, half - 1 if s == 0 else half, 1 - s)
                steps(pool, body)
                scatter(STEPS - 1, STEPS // 2, 0)

            held(pool, ready, READY)
            held(pool, filled, 16 * STEPS)
            for ph in PHASES:
                gate(pool, ph)
                if ph in EDGE:
                    if ph == "E4":
                        held(pool, gates_filled, 16 * 2 * STEPS)
                    edge(ph)
                elif ph == "A6":
                    def body(c, half, s):
                        held(pool, agg_in.sems[s], agg_in.at("A6", half, s))
                        nc.gpsimd.tensor_tensor(din[s][:], din[s][:], a_row[2][:, None, :].to_broadcast([P, NT, F]),
                                                mul).then_inc(agg_ok.sem, 1)
                    steps(pool, body)

        @block.scalar
        def _(act):
            act.wait_ge(prep, 1)
            av = node_view(agg_d)
            zv = zeros[:].rearrange("p (k f) -> p k f", k=NT)
            with act.Fori(0, STEPS) as c:
                act.dma_start(av[c], zv).then_inc(filled, 16)

            def root(dst, src):
                return nc.scalar.activation(dst, src, ACT.Sqrt, bias=eps_col[:])

            def node_std(ph, c):
                act.wait_ge(nmoments.sem, nmoments.at(ph, c))
                root(nstd[:], nmv[:, :, 1]).then_inc(nstd_ok.sem, 1)

            def edge(ph):
                def body(c, half, s):
                    if ph in LN_EDGE:
                        act.wait_ge(emoments.sem, emoments.at(ph, c))
                        root(estd[:], emv[:, :, 1]).then_inc(estd_ok.sem, 1)
                    if ph == "E0":
                        node_std(ph, c)
                    if ph == "E3":
                        act.wait_ge(seg_ok.sem, seg_ok.at(ph, c))
                        nc.scalar.activation(act_in[:], segT[s][:], ACT.Gelu_apprx_tanh).then_inc(act_ok.sem, 1)
                    if ph == "E4":
                        act.wait_ge(seg_done.sem, seg_done.at(ph, c))
                        nc.scalar.copy(act_in[:], seg_ps[s][:]).then_inc(act_ok.sem, 1)
                        nc.scalar.copy(cnt[:], cnt_ps[0:NTYPES, :]).then_inc(act_ok.sem, 1)
                    else:
                        if not (isinstance(c, int) and c < 2):
                            act.wait_ge(scattered.sems[s], scattered.at(ph, half - 1, s))
                        act.wait_ge(out_done.sem, out_done.at(ph, c))
                        nc.scalar.copy(res[s][:].rearrange("p k f -> p (k f)"), out_ps[s][:]).then_inc(res_ok.sem, 1)
                steps(act, body)

            def dense(ph):
                ov = node_view(OUT[ph])

                def body(c, half, s):
                    if ph in ("A1", "A5", "A3", "A8"):
                        for g in range(2):
                            cols = slice(g * 4 * F, (g + 1) * 4 * F)
                            act.wait_ge(tp_done.sem, tp_done.at(ph, c, g + 1))
                            if ph == "A5":
                                nc.scalar.activation(zT[:, cols], tp_ps[g][:], ACT.Identity, bias=c_col[1][:],
                                                     scale=a_col[1][:]).then_inc(zT_ok.sem, 1)
                            else:
                                ready_to = zT_raw if ph == "A3" else zT_ok
                                nc.scalar.activation(zT[:, cols], tp_ps[g][:], ACT.Relu).then_inc(ready_to.sem, 1)
                    if ph == "A7":
                        act.wait_ge(agg_ok.sem, agg_ok.at(ph, c))
                        nc.scalar.activation(z[:], din[s][:], ACT.Gelu_apprx_tanh).then_inc(gelu_ok.sem, 1)
                    if ph == "A8":
                        for g in range(2):
                            for k in range(4 * g, 4 * g + 4):
                                act.wait_ge(y_done.sem, y_done.at(ph, c, k + 1))
                                if g == 1 or not (isinstance(c, int) and c == 0):
                                    if g == 1:
                                        act.wait_ge(zhn_ok.sem, zhn_ok.at(ph, c, 1))
                                    else:
                                        act.wait_ge(zhn_ok.sem, zhn_ok.at(ph, c - 1, 2))
                                nc.scalar.activation(rz[:, k % 4, :], bank[2 + k % 4][:, 0:2 * F],
                                                     ACT.Sigmoid).then_inc(gate_ok.sem, 1)
                            act.wait_ge(nin_ok.sem, nin_ok.at(ph, c, g + 1))
                            n4 = hbuf[:, 4 * g:4 * g + 4, 0:F]
                            nc.scalar.activation(n4, n4, ACT.Tanh).then_inc(tanh_ok.sem, 1)
                    if ph in ST:
                        node_std(ph, c)
                    if ph == "A1":
                        act.wait_ge(nbias_ok.sem, nbias_ok.at(ph, c))
                        if not (isinstance(c, int) and c == 0):
                            act.wait_ge(gram_done.sem, gram_done.at(ph, c - 1))
                        for k in range(NT):
                            nc.scalar.activation(hbuf[:, k, 0:F], yout[s][:, k, 0:F], ACT.Relu,
                                                 bias=nbias[:, k:k + 1], scale=nrs[:, k:k + 1]).then_inc(h_ok.sem, 1)
                    held(act, y_ok.sem, y_ok.at(ph, c))
                    width = W1C if ph == "A1" else F
                    act.dma_start(ov[c], yout[s][:, :, 0:width]).then_inc(stored.sems[s], 16)
                steps(act, body)
                if ph in COEF_OF:
                    i = COEF_OF[ph]
                    act.wait_ge(coef, 9 * i + 5)
                    root(bn_col[:, 4:5], bn_col[:, 3:4]).then_inc(coef_std, 1)

            act.wait_ge(weights_in, 16 * 14)
            for ph in PHASES:
                gate(act, ph)
                if ph in EDGE:
                    edge(ph)
                    if ph == "E0":
                        act.wait_ge(degs, 2)
                        nc.scalar.activation(sqd[:], sqd[:], ACT.Sqrt).then_inc(degs, 1)
                else:
                    dense(ph)

        @block.tensor
        def _(pe):
            pe.wait_ge(consts, 7)
            pe.wait_ge(weights_in, 16 * 14)

            def edge(ph):
                def weight(c, half, s):
                    src = {"E3": act_in}.get(ph, segT[s])
                    if ph == "E4":
                        pe.wait_ge(act_ok.sem, act_ok.at(ph, c))
                        if not (isinstance(c, int) and c == 0):
                            pe.wait_ge(seg_ok.sem, seg_ok.at(ph, c - 1))
                        nc.tensor.matmul(msg_ps[:], wm[:], act_in[:], start=True, stop=False)
                        nc.tensor.matmul(msg_ps[:], emb_sb[:], cnt[:], start=False, stop=True).then_inc(msg_done.sem, 1)
                        for k in range(ET):
                            b = 2 + k % 2
                            pe.wait_ge(seg_ok.sem, seg_ok.at(ph, c, k + 1))
                            if k >= 2:
                                pe.wait_ge(res_ok.sem, res_ok.at(ph, c, k - 1))
                            elif not (isinstance(c, int) and c == 0):
                                pe.wait_ge(res_ok.sem, res_ok.at(ph, c - 1, k + 3))
                            nc.tensor.matmul(bank[b][:, 0:3 * F], segT[s][:, k * P:(k + 1) * P], wih[:],
                                             start=True, stop=True).then_inc(out_done.sem, 1)
                        return
                    if ph == "E3":
                        pe.wait_ge(act_ok.sem, act_ok.at(ph, c))
                    else:
                        pe.wait_ge(seg_ok.sem, seg_ok.at(ph, c))
                    if not (isinstance(c, int) and c < 2):
                        pe.wait_ge(res_ok.sem, res_ok.at(ph, c - 2))
                    for k in range(ET):
                        last = nc.tensor.matmul(out_ps[s][:, k * F:(k + 1) * F], src[:, k * P:(k + 1) * P], EW[ph][:],
                                                start=True, stop=True)
                    last.then_inc(out_done.sem, 1)

                def body(c, half, s):
                    start = isinstance(c, int) and c == 0
                    pe.wait_ge(sel_ok.sem, sel_ok.at(ph, c))
                    if ph in ("E1", "E2"):
                        pe.wait_ge(msg_ok.sem, msg_ok.at(ph, c))
                    elif ph == "E4":
                        pe.wait_ge(scaled.sem, scaled.at(ph, c))
                        pe.wait_ge(onehot_ok.sem, onehot_ok.at(ph, c))
                        if not start:
                            pe.wait_ge(act_ok.sem, act_ok.at(ph, c - 1))
                    else:
                        pe.wait_ge(centred.sem, centred.at(ph, c))
                    if not (isinstance(c, int) and c < 2):
                        pe.wait_ge(seg_ok.sem, seg_ok.at(ph, c - 2))
                    if ph == "E4":
                        for k in range(ET):
                            nc.tensor.matmul(cnt_ps[0:NTYPES, k * P:(k + 1) * P], onehot[s][:, k, :], sel[s][:, k, :],
                                             start=True, stop=True)
                    for k in range(ET):
                        last = nc.tensor.matmul(seg_ps[s][:, k * P:(k + 1) * P], msg[s][:, k, :], sel[s][:, k, :],
                                                start=True, stop=True)
                    last.then_inc(seg_done.sem, 1)
                    weight(c, half, s)
                    if ph == "E0":
                        pe.wait_ge(oh_ok.sem, oh_ok.at(ph, c))
                        for k in range(ET):
                            last = nc.tensor.matmul(deg_ps[:, 0:NODE_TILES], oh_lo[:, k, :], oh_hi[:, k, :],
                                                    start=start and k == 0, stop=False, skip_group_check=True)
                        last.then_inc(deg_done.sem, 1)
                steps(pe, body)

            def dense(ph):
                def body(c, half, s):
                    start = isinstance(c, int) and c == 0
                    for g in range(2):
                        ks = range(4 * g, 4 * g + 4)
                        if ph == "A5":
                            pe.wait_ge(loaded.sems[s], loaded.at(ph, half, s))
                        else:
                            pe.wait_ge(z_ok.sem, z_ok.at(ph, c, 4 * g + 4))
                        if not start:
                            pe.wait_ge(zT_ok.sem, zT_ok.at(ph, c - 1, g + 1))
                        for k in ks:
                            src = xin[s] if ph == "A5" else z
                            last = nc.tensor.transpose(tp_ps[g][:, k % 4 * P:(k % 4 + 1) * P], src[:, k, :], ident[:])
                        last.then_inc(tp_done.sem, 1)
                    for g in range(2):
                        ks = range(4 * g, 4 * g + 4)
                        pe.wait_ge(zT_ok.sem, zT_ok.at(ph, c, g + 1))
                        if ph == "A8":
                            pe.wait_ge(agg_in.sems[s], agg_in.at(ph, half, s))
                            for k in ks:
                                b = bank[2 + k % 4]
                                if g == 1:
                                    pe.wait_ge(hn_ok.sem, hn_ok.at(ph, c, k - 3))
                                    pe.wait_ge(gate_ok.sem, gate_ok.at(ph, c, k - 3))
                                elif not start:
                                    pe.wait_ge(hn_ok.sem, hn_ok.at(ph, c - 1, k + 5))
                                    pe.wait_ge(gate_ok.sem, gate_ok.at(ph, c - 1, k + 5))
                                nc.tensor.matmul(b[:, 0:3 * F], zT[:, k * P:(k + 1) * P], whh[:], start=True, stop=False,
                                                 skip_group_check=True)
                                nc.tensor.matmul(b[:, 0:2 * F], ident[:], din3[s][:, k, 0:2 * F], start=False, stop=True,
                                                 skip_group_check=True).then_inc(y_done.sem, 1)
                            continue
                        pe.wait_ge(agg_ok.sem, agg_ok.at(ph, c, 4 * g + 4))
                        if not start:
                            if ph == "A1":
                                pe.wait_ge(y_ok.sem, y_ok.at(ph, c - 1, g + 1))
                            else:
                                pe.wait_ge(y_raw.sem, y_raw.at(ph, c - 1, 4 * g + 4))
                        for k in ks:
                            o = y_ps[g][:, k % 4 * F:(k % 4 + 1) * F]
                            nc.tensor.matmul(o, zT[:, k * P:(k + 1) * P], NW[ph][:], start=True, stop=False)
                            last = nc.tensor.matmul(o, ident[:], din[s][:, k, :], start=False, stop=True)
                        last.then_inc(y_done.sem, 1)
                    if ph in COEF_OF:
                        if ph == "A1":
                            pe.wait_ge(h_ok.sem, h_ok.at(ph, c))
                        else:
                            pe.wait_ge(y_ok.sem, y_ok.at(ph, c))
                        for k in range(NT):
                            r = hbuf if ph == "A1" else yout[s]
                            last = nc.tensor.matmul(gram_ps[:, 0:F + 1], r[:, k, 0:F], r[:, k, 0:F + 1],
                                                    start=start and k == 0, stop=False, skip_group_check=True)
                        last.then_inc(gram_done.sem, 1)
                steps(pe, body)

            for ph in PHASES:
                gate(pe, ph)
                if ph in EDGE:
                    edge(ph)
                elif ph in ("A1", "A3", "A5", "A8"):
                    dense(ph)
                if ph in COEF_OF:
                    pe.wait_ge(coef, 9 * COEF_OF[ph] + 9)
                    nc.tensor.matmul(bank[6][:, 0:F], ones[:], diag_a[:], start=True, stop=True)
                    nc.tensor.matmul(bank[6][:, F:2 * F], ones[:], diag_c[:], start=True, stop=True).then_inc(coef_rows, 1)

        @block.vector
        def _(dve):
            v = nc.vector
            v.memset(zeros[:], 0.0).then_inc(prep, 1)
            v.memset(zero_col[:], 0.0)
            v.memset(dst_row[:, 0:1], DST_NONE + 2.0)
            v.memset(eps_col[:], EPS)
            v.memset(hbuf[:, :, F:F + 1], 1.0).then_inc(prep, 1)
            n = [2]

            def done(ins):
                ins.then_inc(prep, 1)
                n[0] += 1
                dve.wait_ge(prep, n[0])

            dve.wait_ge(edges_in, 16 * E_DMAS)
            done(v.tensor_copy(dst_f[:], dst_i[:]))
            done(v.tensor_copy(nxt_f[:], nxt_i[:]))
            done(v.tensor_tensor(nxt_f[:], nxt_f[:], dst_f[:], eq))
            done(v.scalar_tensor_tensor(nxt_f[:], nxt_f[:], 100000.0, dst_f[:], mul, add))
            done(v.tensor_copy(scat[:], nxt_f[:]))
            done(v.tensor_scalar(nxt_i[:], dst_i[:], 7, None, ALU.logical_shift_right))
            done(v.tensor_copy(hi_f[:], nxt_i[:]))
            done(v.tensor_scalar(nxt_i[:], dst_i[:], 127, None, ALU.bitwise_and))
            done(v.tensor_copy(lo_f[:], nxt_i[:]))
            done(v.tensor_copy(typ_f[:], typ_i[:]))
            done(v.tensor_scalar(typ_f[:], typ_f[:], 0.0, float(NTYPES - 1), mx, ALU.min))
            for i in range(64):
                dve.wait_ge(row_in[i % 2], 16 * (i // 2 + 1))
                v.tensor_copy(dst_row[:, 1 + i * ROWC:1 + (i + 1) * ROWC], dst_row_i[:, i % 2, :]).then_inc(rowcast, 1)
            dve.wait_ge(rowcast, 64)
            dve.wait_ge(consts, 7)
            dve.wait_ge(weights_in, 16 * 14)
            done(v.tensor_tensor(emb_sb[:], emb_sb[:], bmsg_sb[:], add))
            done(v.tensor_copy(brow[:, 6 * F:7 * F], brow[:, 5 * F:6 * F]))
            done(v.memset(brow[:, 5 * F:6 * F], 0.0))
            done(v.tensor_tensor(brow[:, 0:3 * F], brow[:, 0:3 * F], brow[:, 3 * F:6 * F], add))
            v.tensor_copy(bgate[:], brow[:, None, 0:3 * F].to_broadcast([P, 4, 3 * F])).then_inc(bgate_ok, 1)
            dve.wait_ge(bgate_ok, 1)
            v.memset(brow[:, 5 * F:6 * F], 0.0).then_inc(bgate_ok, 1)
            dve.wait_ge(bgate_ok, 2)
            dve.sem_inc(ready, READY)

            def moments(ph, c, rows_of):
                for k in range(NT):
                    v.bn_stats(nst[:, k, :], rows_of(k)).then_inc(nstats.sem, 1)
                held(dve, nstats.sem, nstats.at(ph, c))
                if not (isinstance(c, int) and c == 0):
                    held(dve, kept.sem, kept.at(ph, c - 1))
                    held(dve, nstd_ok.sem, nstd_ok.at(ph, c - 1))
                for k in range(NT):
                    v.bn_aggr(nmv[:, k, :], nst[:, k, :]).then_inc(nmoments.sem, 1)
                held(dve, nstd_ok.sem, nstd_ok.at(ph, c))
                if ph == "A1" and not (isinstance(c, int) and c == 0):
                    held(dve, h_ok.sem, h_ok.at(ph, c - 1))
                v.reciprocal(nrs[:], nstd[:]).then_inc(nrs_ok.sem, 1)
                held(dve, nrs_ok.sem, nrs_ok.at(ph, c))
                v.tensor_copy(mean[:, bass.ds(c * NT, NT)], nmv[:, :, 0]).then_inc(kept.sem, 1)
                v.tensor_copy(rstd[:, bass.ds(c * NT, NT)], nrs[:]).then_inc(kept.sem, 1)

            def edge(ph):
                def body(c, half, s):
                    first = isinstance(c, int) and c < 2
                    start = isinstance(c, int) and c == 0
                    m = msg[s]
                    if not first:
                        held(dve, sel_ok.sem, sel_ok.at(ph, c - 2))
                    v.tensor_copy(ecol[s][:, 0, :], dst_f[:, bass.ds(c * ET, ET)]).then_inc(cols_ok.sem, 1)
                    v.tensor_copy(ecol[s][:, 1, :], (dinv_src if ph == "E2" else wgt)[:, bass.ds(c * ET, ET)])\
                        .then_inc(cols_ok.sem, 1)
                    v.tensor_copy(ecol[s][:, 2, :], typ_f[:, bass.ds(c * ET, ET)]).then_inc(cols_ok.sem, 1)
                    dve.wait_ge(gathered.sems[s], gathered.at(ph, half, s))
                    raw = msgw[s] if ph == "E1" else m
                    if ph in LN_EDGE:
                        for k in range(ET):
                            v.bn_stats(est[:, k, :], raw[:, k, 0:F]).then_inc(estats.sem, 1)
                        held(dve, estats.sem, estats.at(ph, c))
                        for k in range(ET):
                            v.bn_aggr(emv[:, k, :], est[:, k, :]).then_inc(emoments.sem, 1)
                        dve.wait_ge(emoments.sem, emoments.at(ph, c))
                        if ph == "E1" and not first:
                            dve.wait_ge(seg_done.sem, seg_done.at(ph, c - 2))
                        for k in range(ET):
                            v.tensor_scalar(m[:, k, :], raw[:, k, 0:F], emv[:, k, 0:1], 0.0, sub, mx)\
                                .then_inc(centred.sem, 1)
                        dve.wait_ge(estd_ok.sem, estd_ok.at(ph, c))
                        v.reciprocal(ers[:], estd[:]).then_inc(ers_ok.sem, 1)
                        dve.wait_ge(ers_ok.sem, ers_ok.at(ph, c))
                    held(dve, cols_ok.sem, cols_ok.at(ph, c))
                    if ph == "E0":
                        v.tensor_copy(eww[:], ers[:]).then_inc(eww_ok.sem, 1)
                    elif ph == "E1":
                        v.tensor_copy(eww[:], raw[:, :, F]).then_inc(eww_ok.sem, 1)
                        dve.wait_ge(eww_ok.sem, eww_ok.at(ph, c))
                        v.tensor_copy(dinv_src[:, bass.ds(c * ET, ET)], eww[:])
                    elif ph == "E2":
                        v.tensor_copy(eww[:], ecol[s][:, 1, :]).then_inc(eww_ok.sem, 1)
                    elif ph == "E3":
                        v.tensor_tensor(eww[:], ers[:], ecol[s][:, 1, :], mul).then_inc(eww_ok.sem, 1)
                    else:
                        v.memset(eww[:], 1.0).then_inc(eww_ok.sem, 1)
                    if ph == "E1":
                        dve.wait_ge(centred.sem, centred.at(ph, c))
                        for k in range(ET):
                            v.scalar_tensor_tensor(m[:, k, :], m[:, k, :], ers[:, k:k + 1], a_row[0][:], mul, mul)\
                                .then_inc(scaled.sem, 1)
                        dve.wait_ge(scaled.sem, scaled.at(ph, c))
                        v.tensor_tensor(m[:], m[:], c_row[0][:, None, :].to_broadcast([P, ET, F]), add)\
                            .then_inc(msg_ok.sem, 1)
                    elif ph == "E2":
                        v.tensor_tensor(m[:], m[:], a_row[1][:, None, :].to_broadcast([P, ET, F]), mul)\
                            .then_inc(scaled.sem, 1)
                        dve.wait_ge(scaled.sem, scaled.at(ph, c))
                        v.tensor_tensor(m[:], m[:], c_row[1][:, None, :].to_broadcast([P, ET, F]), add)\
                            .then_inc(msg_ok.sem, 1)
                    elif ph == "E4":
                        dve.wait_ge(centred.sem, centred.at(ph, c))
                        for k in range(ET):
                            v.tensor_scalar(m[:, k, :], m[:, k, :], ers[:, k:k + 1], None, mul).then_inc(scaled.sem, 1)
                        if not first:
                            dve.wait_ge(seg_done.sem, seg_done.at(ph, c - 2))
                        for k in range(ET):
                            v.tensor_scalar(onehot[s][:, k, :], iota_lo[:, 0:NTYPES], ecol[s][:, 2, k:k + 1], None, eq)\
                                .then_inc(onehot_ok.sem, 1)
                    dve.wait_ge(eww_ok.sem, eww_ok.at(ph, c))
                    if not first:
                        held(dve, seg_done.sem, seg_done.at(ph, c - 2))
                    for k in range(ET):
                        v.tensor_scalar(sel[s][:, k, :], dst_row[:, bass.ds(c * (ET * P) + (k * P + 1), P)],
                                        ecol[s][:, 0, k:k + 1], eww[:, k:k + 1], eq, mul).then_inc(sel_ok.sem, 1)
                    if ph == "E0":
                        if not start:
                            held(dve, deg_done.sem, deg_done.at(ph, c - 1))
                        v.tensor_copy(ecol[s][:, 3, :], hi_f[:, bass.ds(c * ET, ET)]).then_inc(prep, 1)
                        held(dve, prep, n[0] + 2 * c + 1)
                        for k in range(ET):
                            v.tensor_scalar(oh_hi[:, k, :], iota_hi[:], ecol[s][:, 3, k:k + 1], None, eq)\
                                .then_inc(oh_ok.sem, 1)
                        held(dve, oh_ok.sem, oh_ok.at(ph, c, ET))
                        v.tensor_copy(ecol[s][:, 3, :], lo_f[:, bass.ds(c * ET, ET)]).then_inc(prep, 1)
                        held(dve, prep, n[0] + 2 * c + 2)
                        for k in range(ET):
                            v.tensor_scalar(oh_lo[:, k, :], iota_lo[:], ecol[s][:, 3, k:k + 1], None, eq)\
                                .then_inc(oh_ok.sem, 1)
                    if ph == "E4":
                        dve.wait_ge(msg_done.sem, msg_done.at(ph, c))
                        ps = msg_ps
                    else:
                        dve.wait_ge(seg_done.sem, seg_done.at(ph, c))
                        ps = seg_ps[s]
                    if not first:
                        held(dve, out_done.sem, out_done.at(ph, c - 2))
                    for k in range(ET):
                        if k > 0:
                            carry = segT[s][:, k * P - 1:k * P]
                            held(dve, seg_ok.sem, seg_ok.at(ph, c, k))
                        elif start:
                            carry = zero_col[:]
                        else:
                            carry = segT[1 - s][:, ET * P - 1:ET * P]
                            held(dve, seg_ok.sem, seg_ok.at(ph, c - 1))
                        v.tensor_scalar(cmask[:], dst_row[:, bass.ds(c * (ET * P) + (k * P + 1), P)], dst_last(s, c, k),
                                        carry, eq, mul).then_inc(mask_ok.sem, 1)
                        dve.wait_ge(mask_ok.sem, mask_ok.at(ph, c, k + 1))
                        v.tensor_tensor(segT[s][:, k * P:(k + 1) * P], ps[:, k * P:(k + 1) * P], cmask[:], add)\
                            .then_inc(seg_ok.sem, 1)
                    if ph == "E4":
                        if not first:
                            held(dve, scattered.sems[s], scattered.at(ph, half - 1, s))
                        for k in range(ET):
                            dve.wait_ge(out_done.sem, out_done.at(ph, c, k + 1))
                            v.tensor_tensor(res3[s][:, k, :], bank[2 + k % 2][:, 0:3 * F], bgate[:, 0, :], add)\
                                .then_inc(res_ok.sem, 1)
                    if ph == "E0":
                        dve.wait_ge(loaded.sems[s], loaded.at(ph, half, s))
                        moments(ph, c, lambda k: xin[s][:, k, :])

                last_f = lastcol

                def dst_last(s, c, k):
                    return last_f[s][:, k:k + 1]

                def with_last(c, half, s):
                    if not (isinstance(c, int) and c < 2):
                        held(dve, mask_ok.sem, mask_ok.at(ph, c - 2))
                    v.tensor_copy(last_f[s][:],
                                  dst_row[:, bass.ds(c * (ET * P), ET * P)].rearrange("p (k q) -> p k q", q=P)[:, :, 0])\
                        .then_inc(last_ok.sem, 1)
                    held(dve, last_ok.sem, last_ok.at(ph, c))
                    body(c, half, s)
                steps(dve, with_last)

            def dense(ph):
                scale_of = {"A1": rdeg, "A3": sqd, "A5": sqd}.get(ph, rdeg)

                def body(c, half, s):
                    first = isinstance(c, int) and c < 2
                    start = isinstance(c, int) and c == 0
                    if not first:
                        held(dve, y_ok.sem, y_ok.at(ph, c - 1))
                    for i, a in enumerate((mean, rstd, scale_of, dinv if ph == "A1" else dinv2)):
                        v.tensor_copy(ncol[s][:, i, :], a[:, bass.ds(c * NT, NT)]).then_inc(ncols_ok.sem, 1)
                    held(dve, ncols_ok.sem, ncols_ok.at(ph, c))
                    X, Dn, Y = xin[s], din[s], yout[s]
                    dve.wait_ge(loaded.sems[s], loaded.at(ph, half, s))
                    if ph in ("A1", "A3", "A6", "A8"):
                        if not start:
                            if ph in ("A1", "A3"):
                                held(dve, tp_done.sem, tp_done.at(ph, c - 1))
                            elif ph == "A8":
                                held(dve, hmn_ok.sem, hmn_ok.at(ph, c - 1))
                                held(dve, tp_done.sem, tp_done.at(ph, c - 1))
                        for k in range(NT):
                            v.tensor_scalar(z[:, k, :], X[:, k, :], ncol[s][:, 0, k:k + 1], ncol[s][:, 1, k:k + 1],
                                            sub, mul).then_inc(z_ok.sem, 1)
                    if ph != "A8":
                        dve.wait_ge(agg_in.sems[s], agg_in.at(ph, half, s))
                    if ph in ("A1", "A3", "A5"):
                        for k in range(NT):
                            v.tensor_scalar(Dn[:, k, :], Dn[:, k, :], ncol[s][:, 2, k:k + 1], None, mul)\
                                .then_inc(agg_ok.sem, 1)
                    if not first:
                        held(dve, stored.sems[s], stored.at(ph, half - 1, s))
                        if ph in ("A3", "A5"):
                            held(dve, gram_done.sem, gram_done.at(ph, c - 2))
                    if ph == "A1":
                        v.tensor_copy(Y[:, :, F:W1C], ncol[s][:, 3, :, None].to_broadcast([P, NT, 4]))
                        for g in range(2):
                            ks = slice(4 * g, 4 * g + 4)
                            dve.wait_ge(y_done.sem, y_done.at(ph, c, g + 1))
                            v.scalar_tensor_tensor(Y[:, ks, 0:F], y_ps[g][:].rearrange("p (k f) -> p k f", f=F), 0.0,
                                                   X[:, ks, :], mx, add).then_inc(y_ok.sem, 1)
                    if ph == "A3":
                        for g in range(2):
                            cols = slice(g * 4 * F, (g + 1) * 4 * F)
                            dve.wait_ge(zT_raw.sem, zT_raw.at(ph, c, g + 1))
                            v.tensor_scalar(zT[:, cols], zT[:, cols], a_col[0][:], c_col[0][:], mul, add)\
                                .then_inc(zT_ok.sem, 1)
                    if ph in ("A3", "A5"):
                        for k in range(NT):
                            dve.wait_ge(y_done.sem, y_done.at(ph, c, k // 4 + 1))
                            v.scalar_tensor_tensor(Y[:, k, 0:F], y_ps[k // 4][:, k % 4 * F:(k % 4 + 1) * F],
                                                   ncol[s][:, 3, k:k + 1], row[:, 0 if ph == "A3" else 1, :],
                                                   mul, add).then_inc(y_raw.sem, 1)
                        dve.wait_ge(y_raw.sem, y_raw.at(ph, c))
                        if isinstance(c, int) and c == STEPS - 1:
                            v.tensor_scalar(Y[:, 0:NT - 2, 0:F], Y[:, 0:NT - 2, 0:F], 0.0, None, mx)
                            v.tensor_scalar(Y[:, NT - 2, 0:F], Y[:, NT - 2, 0:F], 0.0, valid[:], mx, mul)
                            v.memset(Y[:, NT - 1, 0:F], 0.0).then_inc(y_ok.sem, 1)
                        else:
                            v.tensor_scalar(Y[:, :, 0:F], Y[:, :, 0:F], 0.0, None, mx).then_inc(y_ok.sem, 1)
                    if ph == "A6":
                        dve.wait_ge(z_ok.sem, z_ok.at(ph, c))
                        for g in range(2):
                            ks = slice(4 * g, 4 * g + 4)
                            v.scalar_tensor_tensor(z[:, ks, :], z[:, ks, :], 0.0,
                                                   a_row[0][:, None, :].to_broadcast([P, 4, F]), mx, mul)\
                                .then_inc(y_raw.sem, 1)
                        dve.wait_ge(y_raw.sem, y_raw.at(ph, c, 2))
                        v.tensor_tensor(z[:], z[:], X[:], add).then_inc(y_raw.sem, 1)
                        dve.wait_ge(y_raw.sem, y_raw.at(ph, c, 3))
                        v.tensor_tensor(z[:], z[:], c_row[2][:, None, :].to_broadcast([P, NT, F]), add)\
                            .then_inc(y_raw.sem, 1)
                        dve.wait_ge(y_raw.sem, y_raw.at(ph, c, 4))
                        dve.wait_ge(agg_ok.sem, agg_ok.at(ph, c))
                        v.tensor_tensor(Y[:, :, 0:F], z[:], Dn[:], add).then_inc(y_ok.sem, 1)
                    if ph == "A7":
                        v.tensor_tensor(Dn[:], Dn[:], row[:, 2:3, :].to_broadcast([P, NT, F]), add).then_inc(agg_ok.sem, 1)
                        dve.wait_ge(gelu_ok.sem, gelu_ok.at(ph, c))
                        v.tensor_tensor(Y[:, :, 0:F], z[:], X[:], add).then_inc(y_ok.sem, 1)
                    if ph == "A8":
                        G3 = din3[s]
                        dve.wait_ge(agg_in.sems[s], agg_in.at(ph, half, s))
                        for g in range(2):
                            ks = slice(4 * g, 4 * g + 4)
                            hb = hbuf[:, ks, 0:F]
                            for k in range(4 * g, 4 * g + 4):
                                dve.wait_ge(gate_ok.sem, gate_ok.at(ph, c, k + 1))
                                v.tensor_tensor(hbuf[:, k, 0:F], bank[2 + k % 4][:, 2 * F:3 * F],
                                                brow[:, 6 * F:7 * F], add).then_inc(hn_ok.sem, 1)
                            dve.wait_ge(hn_ok.sem, hn_ok.at(ph, c, 4 * g + 4))
                            v.tensor_tensor(hb, hb, rz[:, :, 0:F], mul).then_inc(rhn_ok.sem, 1)
                            dve.wait_ge(rhn_ok.sem, rhn_ok.at(ph, c, g + 1))
                            v.tensor_tensor(hb, hb, G3[:, ks, 2 * F:3 * F], add).then_inc(nin_ok.sem, 1)
                            dve.wait_ge(tanh_ok.sem, tanh_ok.at(ph, c, g + 1))
                            v.scalar_tensor_tensor(z[:, ks, :], z[:, ks, :], 0.0, hb, mx, sub).then_inc(hmn_ok.sem, 1)
                            dve.wait_ge(hmn_ok.sem, hmn_ok.at(ph, c, g + 1))
                            v.tensor_tensor(z[:, ks, :], z[:, ks, :], rz[:, :, F:2 * F], mul).then_inc(zhn_ok.sem, 1)
                            dve.wait_ge(zhn_ok.sem, zhn_ok.at(ph, c, g + 1))
                            v.tensor_tensor(z[:, ks, :], z[:, ks, :], hb, add).then_inc(nzh_ok.sem, 1)
                            dve.wait_ge(nzh_ok.sem, nzh_ok.at(ph, c, g + 1))
                            v.tensor_tensor(Y[:, ks, 0:F], z[:, ks, :], X[:, ks, :], add).then_inc(y_ok.sem, 1)
                    if ph in ST:
                        held(dve, y_ok.sem, y_ok.at(ph, c))
                        moments(ph, c, lambda k: Y[:, k, 0:F])
                    if ph == "A1":
                        v.scalar_tensor_tensor(nbias[:], nmv[:, :, 0], -1.0, nrs[:], mul, mul).then_inc(nbias_ok.sem, 1)
                steps(dve, body)

            def coefficients(ph):
                i = COEF_OF[ph]
                k = [9 * i]

                def one(ins):
                    ins.then_inc(coef, 1)
                    k[0] += 1
                    dve.wait_ge(coef, k[0])

                dve.wait_ge(gram_done.sem, gram_done.end(ph))
                one(v.tensor_tensor(bn_tmp[:], gram_ps[:, 0:F], ident[:], mul))
                one(v.reduce_sum(bn_col[:, 1:2], bn_tmp[:], AX.X))
                one(v.tensor_scalar(bn_col[:, 0:1], gram_ps[:, F:F + 1], 1.0 / N_NODES, None, mul))
                one(v.tensor_tensor(bn_col[:, 2:3], bn_col[:, 0:1], bn_col[:, 0:1], mul))
                one(v.scalar_tensor_tensor(bn_col[:, 3:4], bn_col[:, 1:2], 1.0 / N_NODES, bn_col[:, 2:3], mul, sub))
                dve.wait_ge(coef_std, i + 1)
                one(v.reciprocal(bn_col[:, 5:6], bn_col[:, 4:5]))
                one(v.tensor_tensor(a_col[i][:], bn_col[:, 5:6], vec[:, 2 * i:2 * i + 1], mul))
                one(v.scalar_tensor_tensor(c_col[i][:], a_col[i][:], bn_col[:, 0:1], vec[:, 2 * i + 1:2 * i + 2], mul, sub))
                v.tensor_scalar(diag_a[:], ident[:], a_col[i][:], None, mul)
                v.tensor_scalar(diag_c[:], ident[:], c_col[i][:], -1.0, mul, mul).then_inc(coef, 1)
                k[0] += 1
                dve.wait_ge(coef, k[0])
                v.tensor_scalar(c_col[i][:], c_col[i][:], -1.0, None, mul)
                dve.wait_ge(coef_rows, i + 1)
                v.tensor_copy(a_row[i][:], bank[6][:, 0:F]).then_inc(coef_end, 1)
                v.tensor_copy(c_row[i][:], bank[6][:, F:2 * F]).then_inc(coef_end, 1)
                dve.wait_ge(coef_end, 3 * i + 2)
                if i == 2:
                    v.tensor_tensor(c_row[2][:], c_row[2][:], c_row[0][:], add).then_inc(coef_end, 1)
                else:
                    v.memset(hbuf[:, :, F:F + 1], 1.0).then_inc(coef_end, 1)
                dve.wait_ge(coef_end, 3 * i + 3)
                if i == 0:
                    for b in yout:
                        v.memset(b[:, :, F:F + 1], 1.0).then_inc(ones_ok, 1)
                    dve.wait_ge(ones_ok, 2)
                dve.sem_inc(coef_ready, 1)

            for ph in PHASES:
                if ph in EDGE:
                    gate(dve, ph)
                    edge(ph)
                    if ph == "E0":
                        dve.wait_ge(deg_done.sem, deg_done.end("E0"))
                        v.tensor_copy(deg[:], deg_ps[:, 0:NODE_TILES]).then_inc(degs, 1)
                        dve.wait_ge(degs, 1)
                        v.tensor_scalar(sqd[:], deg[:], 1.0, None, add).then_inc(degs, 1)
                        dve.wait_ge(degs, 3)
                        v.tensor_scalar(rdeg[:], deg[:], 1.0, None, mx).then_inc(degs, 1)
                        dve.wait_ge(degs, 4)
                        v.reciprocal(rdeg[:], rdeg[:]).then_inc(degs, 1)
                        v.reciprocal(dinv[:], sqd[:]).then_inc(degs, 1)
                        v.tensor_scalar(dinv2[:], deg[:], 1.0, None, add).then_inc(degs, 1)
                        dve.wait_ge(degs, 7)
                        v.reciprocal(dinv2[:], dinv2[:]).then_inc(degs, 1)
                        dve.wait_ge(degs, 8)
                else:
                    gate(dve, ph)
                    dense(ph)
                    if ph in COEF_OF:
                        if ph == "A1":
                            for s in range(2):
                                held(dve, stored.sems[s], stored.end("A1", s))
                        coefficients(ph)


_OUT = "out_dram"


def kernel(**inputs):
    import concourse.bacc as bacc
    from concourse.bass_utils import run_bass_kernel_spmd

    def edge_columns(a, fill):
        p = np.full((EPAD,), fill, a.dtype)
        p[:N_EDGES] = a
        return np.ascontiguousarray(p.reshape(EDGE_TILES, P).T)

    i = {k: np.asarray(v) for k, v in inputs.items()}
    xp = np.zeros((NPAD, F), i["x"].dtype)
    xp[:N_NODES] = i["x"]
    dst = i["dst"]
    nxt = np.concatenate([dst[1:], np.full((1,), DST_NONE, dst.dtype)])
    drow = np.full((1, EPAD), DST_NONE, dst.dtype)
    drow[0, :N_EDGES] = dst
    W0 = i["L0_gnn_W"]
    t = lambda a: np.ascontiguousarray(a.T)
    arrays = {
        "x": xp,
        "gidx": edge_columns(i["src"], 0).view(np.uint32),
        "dst": edge_columns(dst, DST_NONE),
        "nxt": edge_columns(nxt, DST_NONE),
        "typ": edge_columns(i["edge_type_9"], 0),
        "wgt": edge_columns(i["edge_weight1"][:, 0], 0),
        "dstrow": drow,
        "WaT": t(W0[:, :F]), "WbT": t(W0[:, F:]),
        "W1": i["L1_gnn_W1"], "W2": i["L1_gnn_W2"], "WL2T": t(i["L2_gnn_W"]),
        "WmT": i["L3_gnn_W_msg"].T.copy(), "WihT": t(i["L3_gnn_W_ih"]), "WhhT": t(i["L3_gnn_W_hh"]),
        "emb": i["L3_gnn_edge_embed"],
        "vecs": np.ascontiguousarray(np.stack([i[f"L1_gnn_bn{k}_{n}"] for k in range(3) for n in ("gamma", "beta")], 1)),
        "rows": np.stack([i["L1_gnn_b1"], i["L1_gnn_b2"], i["L2_gnn_b"], i["L3_gnn_b_msg"]]),
        "b3": np.concatenate([i["L3_gnn_b_ih"], i["L3_gnn_b_hh"]])[None, :],
    }
    nc = bacc.Bacc("TRN2", target_bir_lowering=False, num_devices=1)
    args = [nc.dram_tensor(f"in_{n}", a.shape, mybir.dt.from_np(a.dtype), kind="ExternalInput").ap()
            for n, a in arrays.items()]
    args.append(nc.dram_tensor(_OUT, (NPAD, F), mybir.dt.float32, kind="ExternalOutput").ap())
    build(nc, *args)
    r = run_bass_kernel_spmd(nc, [{f"in_{n}": np.ascontiguousarray(a) for n, a in arrays.items()}], core_ids=[0])
    return np.asarray(r.results[0][_OUT])[:N_NODES]
```

```python
import numpy as np
import concourse.bass as bass
from concourse import mybir

N_NODES, N_EDGES, F = 50000, 25000, 128
P = 128
STEPS = 49
NT = 8
ET = 4
NODE_TILES, EDGE_TILES = STEPS * NT, STEPS * ET
NPAD, EPAD = NODE_TILES * P, EDGE_TILES * P
W1C = F + 4
NTYPES = 9
EPS = 1e-5
DST_NONE = 60000
LAST_ROWS = N_NODES - (NODE_TILES - 2) * P

PHASES = ["E0", "A1", "E1", "A3", "E2", "A5", "A6", "E3", "A7", "E4", "A8"]
EDGE = ["E0", "E1", "E2", "E3", "E4"]
LN_EDGE = ["E0", "E1", "E3", "E4"]
DENSE = ["A1", "A3", "A5", "A6", "A7", "A8"]


class Stage:

    def __init__(self, nc, name, per):
        self.sem = nc.alloc_semaphore(name)
        self.per = per

    def before(self, phase):
        return sum(STEPS * self.per.get(p, 0) for p in PHASES[:PHASES.index(phase)])

    def at(self, phase, step, k=None):
        per = self.per[phase]
        return step * per + (self.before(phase) + (per if k is None else k))

    def end(self, phase):
        return self.before(phase) + STEPS * self.per.get(phase, 0)


class Slots:

    def __init__(self, nc, name, per, n):
        own = [nc.alloc_semaphore(f"{name}{s}") for s in range(n)]
        self.sems = own * (4 // n)
        self.n, self.per = n, per

    def before(self, phase, s):
        return 16 * sum(self.per.get(p, 0) * len(range(s % self.n, STEPS, self.n)) for p in PHASES[:PHASES.index(phase)])

    def at(self, phase, q, s, back=0):
        q, s = q + (s - back) // 4 if (s - back) // 4 else q, (s - back) % 4
        per = 16 * self.per[phase]
        return q * (per * (4 // self.n)) + (self.before(phase, s) + per * (s // self.n + 1))

    def end(self, phase, s):
        return self.before(phase, s) + 16 * self.per.get(phase, 0) * len(range(s % self.n, STEPS, self.n))


def steps(eng, *stages):
    longest = max(lag for lag, _ in stages)
    first = (4 + longest + 3) // 4

    def turn(t):
        for lag, body in stages:
            if 0 <= t - lag < STEPS:
                body(t - lag, (t - lag) // 4, (t - lag) % 4)

    for t in range(4 * first):
        turn(t)
    with eng.Fori(first, STEPS // 4) as group:
        for i in range(4):
            for lag, body in stages:
                back = (i - lag) // 4
                body(group * 4 + (i - lag), group + back if back else group, (i - lag) % 4)
    for t in range(STEPS - 1, STEPS + longest):
        turn(t)


def early(step, n):
    return isinstance(step, int) and step < n


def build(nc, x, gidx_d, dst_d, nxt_d, typ_d, wgt_d, dstrow_d, WaT, WbT, W1, W2, WL2T, WmT, WihT, WhhT,
          emb, vecs, rows, b3, out):
    f32, u32, i32 = mybir.dt.float32, mybir.dt.uint32, mybir.dt.int32
    bf16, u16 = mybir.dt.bfloat16, mybir.dt.uint16
    ALU, ACT, AX = mybir.AluOpType, mybir.ActivationFunctionType, mybir.AxisListType
    add, sub, mul, mx, eq = ALU.add, ALU.subtract, ALU.mult, ALU.max, ALU.is_equal

    def sb(name, shape, dt=f32):
        return nc.alloc_sbuf_tensor(name, shape, dt)

    def sem(name):
        return nc.alloc_semaphore(name)

    x1_d = nc.dram_tensor("x1_rows", [NPAD, W1C], f32).ap()
    t1_d = nc.dram_tensor("t1_rows", [NPAD, F], f32).ap()
    t2_d = nc.dram_tensor("t2_rows", [NPAD, F], f32).ap()
    x2_d = nc.dram_tensor("x2_rows", [NPAD, F], f32).ap()
    x3_d = nc.dram_tensor("x3_rows", [NPAD, F], f32).ap()
    agg_d = nc.dram_tensor("agg_rows", [NPAD, F], f32).ap()
    gates_d = nc.dram_tensor("gate_rows", [NPAD, 3 * F], f32).ap()

    def node_view(ap):
        return ap.rearrange("(c k p) f -> c p k f", k=NT, p=P)

    ident, ones = sb("ident", [P, P]), sb("ones", [P, P])
    iota_lo, iota_hi = sb("iota_lo", [P, P]), sb("iota_hi", [P, NODE_TILES])
    wa, wb = sb("wa", [P, F]), sb("wb", [P, F])
    w1, w2, wl2, wm = sb("w1", [P, F]), sb("w2", [P, F]), sb("wl2", [P, F]), sb("wm", [P, F])
    wih, whh = sb("wih", [P, 3 * F]), sb("whh", [P, 3 * F])
    emb_sb, bmsg_sb = sb("emb_sb", [NTYPES, F]), sb("bmsg_sb", [NTYPES, F])
    vec = sb("vec", [P, 6])
    row = sb("row", [P, 3, F])
    brow = sb("brow", [P, 7 * F])
    bgate = sb("bgate", [P, 4, 3 * F])
    zeros = sb("zeros", [P, NT * F])
    zero_col, eps_col = sb("zero_col", [P, 1]), sb("eps_col", [P, 1])
    gidx, scat = sb("gidx", [P, EDGE_TILES], u32), sb("scat", [P, EDGE_TILES], u32)
    dst_i, nxt_i = sb("dst_i", [P, EDGE_TILES], i32), sb("nxt_i", [P, EDGE_TILES], i32)
    dst_f, nxt_f = sb("dst_f", [P, EDGE_TILES]), sb("nxt_f", [P, EDGE_TILES])
    hi_f, lo_f = sb("hi_f", [P, EDGE_TILES]), sb("lo_f", [P, EDGE_TILES])
    typ_i, typ_f = sb("typ_i", [P, EDGE_TILES], i32), sb("typ_f", [P, EDGE_TILES])
    wgt = sb("wgt", [P, EDGE_TILES])
    dinv_src = sb("dinv_src", [P, EDGE_TILES])
    drow = [sb(f"drow{s}", [P, 1 + ET * P], i32) for s in range(4)]
    deg, rdeg = sb("deg", [P, NODE_TILES]), sb("rdeg", [P, NODE_TILES])
    sqd, dinv, dinv2 = sb("sqd", [P, NODE_TILES]), sb("dinv", [P, NODE_TILES]), sb("dinv2", [P, NODE_TILES])
    mean, rstd = sb("mean", [P, NODE_TILES]), sb("rstd", [P, NODE_TILES])
    mbias = sb("mbias", [P, NODE_TILES])
    valid = sb("valid", [P, 1])
    bn_col = sb("bn_col", [P, 8])
    bn_tmp = sb("bn_tmp", [P, P])
    diag_a, diag_c = sb("diag_a", [P, P]), sb("diag_c", [P, P])
    a_col, c_col = [sb(f"a_col{i}", [P, 1]) for i in range(3)], [sb(f"c_col{i}", [P, 1]) for i in range(3)]
    a_row, c_row = [sb(f"a_row{i}", [P, F]) for i in range(3)], [sb(f"c_row{i}", [P, F]) for i in range(3)]

    def four(name, shape, n, dt=f32):
        return [sb(f"{name}{s}", shape, dt) for s in range(n)] * (4 // n)

    xin = four("xin", [P, NT, F], 4)
    din = four("din", [P, NT, F], 4)
    din3 = four("din3", [P, NT, 3 * F], 2)
    ncol = four("ncol", [P, 5, NT], 4)
    nst, nmv = sb("nst", [P, NT, 6]), sb("nmv", [P, NT, 2])
    nstd, nrs, nbias = sb("nstd", [P, NT]), four("nrs", [P, NT], 2), four("nbias", [P, NT], 2)
    zb = four("z", [P, NT, F], 4)
    zT = four("zT", [P, NT * F], 2)
    yout = four("yout", [P, NT, W1C], 4)
    hbuf = four("hbuf", [P, NT, F + 1], 2)
    rz = [[din[2 * i + g][:].rearrange("p (k a) f -> p k (a f)", a=2) for g in range(2)] for i in range(2)] * 2

    grow, srow = four("grow", [P, ET], 4, u32), four("srow", [P, ET], 2, u32)
    msg = [b[:, 0:ET, :] for b in zb]
    sel = [b[:, ET:2 * ET, :] for b in zb]
    msgw = [b[:, 0:ET, :] for b in yout]
    segT = [b[:, 0:ET * P] for b in zT]
    act_in = [b[:, ET * P:2 * ET * P] for b in zT]
    res3 = [b[:, 0:ET, :] for b in din3]
    ecol = four("ecol", [P, 3, ET], 4)
    lastcol = four("lastcol", [P, ET], 4)
    est, emv = sb("est", [P, ET, 6]), sb("emv", [P, ET, 2])
    estd, ers, eww = sb("estd", [P, ET]), sb("ers", [P, ET]), sb("eww", [P, ET])
    onehot = four("onehot", [P, ET, NTYPES], 2)
    cmask = sb("cmask", [P, P])
    cnt = sb("cnt", [NTYPES, ET * P])
    res = four("res", [P, ET, F], 2)
    oh_lo, oh_hi = sb("oh_lo", [P, ET, P], bf16), sb("oh_hi", [P, ET, NODE_TILES], bf16)
    digit = sb("digit", [P, 2, ET])

    bank = [nc.alloc_psum_tensor(f"bank{i}", [P, 512], f32) for i in range(8)]
    seg_ps, out_ps = bank[0:2] * 2, bank[2:4] * 2
    cnt_ps, msg_ps = bank[4], bank[5]
    tp_ps, y_ps, gram_ps = bank[0:2], bank[2:4], bank[7]
    deg_ps = bank[6]
    gate_ps = [bank[2], bank[3], bank[6], bank[7]]

    D = DENSE
    loaded = Slots(nc, "loaded", {p: 1 for p in ["E0"] + D}, 4)
    agg_in = Slots(nc, "agg_in", {p: 1 for p in D}, 4)
    stored = Slots(nc, "stored", {p: 1 for p in D}, 4)
    gathered = Slots(nc, "gathered", {p: ET for p in EDGE}, 4)
    scattered = Slots(nc, "scattered", {p: ET for p in EDGE}, 2)
    drow_in = Slots(nc, "drow_in", {p: 1 for p in EDGE}, 4)
    idx_ok, srow_ok = (Stage(nc, n, {p: 1 for p in EDGE}) for n in ("idx_ok", "srow_ok"))
    cols_ok = Stage(nc, "cols_ok", {p: 3 for p in EDGE})
    estats = Stage(nc, "estats", {p: ET for p in LN_EDGE})
    emoments = Stage(nc, "emoments", {p: ET for p in LN_EDGE})
    ers_ok = Stage(nc, "ers_ok", {p: 1 for p in LN_EDGE})
    eww_ok = Stage(nc, "eww_ok", {p: 1 for p in EDGE})
    centred = Stage(nc, "centred", {p: ET for p in LN_EDGE})
    scaled = Stage(nc, "scaled", {"E1": ET, "E2": 1, "E4": ET})
    msg_ok = Stage(nc, "msg_ok", {"E1": 1, "E2": 1})
    sel_ok = Stage(nc, "sel_ok", {p: ET for p in EDGE})
    onehot_ok = Stage(nc, "onehot_ok", {"E4": ET})
    mask_ok = Stage(nc, "mask_ok", {p: ET for p in EDGE})
    seg_ok = Stage(nc, "seg_ok", {p: ET for p in EDGE})
    res_ok = Stage(nc, "res_ok", {p: ET if p == "E4" else 1 for p in EDGE})
    oh_ok = Stage(nc, "oh_ok", {"E0": 2 * ET})
    estd_ok = Stage(nc, "estd_ok", {p: 1 for p in LN_EDGE})
    act_ok = Stage(nc, "act_ok", {"E3": 1, "E4": 2})
    seg_done = Stage(nc, "seg_done", {p: 1 for p in EDGE})
    msg_done = Stage(nc, "msg_done", {"E4": 1})
    out_done = Stage(nc, "out_done", {p: ET if p == "E4" else 1 for p in EDGE})
    deg_done = Stage(nc, "deg_done", {"E0": 1})
    ST = ["E0", "A1", "A6", "A7"]
    ncols_ok = Stage(nc, "ncols_ok", {p: 5 for p in D})
    z_ok = Stage(nc, "z_ok", {p: NT for p in ("A1", "A3", "A6", "A8")})
    agg_ok = Stage(nc, "agg_ok", {"A1": NT, "A3": NT, "A5": NT, "A6": 2, "A7": 1})
    tp_done = Stage(nc, "tp_done", {"A1": 2, "A3": 2, "A5": 2, "A8": 2})
    zT_raw = Stage(nc, "zT_raw", {"A3": 2})
    zT_ok = Stage(nc, "zT_ok", {"A1": 2, "A3": 2, "A5": 2, "A8": 2})
    y_done = Stage(nc, "y_done", {"A1": 2, "A3": 2, "A5": 2, "A8": NT})
    y_raw = Stage(nc, "y_raw", {"A3": NT, "A5": NT, "A6": 2})
    y_ok = Stage(nc, "y_ok", {"A1": 2, "A3": 1, "A5": 1, "A6": 1, "A7": 1, "A8": 2})
    gelu_ok = Stage(nc, "gelu_ok", {"A7": 1})
    nstats = Stage(nc, "nstats", {p: NT for p in ST})
    nmoments = Stage(nc, "nmoments", {p: NT for p in ST})
    kept = Stage(nc, "kept", {p: 2 for p in ST})
    nstd_ok = Stage(nc, "nstd_ok", {"A1": 1})
    nrs_ok = Stage(nc, "nrs_ok", {"A1": 1})
    nbias_ok = Stage(nc, "nbias_ok", {"A1": 1})
    h_ok = Stage(nc, "h_ok", {"A1": NT})
    gram_done = Stage(nc, "gram_done", {"A1": 1, "A3": 1, "A5": 1})
    gate_ok = Stage(nc, "gate_ok", {"A8": NT})
    hn_ok = Stage(nc, "hn_ok", {"A8": NT})
    rhn_ok = Stage(nc, "rhn_ok", {"A8": 2})
    nin_ok = Stage(nc, "nin_ok", {"A8": 2})
    tanh_ok = Stage(nc, "tanh_ok", {"A8": 2})
    hmn_ok = Stage(nc, "hmn_ok", {"A8": 2})
    zhn_ok = Stage(nc, "zhn_ok", {"A8": 2})
    nzh_ok = Stage(nc, "nzh_ok", {"A8": 2})
    mom, mom_std = sem("mom"), sem("mom_std")
    consts, weights_in, edges_in = sem("consts"), sem("weights_in"), sem("edges_in")
    filled, gates_filled, prep = sem("filled"), sem("gates_filled"), sem("prep")
    bgate_ok, ready, degs = sem("bgate_ok"), sem("ready"), sem("degs")
    digits_ok = Stage(nc, "digits_ok", {"E0": 2})
    last_ok = Stage(nc, "last_ok", {p: 1 for p in EDGE})
    coef_end, ones_ok = sem("coef_end"), sem("ones_ok")
    coef, coef_std, coef_rows, coef_ready, passed = (sem("coef"), sem("coef_std"), sem("coef_rows"),
                                                     sem("coef_ready"), sem("passed"))
    READY = 1
    W_DMAS, E_DMAS = 8 + 2 + 1 + 3 + 2, 6
    MOM_OF = {"E0": 0, "A6": 1, "A7": 2}
    WEIGHT_LAG = {"E0": 3, "E1": 3, "E2": 3, "E3": 4, "E4": 4}
    COEF_OF = {"A1": 0, "A3": 1, "A5": 2}
    SRC = {"E0": x, "E1": x1_d, "E2": t1_d, "E3": x2_d, "E4": x3_d}
    XIN = {"A1": x, "A3": x1_d, "A5": t1_d, "A6": x1_d, "A7": x2_d, "A8": x3_d}
    DIN = {"A1": agg_d, "A3": agg_d, "A5": agg_d, "A6": t2_d, "A7": agg_d, "A8": gates_d}
    OUT = {"A1": x1_d, "A3": t1_d, "A5": t2_d, "A6": x2_d, "A7": x3_d, "A8": out}
    EW = {"E0": wb, "E1": w1, "E2": w2, "E3": wl2}
    NW = {"A1": wa, "A3": w1, "A5": w2}

    def held(eng, semaphore, value):
        eng.wait_ge(semaphore, value)
        eng.sem_inc(passed, 1)

    def gate(eng, phase):
        if phase == "E0":
            return
        last = PHASES[PHASES.index(phase) - 1]
        landed = scattered if last in EDGE else stored
        for s in range(landed.n):
            held(eng, landed.sems[s], landed.end(last, s))
        if last in COEF_OF:
            held(eng, coef_ready, COEF_OF[last] + 1)

    with nc.Block() as block:

        @block.sync
        def _(sp):
            for a, b in ((gidx, gidx_d), (dst_i, dst_d), (nxt_i, nxt_d), (typ_i, typ_d), (wgt, wgt_d)):
                sp.dma_start(a[:], b).then_inc(edges_in, 16)
            sp.dma_start(vec[:], vecs).then_inc(edges_in, 16)
            for a, b in ((wa, WaT), (wb, WbT), (w1, W1), (w2, W2), (wl2, WL2T), (wm, WmT), (wih, WihT), (whh, WhhT)):
                sp.dma_start(a[:], b).then_inc(weights_in, 16)
            sp.dma_start(emb_sb[:], emb).then_inc(weights_in, 16)
            sp.dma_start(bmsg_sb[:], rows[3:4, :].to_broadcast([NTYPES, F])).then_inc(weights_in, 16)
            sp.dma_start(brow[:, 0:6 * F], b3.to_broadcast([P, 6 * F])).then_inc(weights_in, 16)
            for i in range(3):
                sp.dma_start(row[:, i, :], rows[i:i + 1, :].to_broadcast([P, F])).then_inc(weights_in, 16)

            def transfers(ph):
                src = node_view(XIN[ph] if ph in DENSE else x)[:, :, :, 0:F]
                if ph in DENSE:
                    other, ov = node_view(DIN[ph]), node_view(OUT[ph])
                gv = gates_d.rearrange("(c k p) f -> c p k f", k=4, p=P)

                def load(c, q, s):
                    if not early(c, 4):
                        if ph == "E0":
                            held(sp, nstats.sem, nstats.at(ph, c - 4))
                        else:
                            held(sp, y_ok.sem, y_ok.at(ph, c - 4))
                    sp.dma_start(xin[s][:], src[c]).then_inc(loaded.sems[s], 16)
                    if ph == "E0":
                        if early(c, 1):
                            held(sp, bgate_ok, 2)
                        sp.dma_start(gv[c * 2], bgate[:]).then_inc(gates_filled, 16)
                        sp.dma_start(gv[c * 2 + 1], bgate[:]).then_inc(gates_filled, 16)
                    elif ph != "A8":
                        sp.dma_start(din[s][:], other[c]).then_inc(agg_in.sems[s], 16)

                def load_gates(c, q, s):
                    if not early(c, 2):
                        held(sp, nin_ok.sem, nin_ok.at(ph, c - 2))
                    sp.dma_start(din3[s][:], other[c]).then_inc(agg_in.sems[s], 16)

                def destinations(c, q, s):
                    if not early(c, 4):
                        held(sp, mask_ok.sem, mask_ok.at(ph, c - 4))
                    sp.dma_start(drow[s][:], dstrow_d[0:1, bass.ds(c * (ET * P), 1 + ET * P)].to_broadcast([P, 1 + ET * P]))\
                        .then_inc(drow_in.sems[s], 16)

                def store(c, q, s):
                    held(sp, y_ok.sem, y_ok.at(ph, c))
                    width = W1C if ph == "A1" else F
                    sp.dma_start(ov[c], yout[s][:, :, 0:width]).then_inc(stored.sems[s], 16)

                if ph == "E0":
                    steps(sp, (0, destinations), (1, load))
                elif ph in EDGE:
                    steps(sp, (0, destinations))
                elif ph == "A8":
                    steps(sp, (0, load), (2, load_gates), (4, store))
                else:
                    steps(sp, (0, load), (3, store))

            for ph in PHASES:
                gate(sp, ph)
                transfers(ph)
            sp.wait_ge(gates_filled, 16 * 2 * STEPS)
            for s in range(4):
                sp.wait_ge(stored.sems[s], stored.end("A8", s))

        @block.gpsimd
        def _(pool):
            nc.gpsimd.memset(ident[:], 0.0).then_inc(consts, 1)
            nc.gpsimd.memset(ones[:], 1.0).then_inc(consts, 1)
            nc.gpsimd.iota(iota_lo[:], [[1, P]], base=0, channel_multiplier=0,
                           allow_small_or_imprecise_dtypes=True).then_inc(consts, 1)
            nc.gpsimd.iota(iota_hi[:], [[1, NODE_TILES]], base=0, channel_multiplier=0,
                           allow_small_or_imprecise_dtypes=True).then_inc(consts, 1)
            nc.gpsimd.memset(valid[:], 1.0).then_inc(consts, 1)
            pool.wait_ge(consts, 5)
            nc.gpsimd.affine_select(out=ident[:], in_=ident[:], compare_op=ALU.not_equal, fill=1.0, base=0,
                                    pattern=[[-1, P]], channel_multiplier=1).then_inc(consts, 1)
            nc.gpsimd.affine_select(out=valid[:], in_=valid[:], compare_op=ALU.is_gt, fill=0.0, base=LAST_ROWS,
                                    pattern=[[0, 1]], channel_multiplier=-1).then_inc(consts, 1)

            def edge(ph):
                table = SRC[ph]
                dest = gates_d if ph == "E4" else agg_d

                def gather(c, q, s):
                    if not early(c, 4):
                        held(pool, gathered.sems[s], gathered.at(ph, q, s, 4))
                        held(pool, seg_done.sem, seg_done.at(ph, c - 4))
                    nc.gpsimd.tensor_copy(grow[s][:], gidx[:, bass.ds(c * ET, ET)]).then_inc(idx_ok.sem, 1)
                    held(pool, idx_ok.sem, idx_ok.at(ph, c))
                    for k in range(ET):
                        to = msgw[s][:, k, :] if ph == "E1" else msg[s][:, k, :]
                        pool.indirect_dma_start(
                            out=to, out_offset=None, in_=table,
                            in_offset=bass.IndirectOffsetOnAxis(ap=grow[s][:, k:k + 1], axis=0),
                        ).then_inc(gathered.sems[s], 16)

                def scatter(c, q, s):
                    if not early(c, 2):
                        held(pool, scattered.sems[s], scattered.at(ph, q, s, 2))
                    nc.gpsimd.tensor_copy(srow[s][:], scat[:, bass.ds(c * ET, ET)]).then_inc(srow_ok.sem, 1)
                    held(pool, srow_ok.sem, srow_ok.at(ph, c))
                    held(pool, res_ok.sem, res_ok.at(ph, c))
                    for k in range(ET):
                        src = (res3 if ph == "E4" else res)[s][:, k, :]
                        pool.indirect_dma_start(
                            out=dest, out_offset=bass.IndirectOffsetOnAxis(ap=srow[s][:, k:k + 1], axis=0),
                            in_=src, in_offset=None, bounds_check=NPAD - 1, oob_is_err=False,
                        ).then_inc(scattered.sems[s], 16)
                steps(pool, (0, gather), (WEIGHT_LAG[ph] + 1, scatter))

            held(pool, ready, READY)
            held(pool, filled, 16 * STEPS)
            for ph in PHASES:
                gate(pool, ph)
                if ph in EDGE:
                    if ph == "E4":
                        held(pool, gates_filled, 16 * 2 * STEPS)
                    edge(ph)
                elif ph == "A6":
                    def body(c, q, s):
                        held(pool, agg_in.sems[s], agg_in.at("A6", q, s))
                        nc.gpsimd.tensor_tensor(din[s][:], din[s][:], a_row[2][:, None, :].to_broadcast([P, NT, F]),
                                                mul).then_inc(agg_ok.sem, 1)
                        held(pool, agg_ok.sem, agg_ok.at("A6", c, 1))
                        nc.gpsimd.tensor_tensor(din[s][:], din[s][:], c_row[2][:, None, :].to_broadcast([P, NT, F]),
                                                add).then_inc(agg_ok.sem, 1)
                    steps(pool, (0, body))

        @block.scalar
        def _(act):
            act.wait_ge(prep, 1)
            av = node_view(agg_d)
            zv = zeros[:].rearrange("p (k f) -> p k f", k=NT)
            with act.Fori(0, STEPS) as c:
                act.dma_start(av[c], zv).then_inc(filled, 16)

            def root(dst, src):
                return nc.scalar.activation(dst, src, ACT.Sqrt, bias=eps_col[:])

            def edge(ph):
                def std(c, q, s):
                    act.wait_ge(emoments.sem, emoments.at(ph, c))
                    root(estd[:], emv[:, :, 1]).then_inc(estd_ok.sem, 1)

                def middle(c, q, s):
                    if ph == "E3":
                        act.wait_ge(seg_ok.sem, seg_ok.at(ph, c))
                        if not early(c, 2):
                            act.wait_ge(out_done.sem, out_done.at(ph, c - 2))
                        nc.scalar.activation(act_in[s], segT[s], ACT.Gelu_apprx_tanh).then_inc(act_ok.sem, 1)
                    else:
                        act.wait_ge(seg_done.sem, seg_done.at(ph, c))
                        if not early(c, 2):
                            act.wait_ge(msg_done.sem, msg_done.at(ph, c - 1))
                        nc.scalar.copy(act_in[s], seg_ps[s][:]).then_inc(act_ok.sem, 1)
                        nc.scalar.copy(cnt[:], cnt_ps[0:NTYPES, :]).then_inc(act_ok.sem, 1)

                def result(c, q, s):
                    if not early(c, 2):
                        act.wait_ge(scattered.sems[s], scattered.at(ph, q, s, 2))
                    act.wait_ge(out_done.sem, out_done.at(ph, c))
                    nc.scalar.copy(res[s][:].rearrange("p k f -> p (k f)"), out_ps[s][:]).then_inc(res_ok.sem, 1)

                stages = []
                if ph in LN_EDGE:
                    stages.append((0, std))
                if ph in ("E3", "E4"):
                    stages.append((3 if ph == "E3" else 2, middle))
                if ph != "E4":
                    stages.append((WEIGHT_LAG[ph], result))
                steps(act, *stages)

            def dense(ph):
                def scale(c, q, s):
                    act.wait_ge(agg_in.sems[s], agg_in.at(ph, q, s))
                    act.wait_ge(ncols_ok.sem, ncols_ok.at(ph, c))
                    for k in range(NT):
                        nc.scalar.mul(din[s][:, k, :], din[s][:, k, :], ncol[s][:, 2, k:k + 1]).then_inc(agg_ok.sem, 1)

                def rows(c, q, s):
                    act.wait_ge(loaded.sems[s], loaded.at(ph, q, s))
                    act.wait_ge(ncols_ok.sem, ncols_ok.at(ph, c))
                    if not early(c, 4):
                        act.wait_ge(y_ok.sem, y_ok.at(ph, c - 4))
                    for k in range(NT):
                        nc.scalar.activation(zb[s][:, k, :], xin[s][:, k, :], ACT.Relu, bias=ncol[s][:, 4, k:k + 1],
                                             scale=ncol[s][:, 1, k:k + 1]).then_inc(z_ok.sem, 1)

                def transposed(c, q, s):
                    if not early(c, 2):
                        act.wait_ge(y_done.sem, y_done.at(ph, c - 2))
                    for g in range(2):
                        cols = slice(g * 4 * F, (g + 1) * 4 * F)
                        act.wait_ge(tp_done.sem, tp_done.at(ph, c, g + 1))
                        if ph == "A5":
                            nc.scalar.activation(zT[s][:, cols], tp_ps[g][:], ACT.Identity, bias=c_col[1][:],
                                                 scale=a_col[1][:]).then_inc(zT_ok.sem, 1)
                        else:
                            ready_to = zT_raw if ph == "A3" else zT_ok
                            nc.scalar.activation(zT[s][:, cols], tp_ps[g][:], ACT.Relu).then_inc(ready_to.sem, 1)
                    if ph == "A3":
                        for g in range(2):
                            cols = slice(g * 4 * F, (g + 1) * 4 * F)
                            act.wait_ge(zT_raw.sem, zT_raw.at(ph, c, g + 1))
                            nc.scalar.activation(zT[s][:, cols], zT[s][:, cols], ACT.Identity, bias=c_col[0][:],
                                                 scale=a_col[0][:]).then_inc(zT_ok.sem, 1)

                def gelu(c, q, s):
                    act.wait_ge(agg_ok.sem, agg_ok.at(ph, c))
                    if not early(c, 4):
                        act.wait_ge(y_ok.sem, y_ok.at(ph, c - 4))
                    nc.scalar.activation(zb[s][:], din[s][:], ACT.Gelu_apprx_tanh).then_inc(gelu_ok.sem, 1)

                def std(c, q, s):
                    act.wait_ge(nmoments.sem, nmoments.at(ph, c))
                    root(nstd[:], nmv[:, :, 1]).then_inc(nstd_ok.sem, 1)

                def norm(c, q, s):
                    act.wait_ge(nbias_ok.sem, nbias_ok.at(ph, c))
                    if not early(c, 2):
                        act.wait_ge(gram_done.sem, gram_done.at(ph, c - 2))
                    for k in range(NT):
                        nc.scalar.activation(hbuf[s][:, k, 0:F], yout[s][:, k, 0:F], ACT.Relu,
                                             bias=nbias[s][:, k:k + 1], scale=nrs[s][:, k:k + 1]).then_inc(h_ok.sem, 1)

                def gates(c, q, s):
                    if not early(c, 2):
                        act.wait_ge(zhn_ok.sem, zhn_ok.at(ph, c - 2))
                    for k in range(NT):
                        act.wait_ge(y_done.sem, y_done.at(ph, c, k + 1))
                        nc.scalar.activation(rz[s][k // 4][:, k % 4, :], bank[2 + k % 4][:, 0:2 * F],
                                             ACT.Sigmoid).then_inc(gate_ok.sem, 1)

                def new(c, q, s):
                    for g in range(2):
                        act.wait_ge(nin_ok.sem, nin_ok.at(ph, c, g + 1))
                        n4 = hbuf[s][:, 4 * g:4 * g + 4, 0:F]
                        nc.scalar.activation(n4, n4, ACT.Tanh).then_inc(tanh_ok.sem, 1)

                if ph == "A1":
                    steps(act, (4, std), (1, scale), (2, transposed), (4, norm))
                elif ph in ("A3", "A5"):
                    steps(act, (1, scale), (2, transposed))
                elif ph == "A6":
                    steps(act, (1, rows))
                elif ph == "A7":
                    steps(act, (1, gelu))
                else:
                    steps(act, (1, rows), (3, gates), (2, transposed), (3, new))

            act.wait_ge(weights_in, 16 * 14)
            for ph in PHASES:
                gate(act, ph)
                if ph in EDGE:
                    edge(ph)
                    if ph == "E0":
                        act.wait_ge(degs, 2)
                        nc.scalar.activation(sqd[:], sqd[:], ACT.Sqrt).then_inc(degs, 1)
                else:
                    dense(ph)
                if ph in MOM_OF:
                    act.wait_ge(mom, 3 * MOM_OF[ph] + 1)
                    root(rstd[:], rstd[:]).then_inc(mom_std, 1)
                if ph in COEF_OF:
                    i = COEF_OF[ph]
                    act.wait_ge(coef, 9 * i + 5)
                    root(bn_col[:, 4:5], bn_col[:, 3:4]).then_inc(coef_std, 1)

        @block.tensor
        def _(pe):
            pe.wait_ge(consts, 7)
            pe.wait_ge(weights_in, 16 * 14)

            def edge(ph):
                def message(c, q, s):
                    pe.wait_ge(act_ok.sem, act_ok.at(ph, c))
                    if not early(c, 1):
                        pe.wait_ge(seg_ok.sem, seg_ok.at(ph, c - 1))
                    nc.tensor.matmul(msg_ps[:], wm[:], act_in[s], start=True, stop=False)
                    nc.tensor.matmul(msg_ps[:], emb_sb[:], cnt[:], start=False, stop=True).then_inc(msg_done.sem, 1)

                def sums(c, q, s):
                    start = early(c, 1)
                    pe.wait_ge(sel_ok.sem, sel_ok.at(ph, c))
                    if ph in ("E1", "E2"):
                        pe.wait_ge(msg_ok.sem, msg_ok.at(ph, c))
                    elif ph == "E4":
                        pe.wait_ge(scaled.sem, scaled.at(ph, c))
                        pe.wait_ge(onehot_ok.sem, onehot_ok.at(ph, c))
                        if not start:
                            pe.wait_ge(act_ok.sem, act_ok.at(ph, c - 1))
                    else:
                        pe.wait_ge(centred.sem, centred.at(ph, c))
                    if not early(c, 2):
                        if ph == "E4":
                            pe.wait_ge(act_ok.sem, act_ok.at(ph, c - 2))
                        else:
                            pe.wait_ge(seg_ok.sem, seg_ok.at(ph, c - 2))
                    if ph == "E4":
                        for k in range(ET):
                            nc.tensor.matmul(cnt_ps[0:NTYPES, k * P:(k + 1) * P], onehot[s][:, k, :], sel[s][:, k, :],
                                             start=True, stop=True)
                    for k in range(ET):
                        last = nc.tensor.matmul(seg_ps[s][:, k * P:(k + 1) * P], msg[s][:, k, :], sel[s][:, k, :],
                                                start=True, stop=True)
                    last.then_inc(seg_done.sem, 1)
                    if ph == "E0":
                        pe.wait_ge(oh_ok.sem, oh_ok.at(ph, c))
                        for k in range(ET):
                            last = nc.tensor.matmul(deg_ps[:, 0:NODE_TILES], oh_lo[:, k, :], oh_hi[:, k, :],
                                                    start=start and k == 0, stop=False, skip_group_check=True)
                        last.then_inc(deg_done.sem, 1)

                def weight(c, q, s):
                    if ph == "E4":
                        for k in range(ET):
                            pe.wait_ge(seg_ok.sem, seg_ok.at(ph, c, k + 1))
                            if not early(c, 1):
                                pe.wait_ge(res_ok.sem, res_ok.at(ph, c - 1, k + 1))
                            nc.tensor.matmul(gate_ps[k][:, 0:3 * F], segT[s][:, k * P:(k + 1) * P], wih[:],
                                             start=True, stop=True).then_inc(out_done.sem, 1)
                        return
                    if ph == "E3":
                        pe.wait_ge(act_ok.sem, act_ok.at(ph, c))
                    else:
                        pe.wait_ge(seg_ok.sem, seg_ok.at(ph, c))
                    if not early(c, 2):
                        pe.wait_ge(res_ok.sem, res_ok.at(ph, c - 2))
                    src = (act_in if ph == "E3" else segT)[s]
                    for k in range(ET):
                        last = nc.tensor.matmul(out_ps[s][:, k * F:(k + 1) * F], src[:, k * P:(k + 1) * P], EW[ph][:],
                                                start=True, stop=True)
                    last.then_inc(out_done.sem, 1)

                if ph == "E4":
                    steps(pe, (3, message), (4, weight), (1, sums))
                else:
                    steps(pe, (WEIGHT_LAG[ph], weight), (1, sums))

            def dense(ph):
                def transposes(c, q, s):
                    for g in range(2):
                        if ph == "A5":
                            pe.wait_ge(loaded.sems[s], loaded.at(ph, q, s))
                        else:
                            pe.wait_ge(z_ok.sem, z_ok.at(ph, c, 4 * g + 4))
                        if not early(c, 1):
                            pe.wait_ge((zT_raw if ph == "A3" else zT_ok).sem,
                                       (zT_raw if ph == "A3" else zT_ok).at(ph, c - 1, g + 1))
                        for k in range(4 * g, 4 * g + 4):
                            src = xin[s] if ph == "A5" else zb[s]
                            last = nc.tensor.transpose(tp_ps[g][:, k % 4 * P:(k % 4 + 1) * P], src[:, k, :], ident[:])
                        last.then_inc(tp_done.sem, 1)

                def products(c, q, s):
                    for g in range(2):
                        pe.wait_ge(zT_ok.sem, zT_ok.at(ph, c, g + 1))
                        pe.wait_ge(agg_ok.sem, agg_ok.at(ph, c, 4 * g + 4))
                        if not early(c, 1):
                            if ph == "A1":
                                pe.wait_ge(y_ok.sem, y_ok.at(ph, c - 1, g + 1))
                            else:
                                pe.wait_ge(y_raw.sem, y_raw.at(ph, c - 1, 4 * g + 4))
                        for k in range(4 * g, 4 * g + 4):
                            o = y_ps[g][:, k % 4 * F:(k % 4 + 1) * F]
                            nc.tensor.matmul(o, zT[s][:, k * P:(k + 1) * P], NW[ph][:], start=True, stop=False)
                            last = nc.tensor.matmul(o, ident[:], din[s][:, k, :], start=False, stop=True)
                        last.then_inc(y_done.sem, 1)

                def gate_products(c, q, s):
                    pe.wait_ge(zT_ok.sem, zT_ok.at(ph, c))
                    pe.wait_ge(agg_in.sems[s], agg_in.at(ph, q, s))
                    for k in range(NT):
                        b = bank[2 + k % 4]
                        if k >= 4:
                            pe.wait_ge(hn_ok.sem, hn_ok.at(ph, c, k - 3))
                        elif not early(c, 1):
                            pe.wait_ge(hn_ok.sem, hn_ok.at(ph, c - 1, k + 5))
                        nc.tensor.matmul(b[:, 0:3 * F], zT[s][:, k * P:(k + 1) * P], whh[:], start=True, stop=False,
                                         skip_group_check=True)
                        nc.tensor.matmul(b[:, 0:2 * F], ident[:], din3[s][:, k, 0:2 * F], start=False, stop=True,
                                         skip_group_check=True).then_inc(y_done.sem, 1)

                def gram(c, q, s):
                    if ph == "A1":
                        pe.wait_ge(h_ok.sem, h_ok.at(ph, c))
                    else:
                        pe.wait_ge(y_ok.sem, y_ok.at(ph, c))
                    r = hbuf[s] if ph == "A1" else yout[s]
                    for k in range(NT):
                        last = nc.tensor.matmul(gram_ps[:, 0:F + 1], r[:, k, 0:F], r[:, k, 0:F + 1],
                                                start=early(c, 1) and k == 0, stop=False,
                                                skip_group_check=True)
                    last.then_inc(gram_done.sem, 1)

                if ph == "A8":
                    steps(pe, (3, gate_products), (2, transposes))
                elif ph == "A1":
                    steps(pe, (3, products), (2, transposes), (5, gram))
                else:
                    steps(pe, (3, products), (2, transposes), (4, gram))

            for ph in PHASES:
                gate(pe, ph)
                if ph in EDGE:
                    edge(ph)
                elif ph in ("A1", "A3", "A5", "A8"):
                    dense(ph)
                if ph in COEF_OF:
                    pe.wait_ge(coef, 9 * COEF_OF[ph] + 9)
                    nc.tensor.matmul(bank[6][:, 0:F], ones[:], diag_a[:], start=True, stop=True)
                    nc.tensor.matmul(bank[6][:, F:2 * F], ones[:], diag_c[:], start=True, stop=True).then_inc(coef_rows, 1)

        @block.vector
        def _(dve):
            v = nc.vector
            v.memset(zeros[:], 0.0).then_inc(prep, 1)
            v.memset(zero_col[:], 0.0)
            v.memset(eps_col[:], EPS)
            v.memset(hbuf[0][:, :, F:F + 1], 1.0)
            v.memset(hbuf[1][:, :, F:F + 1], 1.0).then_inc(prep, 1)
            n = [2]

            def done(ins):
                ins.then_inc(prep, 1)
                n[0] += 1
                dve.wait_ge(prep, n[0])

            dve.wait_ge(edges_in, 16 * E_DMAS)
            done(v.tensor_copy(dst_f[:], dst_i[:]))
            done(v.tensor_copy(nxt_f[:], nxt_i[:]))
            done(v.tensor_tensor(nxt_f[:], nxt_f[:], dst_f[:], eq))
            done(v.scalar_tensor_tensor(nxt_f[:], nxt_f[:], 100000.0, dst_f[:], mul, add))
            done(v.tensor_copy(scat[:], nxt_f[:]))
            done(v.tensor_scalar(nxt_i[:], dst_i[:], 7, None, ALU.logical_shift_right))
            done(v.tensor_copy(hi_f[:], nxt_i[:]))
            done(v.tensor_scalar(nxt_i[:], dst_i[:], 127, None, ALU.bitwise_and))
            done(v.tensor_copy(lo_f[:], nxt_i[:]))
            done(v.tensor_copy(typ_f[:], typ_i[:]))
            done(v.tensor_scalar(typ_f[:], typ_f[:], 0.0, float(NTYPES - 1), mx, ALU.min))
            dve.wait_ge(consts, 7)
            dve.wait_ge(weights_in, 16 * 14)
            done(v.tensor_tensor(emb_sb[:], emb_sb[:], bmsg_sb[:], add))
            done(v.tensor_copy(brow[:, 6 * F:7 * F], brow[:, 5 * F:6 * F]))
            done(v.memset(brow[:, 5 * F:6 * F], 0.0))
            done(v.tensor_tensor(brow[:, 0:3 * F], brow[:, 0:3 * F], brow[:, 3 * F:6 * F], add))
            v.tensor_copy(bgate[:], brow[:, None, 0:3 * F].to_broadcast([P, 4, 3 * F])).then_inc(bgate_ok, 1)
            dve.wait_ge(bgate_ok, 1)
            v.memset(brow[:, 5 * F:6 * F], 0.0).then_inc(bgate_ok, 1)
            dve.wait_ge(bgate_ok, 2)
            dve.sem_inc(ready, READY)

            def moments(ph, c, rows_of):
                for k in range(NT):
                    v.bn_stats(nst[:, k, :], rows_of(k)).then_inc(nstats.sem, 1)
                held(dve, nstats.sem, nstats.at(ph, c))
                if not early(c, 1):
                    held(dve, kept.sem, kept.at(ph, c - 1))
                for k in range(NT):
                    v.bn_aggr(nmv[:, k, :], nst[:, k, :]).then_inc(nmoments.sem, 1)

            def keep(ph, c):
                held(dve, nmoments.sem, nmoments.at(ph, c))
                v.tensor_copy(mean[:, bass.ds(c * NT, NT)], nmv[:, :, 0]).then_inc(kept.sem, 1)
                v.tensor_copy(rstd[:, bass.ds(c * NT, NT)], nmv[:, :, 1]).then_inc(kept.sem, 1)

            def edge(ph):
                def columns(c, q, s):
                    if not early(c, 4):
                        held(dve, sel_ok.sem, sel_ok.at(ph, c - 4))
                        held(dve, mask_ok.sem, mask_ok.at(ph, c - 4))
                    v.tensor_copy(ecol[s][:, 0, :], dst_f[:, bass.ds(c * ET, ET)]).then_inc(cols_ok.sem, 1)
                    v.tensor_copy(ecol[s][:, 1, :], (dinv_src if ph == "E2" else wgt)[:, bass.ds(c * ET, ET)])\
                        .then_inc(cols_ok.sem, 1)
                    v.tensor_copy(ecol[s][:, 2, :], typ_f[:, bass.ds(c * ET, ET)]).then_inc(cols_ok.sem, 1)
                    held(dve, drow_in.sems[s], drow_in.at(ph, q, s))
                    v.tensor_copy(lastcol[s][:], drow[s][:, 0:ET * P].rearrange("p (k q) -> p k q", q=P)[:, :, 0])\
                        .then_inc(last_ok.sem, 1)

                def statistics(c, q, s):
                    columns(c, q, s)
                    if ph not in LN_EDGE:
                        return
                    raw = msgw[s] if ph == "E1" else msg[s]
                    dve.wait_ge(gathered.sems[s], gathered.at(ph, q, s))
                    for k in range(ET):
                        v.bn_stats(est[:, k, :], raw[:, k, 0:F]).then_inc(estats.sem, 1)
                    held(dve, estats.sem, estats.at(ph, c))
                    for k in range(ET):
                        v.bn_aggr(emv[:, k, :], est[:, k, :]).then_inc(emoments.sem, 1)

                def front(c, q, s):
                    m = msg[s]
                    raw = msgw[s] if ph == "E1" else m
                    if ph not in LN_EDGE:
                        dve.wait_ge(gathered.sems[s], gathered.at(ph, q, s))
                    else:
                        dve.wait_ge(emoments.sem, emoments.at(ph, c))
                        if ph == "E1" and not early(c, 4):
                            dve.wait_ge(seg_done.sem, seg_done.at(ph, c - 4))
                        for k in range(ET):
                            v.tensor_scalar(m[:, k, :], raw[:, k, 0:F], emv[:, k, 0:1], 0.0, sub, mx)\
                                .then_inc(centred.sem, 1)
                        dve.wait_ge(estd_ok.sem, estd_ok.at(ph, c))
                        v.reciprocal(ers[:], estd[:]).then_inc(ers_ok.sem, 1)
                        dve.wait_ge(ers_ok.sem, ers_ok.at(ph, c))
                    held(dve, cols_ok.sem, cols_ok.at(ph, c))
                    if ph == "E0":
                        v.tensor_copy(eww[:], ers[:]).then_inc(eww_ok.sem, 1)
                    elif ph == "E1":
                        v.tensor_copy(eww[:], raw[:, :, F]).then_inc(eww_ok.sem, 1)
                        v.tensor_copy(dinv_src[:, bass.ds(c * ET, ET)], raw[:, :, F])
                    elif ph == "E2":
                        v.tensor_copy(eww[:], ecol[s][:, 1, :]).then_inc(eww_ok.sem, 1)
                    elif ph == "E3":
                        v.tensor_tensor(eww[:], ers[:], ecol[s][:, 1, :], mul).then_inc(eww_ok.sem, 1)
                    else:
                        v.memset(eww[:], 1.0).then_inc(eww_ok.sem, 1)
                    if ph == "E1":
                        dve.wait_ge(centred.sem, centred.at(ph, c))
                        for k in range(ET):
                            v.scalar_tensor_tensor(m[:, k, :], m[:, k, :], ers[:, k:k + 1], a_row[0][:], mul, mul)\
                                .then_inc(scaled.sem, 1)
                        dve.wait_ge(scaled.sem, scaled.at(ph, c))
                        v.tensor_tensor(m, m, c_row[0][:, None, :].to_broadcast([P, ET, F]), add)\
                            .then_inc(msg_ok.sem, 1)
                    elif ph == "E2":
                        v.tensor_tensor(m, m, a_row[1][:, None, :].to_broadcast([P, ET, F]), mul)\
                            .then_inc(scaled.sem, 1)
                        dve.wait_ge(scaled.sem, scaled.at(ph, c))
                        v.tensor_tensor(m, m, c_row[1][:, None, :].to_broadcast([P, ET, F]), add)\
                            .then_inc(msg_ok.sem, 1)
                    elif ph == "E4":
                        dve.wait_ge(centred.sem, centred.at(ph, c))
                        for k in range(ET):
                            v.tensor_scalar(m[:, k, :], m[:, k, :], ers[:, k:k + 1], None, mul).then_inc(scaled.sem, 1)
                        if not early(c, 2):
                            dve.wait_ge(seg_done.sem, seg_done.at(ph, c - 2))
                        for k in range(ET):
                            v.tensor_scalar(onehot[s][:, k, :], iota_lo[:, 0:NTYPES], ecol[s][:, 2, k:k + 1], None, eq)\
                                .then_inc(onehot_ok.sem, 1)
                    dve.wait_ge(eww_ok.sem, eww_ok.at(ph, c))
                    if not early(c, 4):
                        held(dve, seg_done.sem, seg_done.at(ph, c - 4))
                    for k in range(ET):
                        v.tensor_scalar(sel[s][:, k, :], drow[s][:, k * P + 1:k * P + 1 + P],
                                        ecol[s][:, 0, k:k + 1], eww[:, k:k + 1], eq, mul).then_inc(sel_ok.sem, 1)

                def digits(c, q, s):
                    if not early(c, 1):
                        held(dve, deg_done.sem, deg_done.at(ph, c - 1))
                    v.tensor_copy(digit[:, 0, :], hi_f[:, bass.ds(c * ET, ET)]).then_inc(digits_ok.sem, 1)
                    v.tensor_copy(digit[:, 1, :], lo_f[:, bass.ds(c * ET, ET)]).then_inc(digits_ok.sem, 1)
                    held(dve, digits_ok.sem, digits_ok.at(ph, c))
                    for k in range(ET):
                        v.tensor_scalar(oh_hi[:, k, :], iota_hi[:], digit[:, 0, k:k + 1], None, eq)\
                            .then_inc(oh_ok.sem, 1)
                        v.tensor_scalar(oh_lo[:, k, :], iota_lo[:], digit[:, 1, k:k + 1], None, eq)\
                            .then_inc(oh_ok.sem, 1)

                def totals(c, q, s):
                    start = early(c, 1)
                    if ph == "E4":
                        dve.wait_ge(msg_done.sem, msg_done.at(ph, c))
                        ps = msg_ps
                    else:
                        dve.wait_ge(seg_done.sem, seg_done.at(ph, c))
                        ps = seg_ps[s]
                    held(dve, last_ok.sem, last_ok.at(ph, c))
                    if not early(c, 2):
                        held(dve, out_done.sem, out_done.at(ph, c - 2))
                    for k in range(ET):
                        if k > 0:
                            carry = segT[s][:, k * P - 1:k * P]
                            held(dve, seg_ok.sem, seg_ok.at(ph, c, k))
                        elif start:
                            carry = zero_col[:]
                        else:
                            carry = segT[(s + 3) % 4][:, ET * P - 1:ET * P]
                            held(dve, seg_ok.sem, seg_ok.at(ph, c - 1))
                        v.tensor_scalar(cmask[:], drow[s][:, k * P + 1:k * P + 1 + P],
                                        lastcol[s][:, k:k + 1], carry, eq, mul).then_inc(mask_ok.sem, 1)
                        dve.wait_ge(mask_ok.sem, mask_ok.at(ph, c, k + 1))
                        v.tensor_tensor(segT[s][:, k * P:(k + 1) * P], ps[:, k * P:(k + 1) * P], cmask[:], add)\
                            .then_inc(seg_ok.sem, 1)

                def gate_rows(c, q, s):
                    if not early(c, 2):
                        held(dve, scattered.sems[s], scattered.at(ph, q, s, 2))
                    for k in range(ET):
                        dve.wait_ge(out_done.sem, out_done.at(ph, c, k + 1))
                        v.tensor_tensor(res3[s][:, k, :], gate_ps[k][:, 0:3 * F], bgate[:, 0, :], add)\
                            .then_inc(res_ok.sem, 1)

                def input_moments(c, q, s):
                    if not early(c, 1):
                        keep(ph, c - 1)
                    dve.wait_ge(loaded.sems[s], loaded.at(ph, q, s))
                    moments(ph, c, lambda k: xin[s][:, k, :])

                stages = [(1, front), (3 if ph == "E4" else 2, totals)]
                if ph == "E4":
                    stages.append((4, gate_rows))
                if ph == "E0":
                    stages += [(1, digits), (1, input_moments)]
                stages.append((0, statistics))
                steps(dve, *stages)
                if ph == "E0":
                    keep(ph, STEPS - 1)

            def dense(ph):
                scale_of = {"A1": rdeg, "A3": sqd, "A5": sqd}.get(ph, rdeg)

                def columns(c, q, s):
                    if not early(c, 4):
                        held(dve, y_ok.sem, y_ok.at(ph, c - 4))
                    for i, a in enumerate((mean, rstd, scale_of, dinv if ph == "A1" else dinv2, mbias)):
                        v.tensor_copy(ncol[s][:, i, :], a[:, bass.ds(c * NT, NT)]).then_inc(ncols_ok.sem, 1)

                def front(c, q, s):
                    if ph in ("A1", "A3"):
                        held(dve, ncols_ok.sem, ncols_ok.at(ph, c))
                        dve.wait_ge(loaded.sems[s], loaded.at(ph, q, s))
                        if not early(c, 4):
                            held(dve, tp_done.sem, tp_done.at(ph, c - 4))
                        for k in range(NT):
                            v.tensor_scalar(zb[s][:, k, :], xin[s][:, k, :], ncol[s][:, 0, k:k + 1],
                                            ncol[s][:, 1, k:k + 1], sub, mul).then_inc(z_ok.sem, 1)
                    if ph == "A7":
                        dve.wait_ge(agg_in.sems[s], agg_in.at(ph, q, s))
                        v.tensor_tensor(din[s][:], din[s][:], row[:, 2:3, :].to_broadcast([P, NT, F]), add)\
                            .then_inc(agg_ok.sem, 1)

                def back(c, q, s):
                    X, Dn, Y, z = xin[s], din[s], yout[s], zb[s]
                    if not early(c, 4) and ph != "A8":
                        held(dve, stored.sems[s], stored.at(ph, q, s, 4))
                        if ph in ("A3", "A5"):
                            held(dve, gram_done.sem, gram_done.at(ph, c - 4))
                        if ph == "A1":
                            held(dve, h_ok.sem, h_ok.at(ph, c - 4))
                    if ph == "A1":
                        v.tensor_copy(Y[:, :, F:W1C], ncol[s][:, 3, :, None].to_broadcast([P, NT, 4]))
                        for g in range(2):
                            ks = slice(4 * g, 4 * g + 4)
                            dve.wait_ge(y_done.sem, y_done.at(ph, c, g + 1))
                            v.scalar_tensor_tensor(Y[:, ks, 0:F], y_ps[g][:].rearrange("p (k f) -> p k f", f=F), 0.0,
                                                   X[:, ks, :], mx, add).then_inc(y_ok.sem, 1)
                    if ph in ("A3", "A5"):
                        for k in range(NT):
                            dve.wait_ge(y_done.sem, y_done.at(ph, c, k // 4 + 1))
                            v.scalar_tensor_tensor(Y[:, k, 0:F], y_ps[k // 4][:, k % 4 * F:(k % 4 + 1) * F],
                                                   ncol[s][:, 3, k:k + 1], row[:, 0 if ph == "A3" else 1, :],
                                                   mul, add).then_inc(y_raw.sem, 1)
                        dve.wait_ge(y_raw.sem, y_raw.at(ph, c))
                        if isinstance(c, int) and c == STEPS - 1:
                            v.tensor_scalar(Y[:, 0:NT - 2, 0:F], Y[:, 0:NT - 2, 0:F], 0.0, None, mx)
                            v.tensor_scalar(Y[:, NT - 2, 0:F], Y[:, NT - 2, 0:F], 0.0, valid[:], mx, mul)
                            v.memset(Y[:, NT - 1, 0:F], 0.0).then_inc(y_ok.sem, 1)
                        else:
                            v.tensor_scalar(Y[:, :, 0:F], Y[:, :, 0:F], 0.0, None, mx).then_inc(y_ok.sem, 1)
                    if ph == "A6":
                        dve.wait_ge(z_ok.sem, z_ok.at(ph, c))
                        v.tensor_tensor(z[:], z[:], a_row[0][:, None, :].to_broadcast([P, NT, F]), mul)\
                            .then_inc(y_raw.sem, 1)
                        dve.wait_ge(y_raw.sem, y_raw.at(ph, c, 1))
                        v.tensor_tensor(z[:], z[:], X[:], add).then_inc(y_raw.sem, 1)
                        dve.wait_ge(y_raw.sem, y_raw.at(ph, c, 2))
                        dve.wait_ge(agg_ok.sem, agg_ok.at(ph, c))
                        v.tensor_tensor(Y[:, :, 0:F], z[:], Dn[:], add).then_inc(y_ok.sem, 1)
                    if ph == "A7":
                        dve.wait_ge(gelu_ok.sem, gelu_ok.at(ph, c))
                        v.tensor_tensor(Y[:, :, 0:F], z[:], X[:], add).then_inc(y_ok.sem, 1)
                    if ph == "A8":
                        if not early(c, 2):
                            held(dve, nzh_ok.sem, nzh_ok.at(ph, c - 2))
                        for g in range(2):
                            ks = slice(4 * g, 4 * g + 4)
                            hb = hbuf[s][:, ks, 0:F]
                            for k in range(4 * g, 4 * g + 4):
                                dve.wait_ge(gate_ok.sem, gate_ok.at(ph, c, k + 1))
                                v.tensor_tensor(hbuf[s][:, k, 0:F], bank[2 + k % 4][:, 2 * F:3 * F],
                                                brow[:, 6 * F:7 * F], add).then_inc(hn_ok.sem, 1)
                            dve.wait_ge(hn_ok.sem, hn_ok.at(ph, c, 4 * g + 4))
                            v.tensor_tensor(hb, hb, rz[s][g][:, :, 0:F], mul).then_inc(rhn_ok.sem, 1)
                            dve.wait_ge(rhn_ok.sem, rhn_ok.at(ph, c, g + 1))
                            v.tensor_tensor(hb, hb, din3[s][:, ks, 2 * F:3 * F], add).then_inc(nin_ok.sem, 1)
                    if ph in ST:
                        held(dve, y_ok.sem, y_ok.at(ph, c))
                        moments(ph, c, lambda k: Y[:, k, 0:F])

                def mix(c, q, s):
                    X, Y, z = xin[s], yout[s], zb[s]
                    if not early(c, 4):
                        held(dve, stored.sems[s], stored.at(ph, q, s, 4))
                    for g in range(2):
                        ks = slice(4 * g, 4 * g + 4)
                        hb = hbuf[s][:, ks, 0:F]
                        dve.wait_ge(tanh_ok.sem, tanh_ok.at(ph, c, g + 1))
                        v.tensor_tensor(z[:, ks, :], z[:, ks, :], hb, sub).then_inc(hmn_ok.sem, 1)
                    for g in range(2):
                        ks = slice(4 * g, 4 * g + 4)
                        dve.wait_ge(hmn_ok.sem, hmn_ok.at(ph, c, g + 1))
                        v.tensor_tensor(z[:, ks, :], z[:, ks, :], rz[s][g][:, :, F:2 * F], mul).then_inc(zhn_ok.sem, 1)
                    for g in range(2):
                        ks = slice(4 * g, 4 * g + 4)
                        hb = hbuf[s][:, ks, 0:F]
                        dve.wait_ge(zhn_ok.sem, zhn_ok.at(ph, c, g + 1))
                        v.tensor_tensor(z[:, ks, :], z[:, ks, :], hb, add).then_inc(nzh_ok.sem, 1)
                    for g in range(2):
                        ks = slice(4 * g, 4 * g + 4)
                        dve.wait_ge(nzh_ok.sem, nzh_ok.at(ph, c, g + 1))
                        v.tensor_tensor(Y[:, ks, 0:F], z[:, ks, :], X[:, ks, :], add).then_inc(y_ok.sem, 1)

                def tail(c, q, s):
                    if ph != "A1":
                        keep(ph, c)
                        return
                    dve.wait_ge(nstd_ok.sem, nstd_ok.at(ph, c))
                    if not early(c, 2):
                        dve.wait_ge(h_ok.sem, h_ok.at(ph, c - 2))
                    v.reciprocal(nrs[s][:], nstd[:]).then_inc(nrs_ok.sem, 1)
                    held(dve, nrs_ok.sem, nrs_ok.at(ph, c))
                    v.scalar_tensor_tensor(nbias[s][:], nmv[:, :, 0], -1.0, nrs[s][:], mul, mul)\
                        .then_inc(nbias_ok.sem, 1)
                    held(dve, nbias_ok.sem, nbias_ok.at(ph, c))
                    v.tensor_copy(mean[:, bass.ds(c * NT, NT)], nmv[:, :, 0])
                    v.tensor_copy(rstd[:, bass.ds(c * NT, NT)], nrs[s][:]).then_inc(kept.sem, 1)
                    v.tensor_copy(mbias[:, bass.ds(c * NT, NT)], nbias[s][:]).then_inc(kept.sem, 1)

                later = 2 if ph in ("A6", "A7") else 3
                stages = [(0, columns), (1, front)]
                if ph in ST:
                    stages.append((later + 1, tail))
                if ph == "A8":
                    stages = [(later + 1, mix)] + stages
                stages.append((later, back))
                steps(dve, *stages)

            def roots(ph):
                i = MOM_OF[ph]
                held(dve, kept.sem, kept.end(ph))
                dve.sem_inc(mom, 1)
                dve.wait_ge(mom_std, i + 1)
                v.reciprocal(rstd[:], rstd[:]).then_inc(mom, 1)
                dve.wait_ge(mom, 3 * i + 2)
                v.scalar_tensor_tensor(mbias[:], mean[:], -1.0, rstd[:], mul, mul).then_inc(mom, 1)
                dve.wait_ge(mom, 3 * i + 3)

            def coefficients(ph):
                i = COEF_OF[ph]
                k = [9 * i]

                def one(ins):
                    ins.then_inc(coef, 1)
                    k[0] += 1
                    dve.wait_ge(coef, k[0])

                dve.wait_ge(gram_done.sem, gram_done.end(ph))
                one(v.tensor_tensor(bn_tmp[:], gram_ps[:, 0:F], ident[:], mul))
                one(v.reduce_sum(bn_col[:, 1:2], bn_tmp[:], AX.X))
                one(v.tensor_scalar(bn_col[:, 0:1], gram_ps[:, F:F + 1], 1.0 / N_NODES, None, mul))
                one(v.tensor_tensor(bn_col[:, 2:3], bn_col[:, 0:1], bn_col[:, 0:1], mul))
                one(v.scalar_tensor_tensor(bn_col[:, 3:4], bn_col[:, 1:2], 1.0 / N_NODES, bn_col[:, 2:3], mul, sub))
                dve.wait_ge(coef_std, i + 1)
                one(v.reciprocal(bn_col[:, 5:6], bn_col[:, 4:5]))
                one(v.tensor_tensor(a_col[i][:], bn_col[:, 5:6], vec[:, 2 * i:2 * i + 1], mul))
                one(v.scalar_tensor_tensor(c_col[i][:], a_col[i][:], bn_col[:, 0:1], vec[:, 2 * i + 1:2 * i + 2], mul, sub))
                v.tensor_scalar(diag_a[:], ident[:], a_col[i][:], None, mul)
                v.tensor_scalar(diag_c[:], ident[:], c_col[i][:], -1.0, mul, mul).then_inc(coef, 1)
                k[0] += 1
                dve.wait_ge(coef, k[0])
                v.tensor_scalar(c_col[i][:], c_col[i][:], -1.0, None, mul)
                dve.wait_ge(coef_rows, i + 1)
                v.tensor_copy(a_row[i][:], bank[6][:, 0:F]).then_inc(coef_end, 1)
                v.tensor_copy(c_row[i][:], bank[6][:, F:2 * F]).then_inc(coef_end, 1)
                dve.wait_ge(coef_end, 2 * i + 2)
                if i == 2:
                    v.tensor_tensor(c_row[2][:], c_row[2][:], c_row[0][:], add).then_inc(coef_end, 1)
                    dve.wait_ge(coef_end, 7)
                dve.sem_inc(coef_ready, 1)

            for ph in PHASES:
                if ph in EDGE:
                    gate(dve, ph)
                    edge(ph)
                    if ph == "E0":
                        dve.wait_ge(deg_done.sem, deg_done.end("E0"))
                        v.tensor_copy(deg[:], deg_ps[:, 0:NODE_TILES]).then_inc(degs, 1)
                        dve.wait_ge(degs, 1)
                        v.tensor_scalar(sqd[:], deg[:], 1.0, None, add).then_inc(degs, 1)
                        dve.wait_ge(degs, 3)
                        v.tensor_scalar(rdeg[:], deg[:], 1.0, None, mx).then_inc(degs, 1)
                        dve.wait_ge(degs, 4)
                        v.reciprocal(rdeg[:], rdeg[:]).then_inc(degs, 1)
                        v.reciprocal(dinv[:], sqd[:]).then_inc(degs, 1)
                        v.tensor_scalar(dinv2[:], deg[:], 1.0, None, add).then_inc(degs, 1)
                        dve.wait_ge(degs, 7)
                        v.reciprocal(dinv2[:], dinv2[:]).then_inc(degs, 1)
                        dve.wait_ge(degs, 8)
                        roots(ph)
                else:
                    gate(dve, ph)
                    if ph in ("A3", "A5"):
                        for b in yout[0:4]:
                            v.memset(b[:, :, F:F + 1], 1.0).then_inc(ones_ok, 1)
                        held(dve, ones_ok, 4 if ph == "A3" else 8)
                    dense(ph)
                    if ph in MOM_OF:
                        roots(ph)
                    if ph in COEF_OF:
                        if ph == "A1":
                            for s in range(4):
                                held(dve, stored.sems[s], stored.end("A1", s))
                        coefficients(ph)


_OUT = "out_dram"


def kernel(**inputs):
    import concourse.bacc as bacc
    from concourse.bass_utils import run_bass_kernel_spmd

    def edge_columns(a, fill):
        p = np.full((EPAD,), fill, a.dtype)
        p[:N_EDGES] = a
        return np.ascontiguousarray(p.reshape(EDGE_TILES, P).T)

    i = {k: np.asarray(v) for k, v in inputs.items()}
    xp = np.zeros((NPAD, F), i["x"].dtype)
    xp[:N_NODES] = i["x"]
    dst = i["dst"]
    nxt = np.concatenate([dst[1:], np.full((1,), DST_NONE, dst.dtype)])
    drow = np.full((1, 1 + EPAD), DST_NONE, dst.dtype)
    drow[0, 0] = DST_NONE + 1
    drow[0, 1:1 + N_EDGES] = dst
    W0 = i["L0_gnn_W"]
    t = lambda a: np.ascontiguousarray(a.T)
    arrays = {
        "x": xp,
        "gidx": edge_columns(i["src"], 0).view(np.uint32),
        "dst": edge_columns(dst, DST_NONE),
        "nxt": edge_columns(nxt, DST_NONE),
        "typ": edge_columns(i["edge_type_9"], 0),
        "wgt": edge_columns(i["edge_weight1"][:, 0], 0),
        "dstrow": drow,
        "WaT": t(W0[:, :F]), "WbT": t(W0[:, F:]),
        "W1": i["L1_gnn_W1"], "W2": i["L1_gnn_W2"], "WL2T": t(i["L2_gnn_W"]),
        "WmT": i["L3_gnn_W_msg"].T.copy(), "WihT": t(i["L3_gnn_W_ih"]), "WhhT": t(i["L3_gnn_W_hh"]),
        "emb": i["L3_gnn_edge_embed"],
        "vecs": np.ascontiguousarray(np.stack([i[f"L1_gnn_bn{k}_{n}"] for k in range(3) for n in ("gamma", "beta")], 1)),
        "rows": np.stack([i["L1_gnn_b1"], i["L1_gnn_b2"], i["L2_gnn_b"], i["L3_gnn_b_msg"]]),
        "b3": np.concatenate([i["L3_gnn_b_ih"], i["L3_gnn_b_hh"]])[None, :],
    }
    nc = bacc.Bacc("TRN2", target_bir_lowering=False, num_devices=1)
    args = [nc.dram_tensor(f"in_{n}", a.shape, mybir.dt.from_np(a.dtype), kind="ExternalInput").ap()
            for n, a in arrays.items()]
    args.append(nc.dram_tensor(_OUT, (NPAD, F), mybir.dt.float32, kind="ExternalOutput").ap())
    build(nc, *args)
    r = run_bass_kernel_spmd(nc, [{f"in_{n}": np.ascontiguousarray(a) for n, a in arrays.items()}], core_ids=[0])
    return np.asarray(r.results[0][_OUT])[:N_NODES]
```

```python
import numpy as np
import concourse.bass as bass
from concourse import mybir

N_NODES, N_EDGES, F = 50000, 25000, 128
P = 128
STEPS = 49
NT = 8
ET = 4
NODE_TILES, EDGE_TILES = STEPS * NT, STEPS * ET
NPAD, EPAD = NODE_TILES * P, EDGE_TILES * P
W1C = F + 4
NTYPES = 9
EPS = 1e-5
DST_NONE = 60000
LAST_ROWS = N_NODES - (NODE_TILES - 2) * P

PHASES = ["D0", "E0", "A1", "E1", "A3", "E2", "A5", "A6", "E3", "A7", "E4", "A8"]
EDGE = ["E0", "E1", "E2", "E3", "E4"]
LN_EDGE = ["E0", "E1", "E3", "E4"]
DENSE = ["A1", "A3", "A5", "A6", "A7", "A8"]


class Stage:

    def __init__(self, nc, name, per):
        self.sem = nc.alloc_semaphore(name)
        self.per = per

    def before(self, phase):
        return sum(STEPS * self.per.get(p, 0) for p in PHASES[:PHASES.index(phase)])

    def at(self, phase, step, k=None):
        per = self.per[phase]
        return step * per + (self.before(phase) + (per if k is None else k))

    def end(self, phase):
        return self.before(phase) + STEPS * self.per.get(phase, 0)


class Slots:

    def __init__(self, nc, name, per, n):
        own = [nc.alloc_semaphore(f"{name}{s}") for s in range(n)]
        self.sems = own * (4 // n)
        self.n, self.per = n, per

    def before(self, phase, s):
        return 16 * sum(self.per.get(p, 0) * len(range(s % self.n, STEPS, self.n)) for p in PHASES[:PHASES.index(phase)])

    def at(self, phase, q, s, back=0):
        q, s = q + (s - back) // 4 if (s - back) // 4 else q, (s - back) % 4
        per = 16 * self.per[phase]
        return q * (per * (4 // self.n)) + (self.before(phase, s) + per * (s // self.n + 1))

    def end(self, phase, s):
        return self.before(phase, s) + 16 * self.per.get(phase, 0) * len(range(s % self.n, STEPS, self.n))


def steps(eng, *stages):
    longest = max(lag for lag, _ in stages)
    first = (4 + longest + 3) // 4

    def turn(t):
        for lag, body in stages:
            if 0 <= t - lag < STEPS:
                body(t - lag, (t - lag) // 4, (t - lag) % 4)

    for t in range(4 * first):
        turn(t)
    with eng.Fori(first, STEPS // 4) as group:
        for i in range(4):
            for lag, body in stages:
                back = (i - lag) // 4
                body(group * 4 + (i - lag), group + back if back else group, (i - lag) % 4)
    for t in range(STEPS - 1, STEPS + longest):
        turn(t)


def early(step, n):
    return isinstance(step, int) and step < n


def build(nc, x, gidx_d, dst_d, nxt_d, typ_d, wgt_d, dstrow_d, WaT, WbT, W1, W2, WL2T, WmT, WihT, WhhT,
          emb, vecs, rows, gate_biases, out):
    f32r = mybir.dt.float32r
    f32, u32, i32 = mybir.dt.float32, mybir.dt.uint32, mybir.dt.int32
    bf16 = mybir.dt.bfloat16
    ALU, ACT, AX = mybir.AluOpType, mybir.ActivationFunctionType, mybir.AxisListType
    add, sub, mul, mx, eq = ALU.add, ALU.subtract, ALU.mult, ALU.max, ALU.is_equal

    def sb(name, shape, dt=f32):
        return nc.alloc_sbuf_tensor(name, shape, dt)

    def sem(name):
        return nc.alloc_semaphore(name)

    x1_d = nc.dram_tensor("x1_rows", [NPAD, W1C], f32).ap()
    t1_d = nc.dram_tensor("t1_rows", [NPAD, F], f32).ap()
    t2_d = nc.dram_tensor("t2_rows", [NPAD, F], f32).ap()
    x2_d = nc.dram_tensor("x2_rows", [NPAD, F], f32).ap()
    x3_d = nc.dram_tensor("x3_rows", [NPAD, F], f32).ap()
    agg_d = nc.dram_tensor("agg_rows", [NPAD, F], f32).ap()

    def node_view(ap):
        return ap.rearrange("(c k p) f -> c p k f", k=NT, p=P)

    ident, ones = sb("ident", [P, P]), sb("ones", [P, P])
    iota_lo, iota_hi = sb("iota_lo", [P, P]), sb("iota_hi", [P, NODE_TILES])
    wa, wb = sb("wa", [P, F]), sb("wb", [P, F])
    w1, w2, wl2, wm = sb("w1", [P, F]), sb("w2", [P, F]), sb("wl2", [P, F]), sb("wm", [P, F])
    wih, whh = sb("wih", [P, 3 * F]), sb("whh", [P, 3 * F])
    wih_high, wih_low, whh_high, whh_low = (sb(n, [P, 3 * F], f32r) for n in ("wih_high", "wih_low", "whh_high", "whh_low"))
    emb_sb, bmsg_sb = sb("emb_sb", [NTYPES, F]), sb("bmsg_sb", [NTYPES, F])
    vec = sb("vec", [P, 6])
    row = sb("row", [P, 3, F])
    gb = sb("gb", [P, 6])
    zero_col, eps_col = sb("zero_col", [P, 1]), sb("eps_col", [P, 1])
    gidx, scat = sb("gidx", [P, EDGE_TILES], u32), sb("scat", [P, EDGE_TILES], u32)
    dst_i, nxt_i = sb("dst_i", [P, EDGE_TILES], i32), sb("nxt_i", [P, EDGE_TILES], i32)
    dst_f, nxt_f = sb("dst_f", [P, EDGE_TILES]), sb("nxt_f", [P, EDGE_TILES])
    hi_f, lo_f = sb("hi_f", [P, EDGE_TILES]), sb("lo_f", [P, EDGE_TILES])
    typ_i, typ_f = sb("typ_i", [P, EDGE_TILES], i32), sb("typ_f", [P, EDGE_TILES])
    wgt = sb("wgt", [P, EDGE_TILES])
    dinv_src = sb("dinv_src", [P, EDGE_TILES])
    drow = [sb(f"drow{s}", [P, 1 + ET * P], i32) for s in range(4)]
    deg, rdeg = sb("deg", [P, NODE_TILES]), sb("rdeg", [P, NODE_TILES])
    sqd, dinv, dinv2 = sb("sqd", [P, NODE_TILES]), sb("dinv", [P, NODE_TILES]), sb("dinv2", [P, NODE_TILES])
    mean, rstd = sb("mean", [P, NODE_TILES]), sb("rstd", [P, NODE_TILES])
    mbias = sb("mbias", [P, NODE_TILES])
    valid = sb("valid", [P, 1])
    bn_col = sb("bn_col", [P, 8])
    bn_tmp = sb("bn_tmp", [P, P])
    diag_a, diag_c = sb("diag_a", [P, P]), sb("diag_c", [P, P])
    a_col, c_col = [sb(f"a_col{i}", [P, 1]) for i in range(3)], [sb(f"c_col{i}", [P, 1]) for i in range(3)]
    a_row, c_row = [sb(f"a_row{i}", [P, F]) for i in range(3)], [sb(f"c_row{i}", [P, F]) for i in range(3)]

    def four(name, shape, n, dt=f32):
        return [sb(f"{name}{s}", shape, dt) for s in range(n)] * (4 // n)

    xin = four("xin", [P, NT, F], 4)
    din = four("din", [P, NT, F], 4)
    ncol = four("ncol", [P, 5, NT], 4)
    nst, nmv = sb("nst", [P, NT, 6]), sb("nmv", [P, NT, 2])
    nstd, nrs, nbias = sb("nstd", [P, NT]), four("nrs", [P, NT], 2), four("nbias", [P, NT], 2)
    zb = four("z", [P, NT, F], 4)
    zT = four("zT", [P, NT * F], 2)
    yout = four("yout", [P, NT, W1C], 4)
    hbuf = four("hbuf", [P, NT, F + 1], 2)
    aT = four("aT", [P, NT * F], 2)
    aT_high, aT_low, zT_high, zT_low = (four(n, [P, NT * F], 2, f32r) for n in ("aT_high", "aT_low", "zT_high", "zT_low"))
    zeros = aT[0]
    rn = [sb(f"rn{g}", [P, 4 * P]) for g in range(2)]
    hmn = [sb(f"hmn{g}", [P, 4 * P]) for g in range(2)]
    upd = four("upd", [P, 2, 4 * P], 2)

    grow, srow = four("grow", [P, ET], 4, u32), four("srow", [P, ET], 2, u32)
    msg = [b[:, 0:ET, :] for b in zb]
    sel = [b[:, ET:2 * ET, :] for b in zb]
    msgw = [b[:, 0:ET, :] for b in yout]
    segT = [b[:, 0:ET * P] for b in zT]
    act_in = [b[:, ET * P:2 * ET * P] for b in zT]
    ecol = four("ecol", [P, 3, ET], 4)
    est, emv = sb("est", [P, ET, 6]), sb("emv", [P, ET, 2])
    estd, ers, eww = sb("estd", [P, ET]), sb("ers", [P, ET]), sb("eww", [P, ET])
    onehot = four("onehot", [P, ET, NTYPES], 2)
    first = [hmn[0], hmn[1], rn[0], rn[1]]
    cnt = four("cnt", [NTYPES, ET * P], 2)
    res = four("res", [P, ET, F], 2)
    oh_lo, oh_hi = four("oh_lo", [P, ET, P], 2, bf16), four("oh_hi", [P, ET, NODE_TILES], 2, bf16)
    high, low, last_low = four("high", [P, ET], 2), four("low", [P, ET], 2), four("last_low", [P, 1], 2)

    bank = [nc.alloc_psum_tensor(f"bank{i}", [P, 512], f32) for i in range(8)]
    seg_ps, out_ps = bank[0:2] * 2, bank[2:4] * 2
    cnt_ps, msg_ps = bank[4], bank[5]
    tp_ps, y_ps, gram_ps = bank[0:2], bank[2:4], bank[7]
    deg_ps = bank[6]
    zT_ps, aT_ps, back_ps = bank[0], bank[2], [bank[3], bank[1]]
    r_ps, hn_ps, in_ps, u_ps = bank[4:8]

    D = DENSE
    loaded = Slots(nc, "loaded", {p: 1 for p in ["E0"] + D}, 4)
    agg_in = Slots(nc, "agg_in", {p: 1 for p in D}, 4)
    stored = Slots(nc, "stored", {p: 1 for p in D}, 4)
    gathered = Slots(nc, "gathered", {p: ET for p in EDGE}, 4)
    scattered = Slots(nc, "scattered", {p: ET for p in EDGE}, 2)
    drow_in = Slots(nc, "drow_in", {p: 1 for p in EDGE}, 4)
    idx_ok, srow_ok = (Stage(nc, n, {p: 1 for p in EDGE}) for n in ("idx_ok", "srow_ok"))
    cols_ok = Stage(nc, "cols_ok", {p: 3 for p in EDGE})
    estats = Stage(nc, "estats", {p: ET for p in LN_EDGE})
    emoments = Stage(nc, "emoments", {p: ET for p in LN_EDGE})
    ers_ok = Stage(nc, "ers_ok", {p: 1 for p in LN_EDGE})
    eww_ok = Stage(nc, "eww_ok", {p: 1 for p in EDGE})
    centred = Stage(nc, "centred", {p: ET for p in LN_EDGE})
    scaled = Stage(nc, "scaled", {"E1": ET, "E2": 1, "E4": ET})
    msg_ok = Stage(nc, "msg_ok", {"E1": 1, "E2": 1})
    sel_ok = Stage(nc, "sel_ok", {p: ET for p in EDGE})
    onehot_ok = Stage(nc, "onehot_ok", {"E4": ET})
    mask_ok = Stage(nc, "mask_ok", {p: 1 for p in EDGE})
    seg_ok = Stage(nc, "seg_ok", {p: ET for p in EDGE})
    res_ok = Stage(nc, "res_ok", {p: 1 for p in EDGE})
    high_ok, low_ok = Stage(nc, "high_ok", {"D0": 2}), Stage(nc, "low_ok", {"D0": 1})
    hi_ok, lo_ok = Stage(nc, "hi_ok", {"D0": ET + 1}), Stage(nc, "lo_ok", {"D0": 1})
    apart_ok = Stage(nc, "apart_ok", {"D0": ET - 1})
    estd_ok = Stage(nc, "estd_ok", {p: 1 for p in LN_EDGE})
    act_ok = Stage(nc, "act_ok", {"E3": 1, "E4": 2})
    seg_done = Stage(nc, "seg_done", {p: 1 for p in EDGE})
    msg_done = Stage(nc, "msg_done", {"E4": 1})
    out_done = Stage(nc, "out_done", {p: 1 for p in EDGE})
    deg_done = Stage(nc, "deg_done", {"D0": 1})
    ST = ["E0", "A1", "A6", "A7"]
    MEAN, RSTD, AGG, SELF, BIAS = range(5)
    COLUMNS = {"A1": ((MEAN, mean), (RSTD, rstd), (BIAS, mbias), (AGG, rdeg), (SELF, dinv)),
               "A3": ((MEAN, mean), (RSTD, rstd), (BIAS, mbias), (AGG, dinv), (SELF, dinv2)),
               "A5": ((AGG, dinv), (SELF, dinv2)), "A6": ((RSTD, rstd), (BIAS, mbias)),
               "A7": (), "A8": ((RSTD, rstd), (BIAS, mbias))}
    ncols_ok = Stage(nc, "ncols_ok", {p: len(COLUMNS[p]) for p in D})
    z_ok = Stage(nc, "z_ok", {"A1": NT // 2, "A3": NT // 2, "A6": NT, "A8": NT})
    z2_ok = Stage(nc, "z2_ok", {"A1": NT // 2, "A3": NT // 2})
    agg_ok = Stage(nc, "agg_ok", {"A1": 1, "A3": 2, "A5": 2, "A6": 2, "A7": 1})
    tp_done = Stage(nc, "tp_done", {"A1": 2, "A3": 2, "A5": 2, "A8": 4})
    zT_raw = Stage(nc, "zT_raw", {"A3": 2})
    zT_ok = Stage(nc, "zT_ok", {"A1": 2, "A3": 2, "A5": 2, "A8": 4})
    y_done = Stage(nc, "y_done", {"A1": 2, "A3": 2, "A5": 2, "A6": 2, "A8": NT})
    y_raw = Stage(nc, "y_raw", {"A3": NT, "A5": NT, "A6": 1})
    y_ok = Stage(nc, "y_ok", {"A1": 2, "A3": 1, "A5": 1, "A6": 2, "A7": 1, "A8": 2})
    gelu_ok = Stage(nc, "gelu_ok", {"A7": 1})
    nstats = Stage(nc, "nstats", {p: NT for p in ST})
    nmoments = Stage(nc, "nmoments", {p: NT for p in ST})
    kept = Stage(nc, "kept", {p: 2 for p in ST})
    nstd_ok = Stage(nc, "nstd_ok", {"A1": 1})
    nrs_ok = Stage(nc, "nrs_ok", {"A1": 1})
    nbias_ok = Stage(nc, "nbias_ok", {"A1": 1})
    h_ok = Stage(nc, "h_ok", {"A1": NT})
    gram_done = Stage(nc, "gram_done", {"A1": 1, "A3": 1, "A5": 1})
    gate_ok = Stage(nc, "gate_ok", {"A8": 4})
    hn_ok = Stage(nc, "hn_ok", {"A8": 2})
    nin_ok = Stage(nc, "nin_ok", {"A8": 2})
    tanh_ok = Stage(nc, "tanh_ok", {"A8": 2})
    hmn_ok = Stage(nc, "hmn_ok", {"A8": 2})
    zhn_ok = Stage(nc, "zhn_ok", {"A8": 2})
    nzh_ok = Stage(nc, "nzh_ok", {"A8": 2})
    back_done = Stage(nc, "back_done", {"A8": 2})
    high_part, low_part = Stage(nc, "high_part", {"A8": 4}), Stage(nc, "low_part", {"A8": 4})
    mom, mom_std = sem("mom"), sem("mom_std")
    consts, weights_in, edges_in = sem("consts"), sem("weights_in"), sem("edges_in")
    filled, prep, ready, degs = sem("filled"), sem("prep"), sem("ready"), sem("degs")
    coef_end, ones_ok = sem("coef_end"), sem("ones_ok")
    coef, coef_std, coef_rows, coef_ready, passed = (sem("coef"), sem("coef_std"), sem("coef_rows"),
                                                     sem("coef_ready"), sem("passed"))
    READY = 1
    W_DMAS, E_DMAS = 8 + 2 + 1 + 3, 6
    MOM_OF = {"E0": 0, "A6": 1, "A7": 2}
    WEIGHT_LAG = {"E0": 3, "E1": 3, "E2": 3, "E3": 4, "E4": 4}
    COEF_OF = {"A1": 0, "A3": 1, "A5": 2}
    SRC = {"E0": x, "E1": x1_d, "E2": t1_d, "E3": x2_d, "E4": x3_d}
    XIN = {"A1": x, "A3": x1_d, "A5": t1_d, "A6": x1_d, "A7": x2_d, "A8": x3_d}
    DIN = {"A1": agg_d, "A3": agg_d, "A5": agg_d, "A6": t2_d, "A7": agg_d, "A8": agg_d}
    OUT = {"A1": x1_d, "A3": t1_d, "A5": t2_d, "A6": x2_d, "A7": x3_d, "A8": out}
    EW = {"E0": wb, "E1": w1, "E2": w2, "E3": wl2}
    NW = {"A1": wa, "A3": w1, "A5": w2}

    def held(eng, semaphore, value):
        eng.wait_ge(semaphore, value)
        eng.sem_inc(passed, 1)

    def gate(eng, phase):
        if PHASES.index(phase) <= 1:
            return
        last = PHASES[PHASES.index(phase) - 1]
        landed = scattered if last in EDGE else stored
        for s in range(landed.n):
            held(eng, landed.sems[s], landed.end(last, s))
        if last in COEF_OF:
            held(eng, coef_ready, COEF_OF[last] + 1)

    with nc.Block() as block:

        @block.sync
        def _(sp):
            for a, b in ((gidx, gidx_d), (dst_i, dst_d), (nxt_i, nxt_d), (typ_i, typ_d), (wgt, wgt_d)):
                sp.dma_start(a[:], b).then_inc(edges_in, 16)
            sp.dma_start(vec[:], vecs).then_inc(edges_in, 16)
            for a, b in ((wa, WaT), (wb, WbT), (w1, W1), (w2, W2), (wl2, WL2T), (wm, WmT), (wih, WihT), (whh, WhhT)):
                sp.dma_start(a[:], b).then_inc(weights_in, 16)
            sp.dma_start(emb_sb[:], emb).then_inc(weights_in, 16)
            sp.dma_start(bmsg_sb[:], rows[3:4, :].to_broadcast([NTYPES, F])).then_inc(weights_in, 16)
            sp.dma_start(gb[:], gate_biases).then_inc(weights_in, 16)
            for i in range(3):
                sp.dma_start(row[:, i, :], rows[i:i + 1, :].to_broadcast([P, F])).then_inc(weights_in, 16)

            sp.wait_ge(prep, 1)
            av = node_view(agg_d)
            zv = zeros[:].rearrange("p (k f) -> p k f", k=NT)
            with sp.Fori(0, STEPS) as c:
                sp.dma_start(av[c], zv).then_inc(filled, 16)

            def transfers(ph):
                AHEAD = ph in DENSE and PHASES[PHASES.index(ph) - 1] in EDGE
                src = node_view(XIN[ph] if ph in DENSE else x)[:, :, :, 0:F]
                if ph in DENSE:
                    other, ov = node_view(DIN[ph]), node_view(OUT[ph])

                def prefetch():
                    if ph == "A1":
                        held(sp, nstats.sem, nstats.end("E0"))
                    for s in range(4):
                        sp.dma_start(xin[s][:], src[s]).then_inc(loaded.sems[s], 16)

                def load(c, q, s):
                    if not early(c, 4):
                        if ph == "E0":
                            held(sp, nstats.sem, nstats.at(ph, c - 4))
                        else:
                            held(sp, y_ok.sem, y_ok.at(ph, c - 4))
                    if not (AHEAD and early(c, 4)):
                        sp.dma_start(xin[s][:], src[c]).then_inc(loaded.sems[s], 16)
                    if ph != "E0":
                        sp.dma_start(din[s][:], other[c]).then_inc(agg_in.sems[s], 16)

                def destinations(c, q, s):
                    if not early(c, 4):
                        held(sp, sel_ok.sem, sel_ok.at(ph, c - 4))
                        held(sp, mask_ok.sem, mask_ok.at(ph, c - 4))
                    sp.dma_start(drow[s][:], dstrow_d[0:1, bass.ds(c * (ET * P), 1 + ET * P)].to_broadcast([P, 1 + ET * P]))\
                        .then_inc(drow_in.sems[s], 16)

                def store(c, q, s):
                    held(sp, y_ok.sem, y_ok.at(ph, c))
                    width = W1C if ph == "A1" else F
                    sp.dma_start(ov[c], yout[s][:, :, 0:width]).then_inc(stored.sems[s], 16)

                if AHEAD:
                    prefetch()
                gate(sp, ph)
                if ph == "E0":
                    steps(sp, (0, destinations), (1, load))
                elif ph in EDGE:
                    steps(sp, (0, destinations))
                elif ph == "A8":
                    steps(sp, (0, load), (4, store))
                else:
                    steps(sp, (0, load), (3, store))

            for ph in PHASES[1:]:
                transfers(ph)
            for s in range(4):
                sp.wait_ge(stored.sems[s], stored.end("A8", s))

        @block.gpsimd
        def _(pool):
            nc.gpsimd.memset(ident[:], 0.0).then_inc(consts, 1)
            nc.gpsimd.memset(ones[:], 1.0).then_inc(consts, 1)
            nc.gpsimd.iota(iota_lo[:], [[1, P]], base=0, channel_multiplier=0,
                           allow_small_or_imprecise_dtypes=True).then_inc(consts, 1)
            nc.gpsimd.iota(iota_hi[:], [[1, NODE_TILES]], base=0, channel_multiplier=0,
                           allow_small_or_imprecise_dtypes=True).then_inc(consts, 1)
            nc.gpsimd.memset(valid[:], 1.0).then_inc(consts, 1)
            pool.wait_ge(consts, 5)
            nc.gpsimd.affine_select(out=ident[:], in_=ident[:], compare_op=ALU.not_equal, fill=1.0, base=0,
                                    pattern=[[-1, P]], channel_multiplier=1).then_inc(consts, 1)
            nc.gpsimd.affine_select(out=valid[:], in_=valid[:], compare_op=ALU.is_gt, fill=0.0, base=LAST_ROWS,
                                    pattern=[[0, 1]], channel_multiplier=-1).then_inc(consts, 1)

            def edge(ph):
                table = SRC[ph]

                def gather_numbers(c, q, s):
                    if not early(c, 4):
                        held(pool, gathered.sems[s], gathered.at(ph, q, s, 4))
                    nc.gpsimd.tensor_copy(grow[s][:], gidx[:, bass.ds(c * ET, ET)]).then_inc(idx_ok.sem, 1)

                def gather(c, q, s):
                    if not early(c, 4):
                        held(pool, seg_done.sem, seg_done.at(ph, c - 4))
                    held(pool, idx_ok.sem, idx_ok.at(ph, c))
                    for k in range(ET):
                        to = msgw[s][:, k, :] if ph == "E1" else msg[s][:, k, :]
                        pool.indirect_dma_start(
                            out=to, out_offset=None, in_=table,
                            in_offset=bass.IndirectOffsetOnAxis(ap=grow[s][:, k:k + 1], axis=0),
                        ).then_inc(gathered.sems[s], 16)

                def scatter_numbers(c, q, s):
                    if not early(c, 2):
                        held(pool, scattered.sems[s], scattered.at(ph, q, s, 2))
                    nc.gpsimd.tensor_copy(srow[s][:], scat[:, bass.ds(c * ET, ET)]).then_inc(srow_ok.sem, 1)

                def scatter(c, q, s):
                    held(pool, srow_ok.sem, srow_ok.at(ph, c))
                    held(pool, res_ok.sem, res_ok.at(ph, c))
                    if ph == "E0" and early(c, 1):
                        held(pool, filled, 16 * STEPS)
                    for k in range(ET):
                        pool.indirect_dma_start(
                            out=agg_d, out_offset=bass.IndirectOffsetOnAxis(ap=srow[s][:, k:k + 1], axis=0),
                            in_=res[s][:, k, :], in_offset=None, bounds_check=NPAD - 1, oob_is_err=False,
                        ).then_inc(scattered.sems[s], 16)

                lag = WEIGHT_LAG[ph] + 2
                steps(pool, (0, gather_numbers), (1, gather), (lag - 1, scatter_numbers), (lag, scatter))

            def dense(ph):
                def scale(c, q, s):
                    tile = din[s][:]
                    held(pool, agg_in.sems[s], agg_in.at(ph, q, s))
                    n = 0
                    if ph in ("A1", "A3", "A5"):
                        held(pool, ncols_ok.sem, ncols_ok.at(ph, c))
                    if ph != "A7":
                        factor = a_row[2][:, None, :] if ph == "A6" else ncol[s][:, AGG, :, None]
                        nc.gpsimd.tensor_tensor(tile, tile, factor.to_broadcast([P, NT, F]), mul).then_inc(agg_ok.sem, 1)
                        n = 1
                    if ph == "A1":
                        return
                    if n:
                        held(pool, agg_ok.sem, agg_ok.at(ph, c, n))
                    bias = c_row[2][:, None, :] if ph == "A6" else row[:, {"A3": 0, "A5": 1, "A7": 2}[ph], None, :]
                    nc.gpsimd.tensor_tensor(tile, tile, bias.to_broadcast([P, NT, F]), add).then_inc(agg_ok.sem, 1)

                if ph == "A8":
                    def low_parts(c, q, s, g):
                        cols = slice(g * 4 * P, (g + 1) * 4 * P)
                        for i, (low, full, high) in enumerate(((zT_low, zT, zT_high), (aT_low, aT, aT_high))):
                            held(pool, high_part.sem, high_part.at(ph, c, 2 * g + i + 1))
                            nc.gpsimd.tensor_tensor(low[s][:, cols], full[s][:, cols], high[s][:, cols].bitcast(f32), sub)\
                                .then_inc(low_part.sem, 1)

                    steps(pool, (3, lambda c, q, s: low_parts(c, q, s, 1)), (2, lambda c, q, s: low_parts(c, q, s, 0)))
                    return
                steps(pool, (1 if ph in ("A1", "A3", "A5") else 0, scale))

            held(pool, ready, READY)
            for ph in PHASES[1:]:
                gate(pool, ph)
                if ph in EDGE:
                    edge(ph)
                else:
                    dense(ph)

        @block.scalar
        def _(act):
            def low_columns(c, q, s):
                if not early(c, 2):
                    act.wait_ge(apart_ok.sem, apart_ok.at("D0", c - 2))
                nc.scalar.mul(low[s][:], lo_f[:, bass.ds(c * ET, ET)], -1.0).then_inc(low_ok.sem, 1)

            def low_distance(c, q, s):
                act.wait_ge(low_ok.sem, low_ok.at("D0", c))
                if not early(c, 2):
                    act.wait_ge(lo_ok.sem, lo_ok.at("D0", c - 2))
                for k in range(ET - 1):
                    nc.scalar.activation(upd[s][:, 0, k * P:(k + 1) * P], iota_lo[:], ACT.Abs, bias=low[s][:, k:k + 1])\
                        .then_inc(apart_ok.sem, 1)

            def low_digits(c, q, s):
                act.wait_ge(apart_ok.sem, apart_ok.at("D0", c))
                if not early(c, 2):
                    act.wait_ge(deg_done.sem, deg_done.at("D0", c - 2))
                nc.scalar.activation(oh_lo[s][:, 0:ET - 1, :].rearrange("p k f -> p (k f)"),
                                     upd[s][:, 0, 0:(ET - 1) * P], ACT.Relu,
                                     bias=ones[:, 0:1], scale=-1.0).then_inc(lo_ok.sem, 1)

            act.wait_ge(consts, 7)
            act.wait_ge(ready, READY)
            steps(act, (2, low_digits), (1, low_distance), (0, low_columns))

            def root(dst, src):
                return nc.scalar.activation(dst, src, ACT.Sqrt, bias=eps_col[:])

            def edge(ph):
                def std(c, q, s):
                    act.wait_ge(emoments.sem, emoments.at(ph, c))
                    root(estd[:], emv[:, :, 1]).then_inc(estd_ok.sem, 1)

                def middle(c, q, s):
                    if ph == "E3":
                        act.wait_ge(seg_ok.sem, seg_ok.at(ph, c))
                        if not early(c, 2):
                            act.wait_ge(out_done.sem, out_done.at(ph, c - 2))
                        nc.scalar.activation(act_in[s], segT[s], ACT.Gelu_apprx_tanh).then_inc(act_ok.sem, 1)
                    else:
                        act.wait_ge(seg_done.sem, seg_done.at(ph, c))
                        if not early(c, 2):
                            act.wait_ge(msg_done.sem, msg_done.at(ph, c - 2))
                        nc.scalar.copy(act_in[s], seg_ps[s][:]).then_inc(act_ok.sem, 1)
                        nc.scalar.copy(cnt[s][:], cnt_ps[0:NTYPES, :]).then_inc(act_ok.sem, 1)

                def result(c, q, s):
                    if not early(c, 2):
                        act.wait_ge(scattered.sems[s], scattered.at(ph, q, s, 2))
                    act.wait_ge(out_done.sem, out_done.at(ph, c))
                    nc.scalar.copy(res[s][:].rearrange("p k f -> p (k f)"), out_ps[s][:]).then_inc(res_ok.sem, 1)

                stages = []
                if ph in ("E3", "E4"):
                    stages.append((3 if ph == "E3" else 2, middle))
                stages.append((WEIGHT_LAG[ph], result))
                if ph in LN_EDGE:
                    stages.append((0, std))
                steps(act, *stages)

            def dense(ph):
                def rows(c, q, s, tiles=range(NT)):
                    act.wait_ge(loaded.sems[s], loaded.at(ph, q, s))
                    act.wait_ge(ncols_ok.sem, ncols_ok.at(ph, c))
                    if not early(c, 4):
                        last = y_ok if ph == "A6" else tp_done
                        act.wait_ge(last.sem, last.at(ph, c - 4))
                    ready_to = z2_ok if ph in ("A1", "A3") else z_ok
                    for k in tiles:
                        nc.scalar.activation(zb[s][:, k, :], xin[s][:, k, :], ACT.Relu, bias=ncol[s][:, 4, k:k + 1],
                                             scale=ncol[s][:, 1, k:k + 1]).then_inc(ready_to.sem, 1)

                def transposed(c, q, s):
                    if not early(c, 2):
                        act.wait_ge(y_done.sem, y_done.at(ph, c - 2))
                    for g in range(2):
                        cols = slice(g * 4 * F, (g + 1) * 4 * F)
                        act.wait_ge(tp_done.sem, tp_done.at(ph, c, g + 1))
                        if ph == "A5":
                            nc.scalar.activation(zT[s][:, cols], tp_ps[g][:], ACT.Identity, bias=c_col[1][:],
                                                 scale=a_col[1][:]).then_inc(zT_ok.sem, 1)
                        else:
                            ready_to = zT_raw if ph == "A3" else zT_ok
                            nc.scalar.activation(zT[s][:, cols], tp_ps[g][:], ACT.Relu).then_inc(ready_to.sem, 1)
                    if ph == "A3":
                        for g in range(2):
                            cols = slice(g * 4 * F, (g + 1) * 4 * F)
                            act.wait_ge(zT_raw.sem, zT_raw.at(ph, c, g + 1))
                            nc.scalar.activation(zT[s][:, cols], zT[s][:, cols], ACT.Identity, bias=c_col[0][:],
                                                 scale=a_col[0][:]).then_inc(zT_ok.sem, 1)

                def gelu(c, q, s):
                    act.wait_ge(agg_ok.sem, agg_ok.at(ph, c))
                    if not early(c, 4):
                        act.wait_ge(y_ok.sem, y_ok.at(ph, c - 4))
                    nc.scalar.activation(zb[s][:], din[s][:], ACT.Gelu_apprx_tanh).then_inc(gelu_ok.sem, 1)

                def std(c, q, s):
                    act.wait_ge(nmoments.sem, nmoments.at(ph, c))
                    root(nstd[:], nmv[:, :, 1]).then_inc(nstd_ok.sem, 1)

                def norm(c, q, s):
                    act.wait_ge(nbias_ok.sem, nbias_ok.at(ph, c))
                    if not early(c, 2):
                        act.wait_ge(gram_done.sem, gram_done.at(ph, c - 2))
                    for k in range(NT):
                        nc.scalar.activation(hbuf[s][:, k, 0:F], yout[s][:, k, 0:F], ACT.Relu,
                                             bias=nbias[s][:, k:k + 1], scale=nrs[s][:, k:k + 1]).then_inc(h_ok.sem, 1)

                def gates(c, q, s, g):
                    if not early(c, 1):
                        act.wait_ge(nzh_ok.sem, nzh_ok.at(ph, c - 1, g + 1))
                    act.wait_ge(y_done.sem, y_done.at(ph, c, 4 * g + 1))
                    nc.scalar.activation(rn[g][:], r_ps[:], ACT.Sigmoid, bias=gb[:, 0:1]).then_inc(gate_ok.sem, 1)
                    if not early(c, 2):
                        act.wait_ge(back_done.sem, back_done.at(ph, c - 2, g + 1))
                    act.wait_ge(y_done.sem, y_done.at(ph, c, 4 * g + 4))
                    nc.scalar.activation(upd[s][:, g, :], u_ps[:], ACT.Sigmoid, bias=gb[:, 1:2]).then_inc(gate_ok.sem, 1)

                def new(c, q, s, g):
                    act.wait_ge(nin_ok.sem, nin_ok.at(ph, c, g + 1))
                    nc.scalar.activation(rn[g][:], rn[g][:], ACT.Tanh, bias=gb[:, 2:3]).then_inc(tanh_ok.sem, 1)

                def turned(c, q, s, g):
                    if not early(c, 2):
                        act.wait_ge(hmn_ok.sem, hmn_ok.at(ph, c - 2, g + 1))
                        act.wait_ge(y_done.sem, y_done.at(ph, c - 2, 4 * g + 4))
                    cols = slice(g * 4 * P, (g + 1) * 4 * P)
                    act.wait_ge(tp_done.sem, tp_done.at(ph, c, 2 * g + 1))
                    nc.scalar.copy(zT[s][:, cols], zT_ps[:]).then_inc(zT_ok.sem, 1)
                    act.wait_ge(tp_done.sem, tp_done.at(ph, c, 2 * g + 2))
                    nc.scalar.copy(aT[s][:, cols], aT_ps[:]).then_inc(zT_ok.sem, 1)

                def half(body, g):
                    return lambda c, q, s: body(c, q, s, g)

                def rows_half(g):
                    return lambda c, q, s: rows(c, q, s, range(4 * g, 4 * g + 4))

                if ph == "A1":
                    steps(act, (4, std), (2, transposed), (1, rows_half(1)), (4, norm))
                elif ph == "A3":
                    steps(act, (2, transposed), (1, rows_half(1)))
                elif ph == "A5":
                    steps(act, (2, transposed))
                elif ph == "A6":
                    steps(act, (1, rows))
                elif ph == "A7":
                    steps(act, (1, gelu))
                else:
                    steps(act, (3, half(gates, 0)), (1, rows_half(0)), (2, half(turned, 0)), (3, half(new, 0)),
                          (3, half(gates, 1)), (1, rows_half(1)), (2, half(turned, 1)), (3, half(new, 1)))

            act.wait_ge(weights_in, 16 * W_DMAS)
            for ph in PHASES[1:]:
                gate(act, ph)
                if ph in EDGE:
                    edge(ph)
                    if ph == "E0":
                        act.wait_ge(degs, 2)
                        nc.scalar.activation(sqd[:], sqd[:], ACT.Sqrt).then_inc(degs, 1)
                else:
                    dense(ph)
                if ph in MOM_OF:
                    act.wait_ge(mom, 3 * MOM_OF[ph] + 1)
                    root(rstd[:], rstd[:]).then_inc(mom_std, 1)
                if ph in COEF_OF:
                    i = COEF_OF[ph]
                    act.wait_ge(coef, 9 * i + 5)
                    root(bn_col[:, 4:5], bn_col[:, 3:4]).then_inc(coef_std, 1)

        @block.tensor
        def _(pe):
            pe.wait_ge(consts, 7)
            pe.wait_ge(weights_in, 16 * W_DMAS)

            def edge(ph):
                def message(c, q, s):
                    pe.wait_ge(act_ok.sem, act_ok.at(ph, c))
                    if not early(c, 1):
                        pe.wait_ge(seg_ok.sem, seg_ok.at(ph, c - 1))
                    nc.tensor.matmul(msg_ps[:], wm[:], act_in[s], start=True, stop=False)
                    nc.tensor.matmul(msg_ps[:], emb_sb[:], cnt[s][:], start=False, stop=True).then_inc(msg_done.sem, 1)

                def sums(c, q, s):
                    start = early(c, 1)
                    pe.wait_ge(sel_ok.sem, sel_ok.at(ph, c))
                    if ph in ("E1", "E2"):
                        pe.wait_ge(msg_ok.sem, msg_ok.at(ph, c))
                    elif ph == "E4":
                        pe.wait_ge(scaled.sem, scaled.at(ph, c))
                        pe.wait_ge(onehot_ok.sem, onehot_ok.at(ph, c))
                        if not start:
                            pe.wait_ge(act_ok.sem, act_ok.at(ph, c - 1))
                    else:
                        pe.wait_ge(centred.sem, centred.at(ph, c))
                    if not early(c, 2):
                        if ph == "E4":
                            pe.wait_ge(act_ok.sem, act_ok.at(ph, c - 2))
                        else:
                            pe.wait_ge(seg_ok.sem, seg_ok.at(ph, c - 2))
                    if ph == "E4":
                        for k in range(ET):
                            nc.tensor.matmul(cnt_ps[0:NTYPES, k * P:(k + 1) * P], onehot[s][:, k, :], sel[s][:, k, :],
                                             start=True, stop=True)
                    for k in range(ET):
                        last = nc.tensor.matmul(seg_ps[s][:, k * P:(k + 1) * P], msg[s][:, k, :], sel[s][:, k, :],
                                                start=True, stop=True)
                    last.then_inc(seg_done.sem, 1)
                def weight(c, q, s):
                    if ph == "E3":
                        pe.wait_ge(act_ok.sem, act_ok.at(ph, c))
                    else:
                        pe.wait_ge(seg_ok.sem, seg_ok.at(ph, c))
                    if not early(c, 2):
                        pe.wait_ge(res_ok.sem, res_ok.at(ph, c - 2))
                    src = (act_in if ph == "E3" else segT)[s]
                    for k in range(ET):
                        o, i = out_ps[s][:, k * F:(k + 1) * F], src[:, k * P:(k + 1) * P]
                        last = nc.tensor.transpose(o, i, ident[:]) if ph == "E4" else \
                            nc.tensor.matmul(o, i, EW[ph][:], start=True, stop=True)
                    last.then_inc(out_done.sem, 1)

                if ph == "E4":
                    steps(pe, (3, message), (4, weight), (1, sums))
                else:
                    steps(pe, (WEIGHT_LAG[ph], weight), (1, sums))

            def dense(ph):
                def transposes(c, q, s):
                    for g in range(2):
                        if ph == "A5":
                            pe.wait_ge(loaded.sems[s], loaded.at(ph, q, s))
                        else:
                            normed = z2_ok if g else z_ok
                            pe.wait_ge(normed.sem, normed.at(ph, c))
                        if not early(c, 1):
                            pe.wait_ge((zT_raw if ph == "A3" else zT_ok).sem,
                                       (zT_raw if ph == "A3" else zT_ok).at(ph, c - 1, g + 1))
                        for k in range(4 * g, 4 * g + 4):
                            src = xin[s] if ph == "A5" else zb[s]
                            last = nc.tensor.transpose(tp_ps[g][:, k % 4 * P:(k % 4 + 1) * P], src[:, k, :], ident[:])
                        last.then_inc(tp_done.sem, 1)

                def products(c, q, s):
                    for g in range(2):
                        pe.wait_ge(zT_ok.sem, zT_ok.at(ph, c, g + 1))
                        if ph == "A1":
                            pe.wait_ge(agg_ok.sem, agg_ok.at(ph, c))
                        if not early(c, 1):
                            if ph == "A1":
                                pe.wait_ge(y_ok.sem, y_ok.at(ph, c - 1, g + 1))
                            else:
                                pe.wait_ge(y_raw.sem, y_raw.at(ph, c - 1, 4 * g + 4))
                        for k in range(4 * g, 4 * g + 4):
                            o = y_ps[g][:, k % 4 * F:(k % 4 + 1) * F]
                            last = nc.tensor.matmul(o, zT[s][:, k * P:(k + 1) * P], NW[ph][:], start=True,
                                                    stop=ph != "A1")
                            if ph == "A1":
                                last = nc.tensor.matmul(o, ident[:], din[s][:, k, :], start=False, stop=True)
                        last.then_inc(y_done.sem, 1)

                def turn(c, q, s, g):
                    for i, (ps, rows) in enumerate(((zT_ps, zb[s]), (aT_ps, din[s]))):
                        if i == 0:
                            pe.wait_ge(z_ok.sem, z_ok.at(ph, c, 4 * g + 4))
                        else:
                            pe.wait_ge(agg_in.sems[s], agg_in.at(ph, q, s))
                        if g:
                            pe.wait_ge(zT_ok.sem, zT_ok.at(ph, c, i + 1))
                        elif not early(c, 1):
                            pe.wait_ge(zT_ok.sem, zT_ok.at(ph, c - 1, i + 3))
                        for k in range(4):
                            last = nc.tensor.transpose(ps[:, k * P:(k + 1) * P], rows[:, 4 * g + k, :], ident[:])
                        last.then_inc(tp_done.sem, 1)

                def gate_products(c, q, s, g):
                    pe.wait_ge(low_part.sem, low_part.at(ph, c, 2 * g + 2))
                    cols = slice(g * 4 * P, (g + 1) * 4 * P)
                    h, a = (zT_high[s][:, cols], zT_low[s][:, cols]), (aT_high[s][:, cols], aT_low[s][:, cols])
                    wh, wi = (whh_high, whh_low), (wih_high, wih_low)
                    for ps, parts, reader, k in (
                            (r_ps, ((wh, h, 0), (wi, a, 0)), gate_ok, 1), (hn_ps, ((wh, h, 2),), hn_ok, 1),
                            (in_ps, ((wi, a, 2),), nin_ok, 1), (u_ps, ((wh, h, 1), (wi, a, 1)), gate_ok, 2)):
                        per = reader.per[ph] // 2
                        if g:
                            pe.wait_ge(reader.sem, reader.at(ph, c, k))
                        elif not early(c, 1):
                            pe.wait_ge(reader.sem, reader.at(ph, c - 1, per + k))
                        passes = [(w[u][:, i * F:(i + 1) * F], m[v_]) for w, m, i in parts
                                  for u, v_ in ((0, 0), (0, 1), (1, 0))]
                        for j, (w, m) in enumerate(passes):
                            last = nc.tensor.matmul(ps[:], w, m, start=j == 0,
                                                    stop=j == len(passes) - 1)
                        last.then_inc(y_done.sem, 1)

                def back(c, q, s, g):
                    pe.wait_ge(nzh_ok.sem, nzh_ok.at(ph, c, g + 1))
                    if not early(c, 1):
                        pe.wait_ge(y_ok.sem, y_ok.at(ph, c - 1, g + 1))
                    for k in range(4):
                        last = nc.tensor.transpose(back_ps[g][:, k * F:(k + 1) * F], upd[s][:, g, k * P:(k + 1) * P],
                                                   ident[:])
                    last.then_inc(back_done.sem, 1)

                def half(body, g):
                    return lambda c, q, s: body(c, q, s, g)

                def plus(c, q, s):
                    pe.wait_ge(loaded.sems[s], loaded.at(ph, q, s))
                    pe.wait_ge(agg_ok.sem, agg_ok.at(ph, c))
                    for g in range(2):
                        if not early(c, 1):
                            pe.wait_ge(y_ok.sem, y_ok.at(ph, c - 1, g + 1))
                        ks = slice(4 * g, 4 * g + 4)
                        nc.tensor.matmul(y_ps[g][:], ident[:], xin[s][:, ks, :], start=True, stop=False)
                        nc.tensor.matmul(y_ps[g][:], ident[:], din[s][:, ks, :], start=False, stop=True)\
                            .then_inc(y_done.sem, 1)

                def gram(c, q, s):
                    if ph == "A1":
                        pe.wait_ge(h_ok.sem, h_ok.at(ph, c))
                    else:
                        pe.wait_ge(y_ok.sem, y_ok.at(ph, c))
                    r = hbuf[s] if ph == "A1" else yout[s]
                    for k in range(NT):
                        last = nc.tensor.matmul(gram_ps[:, 0:F + 1], r[:, k, 0:F], r[:, k, 0:F + 1],
                                                start=early(c, 1) and k == 0, stop=False,
                                                skip_group_check=True)
                    last.then_inc(gram_done.sem, 1)

                if ph == "A8":
                    steps(pe, (3, half(gate_products, 0)), (4, half(back, 0)), (2, half(turn, 0)), (4, half(back, 1)),
                          (3, half(gate_products, 1)), (2, half(turn, 1)))
                elif ph == "A6":
                    steps(pe, (1, plus))
                elif ph == "A1":
                    steps(pe, (3, products), (2, transposes), (5, gram))
                else:
                    steps(pe, (3, products), (2, transposes), (4, gram))

            def degrees(c, q, s):
                pe.wait_ge(lo_ok.sem, lo_ok.at("D0", c))
                pe.wait_ge(hi_ok.sem, hi_ok.at("D0", c))
                for k in range(ET):
                    last = nc.tensor.matmul(deg_ps[:, 0:NODE_TILES], oh_lo[s][:, k, :], oh_hi[s][:, k, :],
                                            start=early(c, 1) and k == 0, stop=False, skip_group_check=True)
                last.then_inc(deg_done.sem, 1)

            steps(pe, (0, degrees))
            for ph in PHASES[1:]:
                gate(pe, ph)
                if ph in EDGE:
                    edge(ph)
                elif ph != "A7":
                    dense(ph)
                if ph in COEF_OF:
                    pe.wait_ge(coef, 9 * COEF_OF[ph] + 9)
                    nc.tensor.matmul(bank[6][:, 0:F], ones[:], diag_a[:], start=True, stop=True)
                    nc.tensor.matmul(bank[6][:, F:2 * F], ones[:], diag_c[:], start=True, stop=True).then_inc(coef_rows, 1)

        @block.vector
        def _(dve):
            v = nc.vector
            v.memset(zeros[:], 0.0).then_inc(prep, 1)
            v.memset(zero_col[:], 0.0)
            v.memset(eps_col[:], EPS)
            v.memset(hbuf[0][:, :, F:F + 1], 1.0)
            v.memset(hbuf[1][:, :, F:F + 1], 1.0).then_inc(prep, 1)
            n = [2]

            def done(ins):
                ins.then_inc(prep, 1)
                n[0] += 1
                dve.wait_ge(prep, n[0])

            dve.wait_ge(edges_in, 16 * E_DMAS)
            done(v.tensor_copy(dst_f[:], dst_i[:]))
            done(v.tensor_copy(nxt_f[:], nxt_i[:]))
            done(v.tensor_tensor(nxt_f[:], nxt_f[:], dst_f[:], eq))
            done(v.scalar_tensor_tensor(nxt_f[:], nxt_f[:], 100000.0, dst_f[:], mul, add))
            done(v.tensor_copy(scat[:], nxt_f[:]))
            done(v.tensor_scalar(nxt_i[:], dst_i[:], 7, None, ALU.logical_shift_right))
            done(v.tensor_copy(hi_f[:], nxt_i[:]))
            done(v.tensor_scalar(nxt_i[:], dst_i[:], 127, None, ALU.bitwise_and))
            done(v.tensor_copy(lo_f[:], nxt_i[:]))
            done(v.tensor_copy(typ_f[:], typ_i[:]))
            done(v.tensor_scalar(typ_f[:], typ_f[:], 0.0, float(NTYPES - 1), mx, ALU.min))
            dve.wait_ge(consts, 7)
            dve.wait_ge(weights_in, 16 * W_DMAS)
            done(v.tensor_tensor(emb_sb[:], emb_sb[:], bmsg_sb[:], add))
            done(v.tensor_tensor(gb[:, 0:2], gb[:, 0:2], gb[:, 3:5], add))
            for w, upper, rest in ((wih, wih_high, wih_low), (whh, whh_high, whh_low)):
                done(v.tensor_copy(upper[:], w[:]))
                done(v.tensor_tensor(rest[:], w[:], upper[:].bitcast(f32), sub))
            dve.sem_inc(ready, READY)

            def row_stats(ph, c, s, ks):
                for k in ks:
                    rows = xin[s][:, k, :] if ph == "E0" else yout[s][:, k, 0:F]
                    v.bn_stats(nst[:, k, :], rows).then_inc(nstats.sem, 1)

            def row_moments(ph, c):
                held(dve, nstats.sem, nstats.at(ph, c))
                if not early(c, 1):
                    held(dve, kept.sem, kept.at(ph, c - 1))
                for k in range(NT):
                    v.bn_aggr(nmv[:, k, :], nst[:, k, :]).then_inc(nmoments.sem, 1)

            def keep(ph, c):
                held(dve, nmoments.sem, nmoments.at(ph, c))
                v.tensor_copy(mean[:, bass.ds(c * NT, NT)], nmv[:, :, 0]).then_inc(kept.sem, 1)
                v.tensor_copy(rstd[:, bass.ds(c * NT, NT)], nmv[:, :, 1]).then_inc(kept.sem, 1)

            def edge(ph):
                def columns(c, q, s):
                    if not early(c, 4):
                        held(dve, sel_ok.sem, sel_ok.at(ph, c - 4))
                    v.tensor_copy(ecol[s][:, 0, :], dst_f[:, bass.ds(c * ET, ET)]).then_inc(cols_ok.sem, 1)
                    v.tensor_copy(ecol[s][:, 1, :], (dinv_src if ph == "E2" else wgt)[:, bass.ds(c * ET, ET)])\
                        .then_inc(cols_ok.sem, 1)
                    v.tensor_copy(ecol[s][:, 2, :], typ_f[:, bass.ds(c * ET, ET)]).then_inc(cols_ok.sem, 1)

                def edge_stats(c, q, s, k):
                    raw = msgw[s] if ph == "E1" else msg[s]
                    if k == 0:
                        dve.wait_ge(gathered.sems[s], gathered.at(ph, q, s))
                    v.bn_stats(est[:, k, :], raw[:, k, 0:F]).then_inc(estats.sem, 1)

                def edge_moments(c, q, s):
                    held(dve, estats.sem, estats.at(ph, c))
                    for k in range(ET):
                        v.bn_aggr(emv[:, k, :], est[:, k, :]).then_inc(emoments.sem, 1)

                def front(c, q, s):
                    m = msg[s]
                    raw = msgw[s] if ph == "E1" else m
                    if ph not in LN_EDGE:
                        dve.wait_ge(gathered.sems[s], gathered.at(ph, q, s))
                    else:
                        dve.wait_ge(emoments.sem, emoments.at(ph, c))
                        if ph == "E1" and not early(c, 4):
                            dve.wait_ge(seg_done.sem, seg_done.at(ph, c - 4))
                        for k in range(ET):
                            v.tensor_scalar(m[:, k, :], raw[:, k, 0:F], emv[:, k, 0:1], 0.0, sub, mx)\
                                .then_inc(centred.sem, 1)
                        dve.wait_ge(estd_ok.sem, estd_ok.at(ph, c))
                        v.reciprocal(ers[:], estd[:]).then_inc(ers_ok.sem, 1)
                        dve.wait_ge(ers_ok.sem, ers_ok.at(ph, c))
                    held(dve, cols_ok.sem, cols_ok.at(ph, c))
                    held(dve, drow_in.sems[s], drow_in.at(ph, q, s))
                    if ph == "E0":
                        v.tensor_copy(eww[:], ers[:]).then_inc(eww_ok.sem, 1)
                    elif ph == "E1":
                        v.tensor_copy(eww[:], raw[:, :, F]).then_inc(eww_ok.sem, 1)
                        v.tensor_copy(dinv_src[:, bass.ds(c * ET, ET)], raw[:, :, F])
                    elif ph == "E2":
                        v.tensor_copy(eww[:], ecol[s][:, 1, :]).then_inc(eww_ok.sem, 1)
                    elif ph == "E3":
                        v.tensor_tensor(eww[:], ers[:], ecol[s][:, 1, :], mul).then_inc(eww_ok.sem, 1)
                    else:
                        v.memset(eww[:], 1.0).then_inc(eww_ok.sem, 1)
                    if ph == "E1":
                        dve.wait_ge(centred.sem, centred.at(ph, c))
                        for k in range(ET):
                            v.scalar_tensor_tensor(m[:, k, :], m[:, k, :], ers[:, k:k + 1], a_row[0][:], mul, mul)\
                                .then_inc(scaled.sem, 1)
                        dve.wait_ge(scaled.sem, scaled.at(ph, c))
                        v.tensor_tensor(m, m, c_row[0][:, None, :].to_broadcast([P, ET, F]), add)\
                            .then_inc(msg_ok.sem, 1)
                    elif ph == "E2":
                        v.tensor_tensor(m, m, a_row[1][:, None, :].to_broadcast([P, ET, F]), mul)\
                            .then_inc(scaled.sem, 1)
                        dve.wait_ge(scaled.sem, scaled.at(ph, c))
                        v.tensor_tensor(m, m, c_row[1][:, None, :].to_broadcast([P, ET, F]), add)\
                            .then_inc(msg_ok.sem, 1)
                    elif ph == "E4":
                        dve.wait_ge(centred.sem, centred.at(ph, c))
                        for k in range(ET):
                            v.tensor_scalar(m[:, k, :], m[:, k, :], ers[:, k:k + 1], None, mul).then_inc(scaled.sem, 1)
                        if not early(c, 2):
                            dve.wait_ge(seg_done.sem, seg_done.at(ph, c - 2))
                        for k in range(ET):
                            v.tensor_scalar(onehot[s][:, k, :], iota_lo[:, 0:NTYPES], ecol[s][:, 2, k:k + 1], None, eq)\
                                .then_inc(onehot_ok.sem, 1)
                    dve.wait_ge(eww_ok.sem, eww_ok.at(ph, c))
                    if not early(c, 4):
                        held(dve, seg_done.sem, seg_done.at(ph, c - 4))
                    for k in range(ET):
                        v.tensor_scalar(sel[s][:, k, :], drow[s][:, k * P + 1:k * P + 1 + P],
                                        ecol[s][:, 0, k:k + 1], eww[:, k:k + 1], eq, mul).then_inc(sel_ok.sem, 1)
                    if not early(c, 4):
                        held(dve, seg_ok.sem, seg_ok.at(ph, c - 4))
                    v.tensor_tensor(first[s][:].rearrange("p (k q) -> p k q", q=P),
                                    drow[s][:, 1:1 + ET * P].rearrange("p (k q) -> p k q", q=P),
                                    drow[s][:, 0:ET * P].rearrange("p (k q) -> p k q", q=P)[:, :, 0:1]
                                    .to_broadcast([P, ET, P]), eq).then_inc(mask_ok.sem, 1)

                def totals(c, q, s, k):
                    ps = msg_ps if ph == "E4" else seg_ps[s]
                    if k == 0:
                        done = msg_done if ph == "E4" else seg_done
                        dve.wait_ge(done.sem, done.at(ph, c))
                        held(dve, mask_ok.sem, mask_ok.at(ph, c))
                        if not early(c, 2):
                            held(dve, out_done.sem, out_done.at(ph, c - 2))
                    if k > 0:
                        carry = segT[s][:, k * P - 1:k * P]
                        held(dve, seg_ok.sem, seg_ok.at(ph, c, k))
                    elif early(c, 1):
                        carry = zero_col[:]
                    else:
                        carry = segT[(s + 3) % 4][:, ET * P - 1:ET * P]
                        held(dve, seg_ok.sem, seg_ok.at(ph, c - 1))
                    cols = slice(k * P, (k + 1) * P)
                    v.scalar_tensor_tensor(segT[s][:, cols], first[s][:, cols], carry, ps[:, cols], mul, add)\
                        .then_inc(seg_ok.sem, 1)

                def node_stats(c, q, s, k):
                    if k == 0:
                        dve.wait_ge(loaded.sems[s], loaded.at(ph, q, s))
                    row_stats(ph, c, s, (2 * k, 2 * k + 1))

                def of_tile(body, k):
                    return lambda c, q, s: body(c, q, s, k)

                stages = [(1, front), (0, columns)]
                for k in range(ET):
                    stages.append((3 if ph == "E4" else 2, of_tile(totals, k)))
                    if ph in LN_EDGE:
                        stages.append((0, of_tile(edge_stats, k)))
                    if ph == "E0":
                        stages.append((1, of_tile(node_stats, k)))
                if ph == "E0":
                    stages.append((2, lambda c, q, s: keep(ph, c)))
                if ph in LN_EDGE:
                    stages.append((0, edge_moments))
                if ph == "E0":
                    stages.append((1, lambda c, q, s: row_moments(ph, c)))
                steps(dve, *stages)

            def dense(ph):
                def columns(c, q, s):
                    if not early(c, 4):
                        last = z_ok if ph == "A8" else y_ok
                        held(dve, last.sem, last.at(ph, c - 4))
                    for i, a in COLUMNS[ph]:
                        v.tensor_copy(ncol[s][:, i, :], a[:, bass.ds(c * NT, NT)]).then_inc(ncols_ok.sem, 1)

                def front(c, q, s):
                    if ph in ("A1", "A3"):
                        held(dve, ncols_ok.sem, ncols_ok.at(ph, c))
                        dve.wait_ge(loaded.sems[s], loaded.at(ph, q, s))
                        if not early(c, 4):
                            held(dve, tp_done.sem, tp_done.at(ph, c - 4))
                        for k in range(NT // 2):
                            v.tensor_scalar(zb[s][:, k, :], xin[s][:, k, :], ncol[s][:, 0, k:k + 1],
                                            ncol[s][:, 1, k:k + 1], sub, mul).then_inc(z_ok.sem, 1)

                def back(c, q, s):
                    X, Dn, Y, z = xin[s], din[s], yout[s], zb[s]
                    if not early(c, 4):
                        held(dve, stored.sems[s], stored.at(ph, q, s, 4))
                        if ph in ("A3", "A5"):
                            held(dve, gram_done.sem, gram_done.at(ph, c - 4))
                        if ph == "A1":
                            held(dve, h_ok.sem, h_ok.at(ph, c - 4))
                    if ph == "A1":
                        v.tensor_copy(Y[:, :, F:W1C], ncol[s][:, 3, :, None].to_broadcast([P, NT, 4]))
                        for g in range(2):
                            ks = slice(4 * g, 4 * g + 4)
                            dve.wait_ge(y_done.sem, y_done.at(ph, c, g + 1))
                            v.scalar_tensor_tensor(Y[:, ks, 0:F], y_ps[g][:].rearrange("p (k f) -> p k f", f=F), 0.0,
                                                   X[:, ks, :], mx, add).then_inc(y_ok.sem, 1)
                    if ph in ("A3", "A5"):
                        held(dve, agg_ok.sem, agg_ok.at(ph, c))
                        for k in range(NT):
                            dve.wait_ge(y_done.sem, y_done.at(ph, c, k // 4 + 1))
                            v.scalar_tensor_tensor(Y[:, k, 0:F], y_ps[k // 4][:, k % 4 * F:(k % 4 + 1) * F],
                                                   ncol[s][:, SELF, k:k + 1], Dn[:, k, :], mul, add).then_inc(y_raw.sem, 1)
                    if ph == "A6":
                        dve.wait_ge(y_raw.sem, y_raw.at(ph, c))
                        for g in range(2):
                            ks = slice(4 * g, 4 * g + 4)
                            dve.wait_ge(y_done.sem, y_done.at(ph, c, g + 1))
                            v.tensor_tensor(Y[:, ks, 0:F], z[:, ks, :], y_ps[g][:].rearrange("p (k f) -> p k f", f=F),
                                            add).then_inc(y_ok.sem, 1)
                    if ph == "A7":
                        dve.wait_ge(gelu_ok.sem, gelu_ok.at(ph, c))
                        v.tensor_tensor(Y[:, :, 0:F], z[:], X[:], add).then_inc(y_ok.sem, 1)

                def relu(c, q, s):
                    Y = yout[s]
                    dve.wait_ge(y_raw.sem, y_raw.at(ph, c))
                    if isinstance(c, int) and c == STEPS - 1:
                        v.tensor_scalar(Y[:, 0:NT - 2, 0:F], Y[:, 0:NT - 2, 0:F], 0.0, None, mx)
                        v.tensor_scalar(Y[:, NT - 2, 0:F], Y[:, NT - 2, 0:F], 0.0, valid[:], mx, mul)
                        v.memset(Y[:, NT - 1, 0:F], 0.0).then_inc(y_ok.sem, 1)
                    else:
                        v.tensor_scalar(Y[:, :, 0:F], Y[:, :, 0:F], 0.0, None, mx).then_inc(y_ok.sem, 1)

                def weighted(c, q, s):
                    dve.wait_ge(z_ok.sem, z_ok.at(ph, c))
                    v.tensor_tensor(zb[s][:], zb[s][:], a_row[0][:, None, :].to_broadcast([P, NT, F]), mul)\
                        .then_inc(y_raw.sem, 1)

                def new_stats(c, q, s):
                    held(dve, y_ok.sem, y_ok.at(ph, c))
                    row_stats(ph, c, s, range(NT))

                def new_moments(c, q, s):
                    row_moments(ph, c)

                def candidate(c, q, s, g):
                    dve.wait_ge(gate_ok.sem, gate_ok.at(ph, c, 2 * g + 1))
                    dve.wait_ge(y_done.sem, y_done.at(ph, c, 4 * g + 2))
                    v.scalar_tensor_tensor(rn[g][:], hn_ps[:], gb[:, 5:6], rn[g][:], add, mul).then_inc(hn_ok.sem, 1)
                    dve.wait_ge(hn_ok.sem, hn_ok.at(ph, c, g + 1))
                    dve.wait_ge(y_done.sem, y_done.at(ph, c, 4 * g + 3))
                    v.tensor_tensor(rn[g][:], rn[g][:], in_ps[:], add).then_inc(nin_ok.sem, 1)

                def mix(c, q, s, g):
                    n, d, u = rn[g][:], hmn[g][:], upd[s][:, g, :]
                    dve.wait_ge(tanh_ok.sem, tanh_ok.at(ph, c, g + 1))
                    v.tensor_tensor(d, zT[s][:, g * 4 * P:(g + 1) * 4 * P], n, sub).then_inc(hmn_ok.sem, 1)
                    dve.wait_ge(hmn_ok.sem, hmn_ok.at(ph, c, g + 1))
                    dve.wait_ge(gate_ok.sem, gate_ok.at(ph, c, 2 * g + 2))
                    v.tensor_tensor(u, d, u, mul).then_inc(zhn_ok.sem, 1)
                    dve.wait_ge(zhn_ok.sem, zhn_ok.at(ph, c, g + 1))
                    v.tensor_tensor(u, u, n, add).then_inc(nzh_ok.sem, 1)

                def high_parts(c, q, s, g):
                    cols = slice(g * 4 * P, (g + 1) * 4 * P)
                    for i, (full, high) in enumerate(((zT, zT_high), (aT, aT_high))):
                        held(dve, zT_ok.sem, zT_ok.at(ph, c, 2 * g + i + 1))
                        v.tensor_copy(high[s][:, cols], full[s][:, cols]).then_inc(high_part.sem, 1)

                def new_rows(c, q, s, g):
                    if not early(c, 4):
                        held(dve, stored.sems[s], stored.at(ph, q, s, 4))
                    ks = slice(4 * g, 4 * g + 4)
                    dve.wait_ge(back_done.sem, back_done.at(ph, c, g + 1))
                    v.tensor_tensor(yout[s][:, ks, 0:F], back_ps[g][:].rearrange("p (k f) -> p k f", f=F),
                                    xin[s][:, ks, :], add).then_inc(y_ok.sem, 1)

                def half(body, g):
                    return lambda c, q, s: body(c, q, s, g)

                def kept_rows(c, q, s):
                    keep(ph, c)

                def factor(c, q, s):
                    dve.wait_ge(nstd_ok.sem, nstd_ok.at(ph, c))
                    if not early(c, 2):
                        dve.wait_ge(h_ok.sem, h_ok.at(ph, c - 2))
                    v.reciprocal(nrs[s][:], nstd[:]).then_inc(nrs_ok.sem, 1)

                def bias(c, q, s):
                    held(dve, nrs_ok.sem, nrs_ok.at(ph, c))
                    v.scalar_tensor_tensor(nbias[s][:], nmv[:, :, 0], -1.0, nrs[s][:], mul, mul)\
                        .then_inc(nbias_ok.sem, 1)

                def kept_factors(c, q, s):
                    held(dve, nbias_ok.sem, nbias_ok.at(ph, c))
                    v.tensor_copy(mean[:, bass.ds(c * NT, NT)], nmv[:, :, 0])
                    v.tensor_copy(rstd[:, bass.ds(c * NT, NT)], nrs[s][:]).then_inc(kept.sem, 1)
                    v.tensor_copy(mbias[:, bass.ds(c * NT, NT)], nbias[s][:]).then_inc(kept.sem, 1)

                stages = {
                    "A1": [(4, factor), (3, back), (4, bias), (0, columns), (4, kept_factors), (3, new_stats),
                           (1, front), (3, new_moments)],
                    "A3": [(3, back), (0, columns), (3, relu), (1, front)],
                    "A5": [(3, back), (0, columns), (3, relu)],
                    "A6": [(2, back), (3, kept_rows), (0, columns), (2, new_stats), (1, weighted), (2, new_moments)],
                    "A7": [(2, back), (3, kept_rows), (2, new_stats), (2, new_moments)]}.get(ph)
                if ph == "A8":
                    stages = [(3, half(high_parts, 1)), (4, half(mix, 1)), (3, half(candidate, 0)), (4, half(new_rows, 0)),
                              (4, half(new_rows, 1)), (2, half(high_parts, 0)), (3, half(mix, 0)),
                              (3, half(candidate, 1)), (0, columns)]
                steps(dve, *stages)

            def roots(ph):
                i = MOM_OF[ph]
                held(dve, kept.sem, kept.end(ph))
                dve.sem_inc(mom, 1)
                dve.wait_ge(mom_std, i + 1)
                v.reciprocal(rstd[:], rstd[:]).then_inc(mom, 1)
                dve.wait_ge(mom, 3 * i + 2)
                v.scalar_tensor_tensor(mbias[:], mean[:], -1.0, rstd[:], mul, mul).then_inc(mom, 1)
                dve.wait_ge(mom, 3 * i + 3)

            def coefficients(ph):
                i = COEF_OF[ph]
                k = [9 * i]

                def one(ins):
                    ins.then_inc(coef, 1)
                    k[0] += 1
                    dve.wait_ge(coef, k[0])

                dve.wait_ge(gram_done.sem, gram_done.end(ph))
                one(v.tensor_tensor(bn_tmp[:], gram_ps[:, 0:F], ident[:], mul))
                one(v.reduce_sum(bn_col[:, 1:2], bn_tmp[:], AX.X))
                one(v.tensor_scalar(bn_col[:, 0:1], gram_ps[:, F:F + 1], 1.0 / N_NODES, None, mul))
                one(v.tensor_tensor(bn_col[:, 2:3], bn_col[:, 0:1], bn_col[:, 0:1], mul))
                one(v.scalar_tensor_tensor(bn_col[:, 3:4], bn_col[:, 1:2], 1.0 / N_NODES, bn_col[:, 2:3], mul, sub))
                dve.wait_ge(coef_std, i + 1)
                one(v.reciprocal(bn_col[:, 5:6], bn_col[:, 4:5]))
                one(v.tensor_tensor(a_col[i][:], bn_col[:, 5:6], vec[:, 2 * i:2 * i + 1], mul))
                one(v.scalar_tensor_tensor(c_col[i][:], a_col[i][:], bn_col[:, 0:1], vec[:, 2 * i + 1:2 * i + 2], mul, sub))
                v.tensor_scalar(diag_a[:], ident[:], a_col[i][:], None, mul)
                v.tensor_scalar(diag_c[:], ident[:], c_col[i][:], -1.0, mul, mul).then_inc(coef, 1)
                k[0] += 1
                dve.wait_ge(coef, k[0])
                v.tensor_scalar(c_col[i][:], c_col[i][:], -1.0, None, mul)
                dve.wait_ge(coef_rows, i + 1)
                v.tensor_copy(a_row[i][:], bank[6][:, 0:F]).then_inc(coef_end, 1)
                v.tensor_copy(c_row[i][:], bank[6][:, F:2 * F]).then_inc(coef_end, 1)
                dve.wait_ge(coef_end, 2 * i + 2)
                if i == 2:
                    v.tensor_tensor(c_row[2][:], c_row[2][:], c_row[0][:], add).then_inc(coef_end, 1)
                    dve.wait_ge(coef_end, 7)
                dve.sem_inc(coef_ready, 1)

            def high_columns(c, q, s):
                if not early(c, 2):
                    held(dve, hi_ok.sem, hi_ok.at("D0", c - 2))
                v.tensor_copy(high[s][:], hi_f[:, bass.ds(c * ET, ET)]).then_inc(high_ok.sem, 1)
                v.tensor_copy(last_low[s][:], lo_f[:, bass.ds(c * ET + (ET - 1), 1)]).then_inc(high_ok.sem, 1)

            def high_digits(c, q, s):
                held(dve, high_ok.sem, high_ok.at("D0", c))
                if not early(c, 2):
                    held(dve, deg_done.sem, deg_done.at("D0", c - 2))
                for k in range(ET):
                    v.tensor_scalar(oh_hi[s][:, k, :], iota_hi[:], high[s][:, k:k + 1], None, eq)\
                        .then_inc(hi_ok.sem, 1)
                v.tensor_scalar(oh_lo[s][:, ET - 1, :], iota_lo[:], last_low[s][:], None, eq).then_inc(hi_ok.sem, 1)

            steps(dve, (1, high_digits), (0, high_columns))
            for ph in PHASES[1:]:
                if ph in EDGE:
                    gate(dve, ph)
                    edge(ph)
                    if ph == "E0":
                        dve.wait_ge(deg_done.sem, deg_done.end("D0"))
                        v.tensor_copy(deg[:], deg_ps[:, 0:NODE_TILES]).then_inc(degs, 1)
                        dve.wait_ge(degs, 1)
                        v.tensor_scalar(sqd[:], deg[:], 1.0, None, add).then_inc(degs, 1)
                        dve.wait_ge(degs, 3)
                        v.tensor_scalar(rdeg[:], deg[:], 1.0, None, mx).then_inc(degs, 1)
                        dve.wait_ge(degs, 4)
                        v.reciprocal(rdeg[:], rdeg[:]).then_inc(degs, 1)
                        v.reciprocal(dinv[:], sqd[:]).then_inc(degs, 1)
                        v.tensor_scalar(dinv2[:], deg[:], 1.0, None, add).then_inc(degs, 1)
                        dve.wait_ge(degs, 7)
                        v.reciprocal(dinv2[:], dinv2[:]).then_inc(degs, 1)
                        dve.wait_ge(degs, 8)
                        roots(ph)
                else:
                    gate(dve, ph)
                    if ph in ("A3", "A5"):
                        for b in yout[0:4]:
                            v.memset(b[:, :, F:F + 1], 1.0).then_inc(ones_ok, 1)
                        held(dve, ones_ok, 4 if ph == "A3" else 8)
                    dense(ph)
                    if ph in MOM_OF:
                        roots(ph)
                    if ph in COEF_OF:
                        if ph == "A1":
                            for s in range(4):
                                held(dve, stored.sems[s], stored.end("A1", s))
                        coefficients(ph)


_OUT = "out_dram"


def kernel(**inputs):
    import concourse.bacc as bacc
    from concourse.bass_utils import run_bass_kernel_spmd

    def edge_columns(a, fill):
        p = np.full((EPAD,), fill, a.dtype)
        p[:N_EDGES] = a
        return np.ascontiguousarray(p.reshape(EDGE_TILES, P).T)

    i = {k: np.asarray(v) for k, v in inputs.items()}
    xp = np.zeros((NPAD, F), i["x"].dtype)
    xp[:N_NODES] = i["x"]
    dst = i["dst"]
    nxt = np.concatenate([dst[1:], np.full((1,), DST_NONE, dst.dtype)])
    drow = np.full((1, 1 + EPAD), DST_NONE, dst.dtype)
    drow[0, 0] = DST_NONE + 1
    drow[0, 1:1 + N_EDGES] = dst
    W0 = i["L0_gnn_W"]
    t = lambda a: np.ascontiguousarray(a.T)
    arrays = {
        "x": xp,
        "gidx": edge_columns(i["src"], 0).view(np.uint32),
        "dst": edge_columns(dst, DST_NONE),
        "nxt": edge_columns(nxt, DST_NONE),
        "typ": edge_columns(i["edge_type_9"], 0),
        "wgt": edge_columns(i["edge_weight1"][:, 0], 0),
        "dstrow": drow,
        "WaT": t(W0[:, :F]), "WbT": t(W0[:, F:]),
        "W1": i["L1_gnn_W1"], "W2": i["L1_gnn_W2"], "WL2T": t(i["L2_gnn_W"]),
        "WmT": i["L3_gnn_W_msg"].T.copy(), "WihT": t(i["L3_gnn_W_ih"]), "WhhT": t(i["L3_gnn_W_hh"]),
        "emb": i["L3_gnn_edge_embed"],
        "vecs": np.ascontiguousarray(np.stack([i[f"L1_gnn_bn{k}_{n}"] for k in range(3) for n in ("gamma", "beta")], 1)),
        "rows": np.stack([i["L1_gnn_b1"], i["L1_gnn_b2"], i["L2_gnn_b"], i["L3_gnn_b_msg"]]),
        "gate_biases": np.concatenate([i["L3_gnn_b_ih"], i["L3_gnn_b_hh"]]).reshape(6, F).T.copy(),
    }
    nc = bacc.Bacc("TRN2", target_bir_lowering=False, num_devices=1)
    args = [nc.dram_tensor(f"in_{n}", a.shape, mybir.dt.from_np(a.dtype), kind="ExternalInput").ap()
            for n, a in arrays.items()]
    args.append(nc.dram_tensor(_OUT, (NPAD, F), mybir.dt.float32, kind="ExternalOutput").ap())
    build(nc, *args)
    r = run_bass_kernel_spmd(nc, [{f"in_{n}": np.ascontiguousarray(a) for n, a in arrays.items()}], core_ids=[0])
    return np.asarray(r.results[0][_OUT])[:N_NODES]
```
